# Optimizing a Trainium2 kernel written in Bass

```python
import numpy as np
import jax
import jax.numpy as jnp

def _softmax(x, axis=-1):
    return jax.nn.softmax(x, axis=axis)

def _gelu(x):
    return jax.nn.gelu(x, approximate=True)

def _silu(x):
    return jax.nn.silu(x)

def _sigmoid(x):
    return jax.nn.sigmoid(x)

def _layernorm(x, axis=-1, eps=1e-05):
    m = jnp.mean(x, axis=axis, keepdims=True)
    v = jnp.var(x, axis=axis, keepdims=True)
    return (x - m) / jnp.sqrt(v + eps)

def _scatter_add(tgt, idx, src, axis=0):
    return tgt.at[idx].add(src)

def _segment_sum(src, seg, n):
    return jax.ops.segment_sum(src, seg, n)
kernel_name = 'mk_seq_postln_d2_jaxref_r8_93d863'

def setup_inputs(seed: int=0):
    np.random.seed(seed)
    _w = jnp.asarray

    def _L0_attn_setup():
        import jax, jax.numpy as jnp
        import numpy as np
        D_MODEL = 128
        NUM_HEADS = 4
        HEAD_QK = 32
        HEAD_V = 64
        EPS = 1e-05
        ROPE_BASE = 10000.0

        def _apply_rotary(q, k):
            T, d = (q.shape[1], q.shape[-1])
            half = d // 2
            inv_freq = 1.0 / ROPE_BASE ** (jnp.arange(0, d, 2, dtype=jnp.float32) / d)
            freqs = jnp.arange(T, dtype=jnp.float32)[:, None] * inv_freq[None, :]
            cos = jnp.cos(freqs)[None, :, None, :]
            sin = jnp.sin(freqs)[None, :, None, :]

            def rot(x):
                x1, x2 = (x[..., :half], x[..., half:])
                return jnp.concatenate([x1 * cos - x2 * sin, x1 * sin + x2 * cos], axis=-1)
            return (rot(q), rot(k))
        key = jax.random.key(seed)
        ks = jax.random.split(key, 7)
        B, T = (2, 256)
        key_dim = NUM_HEADS * HEAD_QK
        value_dim = NUM_HEADS * HEAD_V
        s = 0.02
        return {'x': jax.random.normal(ks[0], (B, T, D_MODEL), jnp.float32), 'Wq': jax.random.normal(ks[1], (key_dim, D_MODEL), jnp.float32) * s, 'Wk': jax.random.normal(ks[2], (key_dim, D_MODEL), jnp.float32) * s, 'Wv': jax.random.normal(ks[3], (value_dim, D_MODEL), jnp.float32) * s, 'Wg': jax.random.normal(ks[4], (value_dim, D_MODEL), jnp.float32) * s, 'Wo': jax.random.normal(ks[5], (D_MODEL, value_dim), jnp.float32) * s, 'g_norm_w': jnp.ones((HEAD_V,), jnp.float32)}
    _L0_attn_in = _L0_attn_setup()

    def _L0_ffn_setup():
        import jax, jax.numpy as jnp
        import numpy as np
        TOP_K = 2
        key = jax.random.key(seed)
        k1, k2, k3, k4, k5 = jax.random.split(key, 5)
        B, S, D, F, E = (2, 128, 128, 256, 8)
        return {'x': jax.random.normal(k1, (B, S, D), dtype=jnp.float32), 'router_kernel_DE': jax.random.normal(k2, (D, E), dtype=jnp.float32) * 0.02, 'kernel_gating_EDF': jax.random.normal(k3, (E, D, F), dtype=jnp.float32) * 0.02, 'kernel_up_EDF': jax.random.normal(k4, (E, D, F), dtype=jnp.float32) * 0.02, 'kernel_down_EFD': jax.random.normal(k5, (E, F, D), dtype=jnp.float32) * 0.02}
    _L0_ffn_in = _L0_ffn_setup()

    def _L1_attn_setup():
        import jax, jax.numpy as jnp
        import numpy as np
        HIDDEN = 128
        HEADS = 8
        HEAD = HIDDEN // HEADS
        EPS = 1e-05

        def _gammas():
            lo = np.log(1.0 / 512.0)
            hi = np.log(1.0 / 32.0)
            lin = np.linspace(lo, hi, HEADS)
            return jnp.asarray(1.0 - np.exp(lin), dtype=jnp.float32)

        def _decay_mask(S, gammas):
            idx = jnp.arange(S)
            diff = idx[:, None] - idx[None, :]
            causal = diff >= 0
            safe = jnp.where(causal, diff, 0).astype(jnp.float32)
            D = jnp.where(causal[None], gammas[:, None, None] ** safe[None], 0.0)
            return D

        def _msr_forward(x, Wq, Wk, Wv, W1, W2, gn_w, gn_b):
            B, S, _ = x.shape
            xh = x.reshape(B, S, HEADS, HEAD)
            q = jnp.einsum('bshd,hde->bshe', xh, Wq)
            k = jnp.einsum('bshd,hde->bshe', xh, Wk)
            v = jnp.einsum('bshd,hde->bshe', xh, Wv)
            D = _decay_mask(S, _gammas())
            scores = jnp.einsum('bnhd,bmhd->bhnm', q, k) * D[None]
            ret = jnp.einsum('bhnm,bmhd->bnhd', scores, v)
            mu = jnp.mean(ret, axis=-1, keepdims=True)
            var = jnp.var(ret, axis=-1, keepdims=True)
            ret = (ret - mu) * jax.lax.rsqrt(var + EPS)
            ret = ret.reshape(B, S, HIDDEN) * gn_w + gn_b
            gated = x @ W1
            out = gated * jax.nn.sigmoid(gated) + ret
            return out @ W2
        key = jax.random.key(seed)
        ks = jax.random.split(key, 7)
        B, S = (2, 256)
        x = jax.random.normal(ks[0], (B, S, HIDDEN), dtype=jnp.float32)
        Wq = jax.random.normal(ks[1], (HEADS, HEAD, HEAD), dtype=jnp.float32) / HEAD
        Wk = jax.random.normal(ks[2], (HEADS, HEAD, HEAD), dtype=jnp.float32) / HEAD
        Wv = jax.random.normal(ks[3], (HEADS, HEAD, HEAD), dtype=jnp.float32) / HEAD
        W1 = jax.random.normal(ks[4], (HIDDEN, HIDDEN), dtype=jnp.float32) / HIDDEN
        W2 = jax.random.normal(ks[5], (HIDDEN, HIDDEN), dtype=jnp.float32) / HIDDEN
        gn_w = jnp.ones((HIDDEN,), dtype=jnp.float32)
        gn_b = jnp.zeros((HIDDEN,), dtype=jnp.float32)
        return {'x': x, 'Wq': Wq, 'Wk': Wk, 'Wv': Wv, 'W1': W1, 'W2': W2, 'gn_w': gn_w, 'gn_b': gn_b}
    _L1_attn_in = _L1_attn_setup()

    def _L1_ffn_setup():
        import jax, jax.numpy as jnp
        import numpy as np
        B, T, D, F, E, TOP_K = (2, 256, 128, 512, 8, 2)
        INIT = 0.02
        key = jax.random.key(seed)
        k0, k1, k2, k3, k4 = jax.random.split(key, 5)
        x = jax.random.normal(k0, (B, T, D), dtype=jnp.float32)
        Wg = jax.random.normal(k1, (D, E), dtype=jnp.float32) * INIT
        W1 = jax.random.normal(k2, (E, D, F), dtype=jnp.float32) * INIT
        W3 = jax.random.normal(k3, (E, D, F), dtype=jnp.float32) * INIT
        W2 = jax.random.normal(k4, (E, F, D), dtype=jnp.float32) * INIT
        return {'x': x, 'Wg': Wg, 'W1': W1, 'W3': W3, 'W2': W2}
    _L1_ffn_in = _L1_ffn_setup()
    _d = {'L0_attn_x': _L0_attn_in['x'], 'L0_attn_Wq': _L0_attn_in['Wq'], 'L0_attn_Wk': _L0_attn_in['Wk'], 'L0_attn_Wv': _L0_attn_in['Wv'], 'L0_attn_Wg': _L0_attn_in['Wg'], 'L0_attn_Wo': _L0_attn_in['Wo'], 'L0_attn_g_norm_w': _L0_attn_in['g_norm_w'], 'L0_ffn_router_kernel_DE': _L0_ffn_in['router_kernel_DE'], 'L0_ffn_kernel_gating_EDF': _L0_ffn_in['kernel_gating_EDF'], 'L0_ffn_kernel_up_EDF': _L0_ffn_in['kernel_up_EDF'], 'L0_ffn_kernel_down_EFD': _L0_ffn_in['kernel_down_EFD'], 'L1_attn_Wq': _L1_attn_in['Wq'], 'L1_attn_Wk': _L1_attn_in['Wk'], 'L1_attn_Wv': _L1_attn_in['Wv'], 'L1_attn_W1': _L1_attn_in['W1'], 'L1_attn_W2': _L1_attn_in['W2'], 'L1_attn_gn_w': _L1_attn_in['gn_w'], 'L1_attn_gn_b': _L1_attn_in['gn_b'], 'L1_ffn_Wg': _L1_ffn_in['Wg'], 'L1_ffn_W1': _L1_ffn_in['W1'], 'L1_ffn_W3': _L1_ffn_in['W3'], 'L1_ffn_W2': _L1_ffn_in['W2']}
    _x0 = _d['L0_attn_x']
    _d['L0_attn_x'] = jax.random.normal(jax.random.fold_in(jax.random.key(seed), 1), (16, 512, 128), dtype=_x0.dtype)
    del _x0
    return _d

def reference(L0_attn_x, L0_attn_Wq, L0_attn_Wk, L0_attn_Wv, L0_attn_Wg, L0_attn_Wo, L0_attn_g_norm_w, L0_ffn_router_kernel_DE, L0_ffn_kernel_gating_EDF, L0_ffn_kernel_up_EDF, L0_ffn_kernel_down_EFD, L1_attn_Wq, L1_attn_Wk, L1_attn_Wv, L1_attn_W1, L1_attn_W2, L1_attn_gn_w, L1_attn_gn_b, L1_ffn_Wg, L1_ffn_W1, L1_ffn_W3, L1_ffn_W2):

    def _L0_attn_ref(x, Wq, Wk, Wv, Wg, Wo, g_norm_w):
        import jax, jax.numpy as jnp
        import numpy as np
        D_MODEL = 128
        NUM_HEADS = 4
        HEAD_QK = 32
        HEAD_V = 64
        EPS = 1e-05
        ROPE_BASE = 10000.0

        def _apply_rotary(q, k):
            T, d = (q.shape[1], q.shape[-1])
            half = d // 2
            inv_freq = 1.0 / ROPE_BASE ** (jnp.arange(0, d, 2, dtype=jnp.float32) / d)
            freqs = jnp.arange(T, dtype=jnp.float32)[:, None] * inv_freq[None, :]
            cos = jnp.cos(freqs)[None, :, None, :]
            sin = jnp.sin(freqs)[None, :, None, :]

            def rot(x):
                x1, x2 = (x[..., :half], x[..., half:])
                return jnp.concatenate([x1 * cos - x2 * sin, x1 * sin + x2 * cos], axis=-1)
            return (rot(q), rot(k))
        B, T, _ = x.shape
        H, dk, dv = (NUM_HEADS, HEAD_QK, HEAD_V)
        q = (x @ Wq.T).reshape(B, T, H, dk)
        k = (x @ Wk.T).reshape(B, T, H, dk)
        q, k = _apply_rotary(q, k)
        q = jnp.transpose(q, (0, 2, 1, 3))
        k = jnp.transpose(k, (0, 2, 1, 3))
        v = jnp.transpose((x @ Wv.T).reshape(B, T, H, dv), (0, 2, 1, 3))
        q = q * dk ** (-0.5)
        log_decay = jnp.log1p(-jnp.exp2(-5.0 - jnp.arange(H, dtype=jnp.float32)))
        t = jnp.arange(T, dtype=jnp.float32)
        diff = t[:, None] - t[None, :]
        decay_mask = jnp.where(diff >= 0, jnp.exp(log_decay[:, None, None] * diff[None]), 0.0)
        scores = jnp.einsum('bhtd,bhsd->bhts', q, k) * decay_mask[None]
        o = jnp.einsum('bhts,bhsd->bhtd', scores, v)
        o = jnp.transpose(o, (0, 2, 1, 3))
        rms = jax.lax.rsqrt(jnp.mean(o * o, axis=-1, keepdims=True) + EPS)
        o_n = o * rms * g_norm_w
        g = (x @ Wg.T).reshape(B, T, H, dv)
        o_g = o_n * (g * jax.nn.sigmoid(g))
        return o_g.reshape(B, T, H * dv) @ Wo.T

    def _L0_ffn_ref(x, router_kernel_DE, kernel_gating_EDF, kernel_up_EDF, kernel_down_EFD):
        import jax, jax.numpy as jnp
        import numpy as np
        TOP_K = 2
        E = router_kernel_DE.shape[-1]
        x = x.astype(jnp.float32)
        logits_BSE = jnp.einsum('BSD,DE->BSE', x, router_kernel_DE)
        probs_BSE = jax.nn.softmax(logits_BSE.astype(jnp.float32), axis=-1)
        weights_BSK, indices_BSK = jax.lax.top_k(probs_BSE, TOP_K)
        norm_weights_BSK = jax.nn.softmax(weights_BSK, axis=-1)
        one_hot_BSKE = jax.nn.one_hot(indices_BSK, num_classes=E, dtype=x.dtype)
        full_weights_BSE = jnp.sum(one_hot_BSKE * norm_weights_BSK[..., None], axis=2)
        gating_BSEF = jnp.einsum('BSD,EDF->BSEF', x, kernel_gating_EDF)
        act_BSEF = jax.nn.silu(gating_BSEF)
        up_BSEF = jnp.einsum('BSD,EDF->BSEF', x, kernel_up_EDF)
        fuse_BSEF = act_BSEF * up_BSEF
        down_BSED = jnp.einsum('BSEF,EFD->BSED', fuse_BSEF, kernel_down_EFD)
        out_BSD = jnp.einsum('BSED,BSE->BSD', down_BSED, full_weights_BSE)
        return out_BSD.astype(jnp.float32)

    def _L1_attn_ref(x, Wq, Wk, Wv, W1, W2, gn_w, gn_b):
        import jax, jax.numpy as jnp
        import numpy as np
        HIDDEN = 128
        HEADS = 8
        HEAD = HIDDEN // HEADS
        EPS = 1e-05

        def _gammas():
            lo = np.log(1.0 / 512.0)
            hi = np.log(1.0 / 32.0)
            lin = np.linspace(lo, hi, HEADS)
            return jnp.asarray(1.0 - np.exp(lin), dtype=jnp.float32)

        def _decay_mask(S, gammas):
            idx = jnp.arange(S)
            diff = idx[:, None] - idx[None, :]
            causal = diff >= 0
            safe = jnp.where(causal, diff, 0).astype(jnp.float32)
            D = jnp.where(causal[None], gammas[:, None, None] ** safe[None], 0.0)
            return D

        def _msr_forward(x, Wq, Wk, Wv, W1, W2, gn_w, gn_b):
            B, S, _ = x.shape
            xh = x.reshape(B, S, HEADS, HEAD)
            q = jnp.einsum('bshd,hde->bshe', xh, Wq)
            k = jnp.einsum('bshd,hde->bshe', xh, Wk)
            v = jnp.einsum('bshd,hde->bshe', xh, Wv)
            D = _decay_mask(S, _gammas())
            scores = jnp.einsum('bnhd,bmhd->bhnm', q, k) * D[None]
            ret = jnp.einsum('bhnm,bmhd->bnhd', scores, v)
            mu = jnp.mean(ret, axis=-1, keepdims=True)
            var = jnp.var(ret, axis=-1, keepdims=True)
            ret = (ret - mu) * jax.lax.rsqrt(var + EPS)
            ret = ret.reshape(B, S, HIDDEN) * gn_w + gn_b
            gated = x @ W1
            out = gated * jax.nn.sigmoid(gated) + ret
            return out @ W2
        return _msr_forward(x, Wq, Wk, Wv, W1, W2, gn_w, gn_b)

    def _L1_ffn_ref(x, Wg, W1, W3, W2):
        import jax, jax.numpy as jnp
        import numpy as np
        B, T, D, F, E, TOP_K = (2, 256, 128, 512, 8, 2)
        INIT = 0.02
        Bb, Tt, Dd = x.shape
        xf = x.reshape(-1, Dd)
        logits = xf @ Wg
        top_v, top_i = jax.lax.top_k(logits, TOP_K)
        top_w = jax.nn.softmax(top_v, axis=-1)
        h1 = jnp.einsum('nd,edf->enf', xf, W1)
        h3 = jnp.einsum('nd,edf->enf', xf, W3)
        y = jnp.einsum('enf,efd->end', jax.nn.silu(h1) * h3, W2)
        y = jnp.transpose(y, (1, 0, 2))
        sel = jnp.take_along_axis(y, top_i[:, :, None], axis=1)
        out = jnp.sum(sel * top_w[:, :, None], axis=1)
        return out.reshape(Bb, Tt, Dd)
    x = L0_attn_x
    x = _layernorm(x + _L0_attn_ref(x, L0_attn_Wq, L0_attn_Wk, L0_attn_Wv, L0_attn_Wg, L0_attn_Wo, L0_attn_g_norm_w), axis=-1)
    x = _layernorm(x + _L0_ffn_ref(x, L0_ffn_router_kernel_DE, L0_ffn_kernel_gating_EDF, L0_ffn_kernel_up_EDF, L0_ffn_kernel_down_EFD), axis=-1)
    x = _layernorm(x + _L1_attn_ref(x, L1_attn_Wq, L1_attn_Wk, L1_attn_Wv, L1_attn_W1, L1_attn_W2, L1_attn_gn_w, L1_attn_gn_b), axis=-1)
    x = _layernorm(x + _L1_ffn_ref(x, L1_ffn_Wg, L1_ffn_W1, L1_ffn_W3, L1_ffn_W2), axis=-1)
    return x

_drawn_inputs = setup_inputs


def setup_inputs(seed=0):
    import zlib

    import numpy as np

    out = dict(_drawn_inputs(seed))
    spreads = {'L0_attn_g_norm_w': (1.0, 0.6), 'L1_attn_gn_w': (1.0, 0.6), 'L1_attn_gn_b': (0.0, 0.8)}
    factors = {'L0_ffn_router_kernel_DE': 8.0,
     'L0_ffn_kernel_gating_EDF': 8.0,
     'L0_ffn_kernel_up_EDF': 8.0,
     'L0_ffn_kernel_down_EFD': 8.0,
     'L1_attn_W1': 8.0,
     'L1_ffn_Wg': 7.785,
     'L1_ffn_W1': 6.864,
     'L1_ffn_W3': 6.827,
     'L1_ffn_W2': 6.836}
    for name, (base, spread) in spreads.items():
        noise = np.random.default_rng([zlib.crc32(name.encode()), seed]).standard_normal(out[name].shape)
        drawn = base * np.exp(spread * noise) if base else spread * noise
        out[name] = jnp.asarray(drawn.astype(out[name].dtype))
    for name, factor in factors.items():
        out[name] = (out[name] * factor).astype(out[name].dtype)
    return out
```

```python
import concourse.bass as bass
from concourse import mybir
from contextlib import ExitStack

P = 128
SEQS, T, D = 16, 512, 128
CH = T // P
TILES = SEQS * CH
TOKENS = SEQS * T
E, TOPK = 8, 2
ROWS = 256
STEPS = TOKENS * TOPK // ROWS + E
REGION = TOKENS + ROWS
LN_EPS = 1e-5
H0, DK0, DV0 = 4, 32, 64
H1, DH1 = 8, 16
F0, F1 = 256, 512

F32 = mybir.dt.float32
BF16 = mybir.dt.bfloat16
I32 = mybir.dt.int32
U32 = mybir.dt.uint32
ALU = mybir.AluOpType
ACT = mybir.ActivationFunctionType
AX = mybir.AxisListType


class Turn:

    def __init__(self, n, half, odd):
        self.n, self.half, self.odd = n, half, odd


def turn(i, sub, lag, count):
    k = sub - lag
    if isinstance(i, int):
        n = 2 * i + k
        return Turn(n, n // 2, n % 2) if 0 <= n < count else None
    return Turn(i * 2 + k, i + k // 2, k % 2)


def wait_count(eng, sem, n):
    if isinstance(n, int) and n <= 0:
        return
    eng.wait_ge(sem, n)


class Chain:

    def __init__(self, sem):
        self.sem, self.per, self.k = sem, 0, 0

    def start(self, eng, t):
        self.eng, self.t, self.k = eng, t, 0

    def link(self, ins):
        self.k += 1
        ins.then_inc(self.sem, 1)
        self.eng.wait_ge(self.sem, self.t.n * self.per + self.k)

    def end(self):
        assert self.per in (0, self.k)
        self.per = self.k


def run_steps(eng, first, last, count, lags, body):
    total = count + max(lags)
    for s in range(2 * first):
        body([turn(s // 2, s % 2, lag, count) for lag in lags])
    with eng.Fori(first, last) as i:
        for sub in range(2):
            body([turn(i, sub, lag, count) for lag in lags])
    for s in range(2 * last, total):
        body([turn(s // 2, s % 2, lag, count) for lag in lags])


def build(nc, x, wq, wqp, wk, wkp, wvg, wo, gnorm, rope_q, rope_k, router0, gate0, up0, down0,
          bd_q, bd_k, bd_kv, w1, w2, gn_w, gn_b, dec_q, dec_k, dec_kt, router1, gate1, up1, down1,
          ident, causal, tri, head0, head1, blk0, blk1, iota_e, region0, iota_s, out):
    scattered = nc.dram_tensor("scattered", ((E + 1) * REGION, D), F32, kind="Internal").ap()
    expert_out = nc.dram_tensor("expert_out", (STEPS * ROWS, D), F32, kind="Internal").ap()
    x_seq = x.rearrange("b (c p) d -> p b c d", p=P)
    out_seq = out.rearrange("b (c p) d -> p b c d", p=P)

    whole = ExitStack()
    with whole:
        def keep(name, shape, dt=F32):
            return whole.enter_context(nc.sbuf_tensor(name, shape, dt))

        c_ident = keep("c_ident", [P, P])
        c_causal = keep("c_causal", [P, P])
        c_tri = keep("c_tri", [P, P], BF16)
        c_ones = keep("c_ones", [P, P], BF16)
        c_iota = keep("c_iota", [P, E])
        c_region = keep("c_region", [P, E])
        c_half = keep("c_half", [P, 2 * T // 16])
        xres = keep("xres", [P, TILES, D])
        top_l = keep("top_l", [P, SEQS, TOPK * CH])
        top_i = keep("top_i", [P, SEQS, TOPK * CH])
        row_r = keep("row_r", [P, SEQS, TOPK * CH])
        logits = keep("logits", [P, TILES, E])
        row_c = keep("row_c", [P, SEQS, TOPK * CH], U32)
        w_top = keep("w_top", [P, SEQS, TOPK * CH])
        base = keep("base", [P, E])
        psum = [whole.enter_context(nc.psum_tensor(f"bank{i}", [P, 512], F32)) for i in range(8)]
        s_const = whole.enter_context(nc.semaphore("s_const"))
        s_cset = whole.enter_context(nc.semaphore("s_cset"))
        w_gu = keep("w_gu", [P, E, 2, F1])
        w_dn = keep("w_dn", [P, E, F1 // P, D])
        s_wx0 = whole.enter_context(nc.semaphore("s_wx0"))
        s_wx1 = whole.enter_context(nc.semaphore("s_wx1"))

        def load_experts(sp, layer, sem):
            g, u, dn, f = ((gate0, up0, down0, F0), (gate1, up1, down1, F1))[layer]
            for e in range(E):
                sp.dma_start(w_gu[:, e, 0, 0:f], g[e]).then_inc(sem, 16)
                sp.dma_start(w_gu[:, e, 1, 0:f], u[e]).then_inc(sem, 16)
                sp.dma_start(w_dn[:, e, 0:f // P, :], dn[e].rearrange("(j p) d -> p j d", p=P)).then_inc(sem, 16)

        used = []

        def new_sem(phase, name):
            used.append(phase.enter_context(nc.semaphore(name)))
            return used[-1]

        def clear_semaphores():
            with nc.Block() as between:
                @between.gpsimd
                def _(pool):
                    numbers = sorted(s.num for s in used)
                    at = 0
                    while at < len(numbers):
                        to = at
                        while to + 1 < len(numbers) and numbers[to + 1] == numbers[to] + 1:
                            to += 1
                        pool.sem_clear(range(numbers[at], numbers[to] + 1))
                        at = to + 1
            used.clear()

        mark = keep("mark", [1, 5])

        def wait_apart(eng, at=4):
            if eng is nc.gpsimd:
                nc.gpsimd.tensor_tensor(mark[:, at:at + 1], c_half[0:1, 0:1], c_half[0:1, 0:1], ALU.add)
            else:
                nc.vector.memset(mark[:, at:at + 1], 0.0)

        class Norm:

            def __init__(self, name, sb, sem):
                self.stats = sb(name + "_stats", [P, CH, 6])
                self.mv = sb(name + "_mv", [P, CH, 2])
                self.ve = sb(name + "_ve", [P, CH])
                self.rstd = sb(name + "_rstd", [P, CH])
                self.chain = Chain(sem(name + "_chain"))
                self.var = sem(name + "_var")
                self.inv = sem(name + "_inv")

            def statistics(self, dve, r, t):
                for c in range(CH):
                    last = nc.vector.bn_stats(self.stats[:, c, :], r[:, c, :])
                self.chain.start(dve, t)
                self.chain.link(last)
                wait_apart(dve)
                for c in range(CH):
                    last = nc.vector.bn_aggr(self.mv[:, c, :], self.stats[:, c, :])
                self.chain.link(last)
                self.chain.end()
                nc.vector.tensor_scalar(self.ve[:], self.mv[:, :, 1], LN_EPS, None, ALU.add).then_inc(self.var, 1)

            def power(self, pool, t):
                pool.wait_ge(self.var, t.n + 1)
                nc.gpsimd.tensor_tensor(self.rstd[:], self.ve[:], c_half[:, 0:CH], ALU.pow).then_inc(self.inv, 1)

            def apply(self, dve, r, to, t, done):
                dve.wait_ge(self.inv, t.n + 1)
                for c in range(CH):
                    last = nc.vector.tensor_scalar(to[:, c, :], r[:, c, :], self.mv[:, c, 0:1],
                                                   self.rstd[:, c:c + 1], ALU.subtract, ALU.mult)
                last.then_inc(done, 1)

        class Router:

            def __init__(self, name, sb, sem, w_router):
                self.w = w_router
                self.xT = sb(name + "_xT", [P, T])
                self.lg = sb(name + "_lg", [P, CH, E])
                self.mx = sb(name + "_mx", [P, CH, 8])
                self.mi = sb(name + "_mi", [P, CH, 8], U32)
                self.ix = sb(name + "_ix", [P, TOPK, CH])
                self.pick = sb(name + "_pick", [P, TOPK * CH, E])
                self.picked = sb(name + "_picked", [P, CH, E], BF16)
                self.rows = sb(name + "_rows", [P, CH, E])
                self.rowk = sb(name + "_rowk", [P, TOPK * CH, E])
                self.dst = sb(name + "_dst", [P, TOPK * CH])
                self.idx = [sb(f"{name}_idx{i}", [P, TOPK * CH], U32) for i in range(2)]
                self.chain = Chain(sem(name + "_chain"))
                self.chain2 = Chain(sem(name + "_chain2"))
                self.tp = sem(name + "_tp")
                self.xT_there = sem(name + "_xT_there")
                self.lg_mm = sem(name + "_lg_mm")
                self.picks = sem(name + "_picks")
                self.ranks_mm = sem(name + "_ranks_mm")
                self.idx_there = sem(name + "_idx_there")
                self.sent = [sem(f"{name}_sent{i}") for i in range(2)]

            def transposes(self, pe, bank, xb, t):
                for c in range(CH):
                    last = nc.tensor.transpose(bank[:, c * P:(c + 1) * P], xb[:, c, :], c_ident[:])
                last.then_inc(self.tp, 1)

            def logits_mm(self, pe, bank, t):
                pe.wait_ge(self.xT_there, t.n + 1)
                for c in range(CH):
                    last = nc.tensor.matmul(bank[:, c * E:(c + 1) * E], self.xT[:, c * P:(c + 1) * P],
                                            self.w[:], start=True, stop=True)
                last.then_inc(self.lg_mm, 1)

            def choose(self, dve, bank, t):
                ch = self.chain
                dve.wait_ge(self.lg_mm, t.n + 1)
                ch.start(dve, t)
                lg = bank[:, 0:CH * E].rearrange("p (c e) -> p c e", c=CH)
                nc.vector.tensor_copy(logits[:, bass.ds(t.n * CH, CH), :], lg)
                ch.link(nc.vector.tensor_copy(self.lg[:], lg))
                wait_apart(dve)
                for c in range(CH):
                    last = nc.vector.max(self.mx[:, c, :], self.lg[:, c, :])
                ch.link(last)
                wait_apart(dve)
                for c in range(CH):
                    last = nc.vector.max_index(self.mi[:, c, :], self.mx[:, c, :], self.lg[:, c, :])
                ch.link(last)
                nc.vector.tensor_copy(top_l[:, bass.ds(t.n, 1), :].rearrange("p o (k c) -> p (o k) c", k=TOPK),
                                      self.mx[:, :, 0:TOPK].rearrange("p c k -> p k c"))
                ch.link(nc.vector.tensor_copy(self.ix[:], self.mi[:, :, 0:TOPK].rearrange("p c k -> p k c")))
                nc.vector.tensor_copy(top_i[:, bass.ds(t.n, 1), :].rearrange("p o n -> p (o n)"),
                                      self.ix[:].rearrange("p k c -> p (k c)"))
                ch.link(nc.vector.tensor_tensor(
                    self.pick[:], c_iota[:].unsqueeze(1).to_broadcast([P, TOPK * CH, E]),
                    self.ix[:].rearrange("p k c -> p (k c)").unsqueeze(2).to_broadcast([P, TOPK * CH, E]),
                    ALU.is_equal))
                ch.end()
                nc.vector.tensor_tensor(self.picked[:], self.pick[:, 0:CH, :], self.pick[:, CH:, :],
                                        ALU.add).then_inc(self.picks, 1)

            def ranks_mm_(self, pe, bank, t):
                pe.wait_ge(self.picks, t.n + 1)
                m = self.picked
                nc.tensor.matmul(bank[:, 0:CH * E], c_tri[:], m[:].rearrange("p c e -> p (c e)"),
                                 start=True, stop=False, skip_group_check=True)
                for c in range(CH - 1):
                    later = CH - 1 - c
                    nc.tensor.matmul(bank[:, (c + 1) * E:CH * E].rearrange("p (c e) -> p c e", e=E), c_ones[:],
                                     m[:, c:c + 1, :].to_broadcast([P, later, E]),
                                     start=False, stop=False, skip_group_check=True)
                for c in range(CH):
                    last = nc.tensor.matmul(bank[:, CH * E:CH * E + E], c_ones[:], m[:, c, :],
                                            start=False, stop=(c == CH - 1), skip_group_check=True)
                last.then_inc(self.ranks_mm, 1)

            def rows_of(self, dve, bank, t):
                ch = self.chain2
                dve.wait_ge(self.ranks_mm, t.n + 1)
                ch.start(dve, t)
                ch.link(nc.vector.tensor_tensor(
                    self.rows[:], bank[:, 0:CH * E].rearrange("p (c e) -> p c e", c=CH),
                    base[:].unsqueeze(1).to_broadcast([P, CH, E]), ALU.add))
                nc.vector.tensor_tensor(base[:], bank[:, CH * E:CH * E + E], base[:], ALU.add)
                for k in range(TOPK):
                    last = nc.vector.tensor_tensor(self.rowk[:, k * CH:(k + 1) * CH, :],
                                                   self.pick[:, k * CH:(k + 1) * CH, :], self.rows[:], ALU.mult)
                ch.link(last)
                ch.link(nc.vector.tensor_reduce(self.dst[:], self.rowk[:], AX.X, ALU.add))
                nc.vector.tensor_copy(row_r[:, bass.ds(t.n, 1), :].rearrange("p o n -> p (o n)"), self.dst[:])
                ch.end()
                nc.vector.tensor_copy(self.idx[t.odd][:], self.dst[:]).then_inc(self.idx_there, 1)

            def scatter(self, pool, xb, t):
                pool.wait_ge(self.idx_there, t.n + 1)
                wait_apart(pool, t.odd)
                for k in range(TOPK):
                    for c in range(CH):
                        j = k * CH + c
                        nc.gpsimd.indirect_dma_start(
                            out=scattered[0:E * REGION, :],
                            out_offset=bass.IndirectOffsetOnAxis(ap=self.idx[t.odd][:, j:j + 1], axis=0),
                            in_=xb[:, c, :], in_offset=None).then_inc(self.sent[t.odd], 16)

        SCATTERS = 16 * TOPK * CH

        def retention0():
            ph = ExitStack()
            with ph:
                def sb(name, shape, dt=F32):
                    return ph.enter_context(nc.sbuf_tensor("a_" + name, shape, dt))

                def sem(name):
                    return new_sem(ph, "a_" + name)

                w_q, w_qp, w_k, w_kp = (sb(n, [P, P]) for n in ("wq", "wqp", "wk", "wkp"))
                w_vg = sb("wvg", [P, 2 * H0 * DV0])
                w_o = sb("wo", [P, 2, D])
                w_on = sb("won", [P, 2, D])
                tri_f = sb("tri_f", [P, P])
                g_n = sb("gn", [P, 1])
                t_q = sb("rope_q", [P, 2, T])
                t_k = sb("rope_k", [P, 2, T])
                m_head = sb("m_head", [P, H0])
                m_blk = sb("m_blk", [P, H0 * DV0])
                w_r = sb("wr", [P, E])
                xb = [sb(f"xb{i}", [P, CH, D]) for i in range(2)]
                xT = [sb(f"xT{i}", [P, T]) for i in range(2)]
                qm = sb("qm", [P, 2, T])
                km = sb("km", [P, 2, T])
                qr = [sb(f"qr{i}", [P, T]) for i in range(2)]
                kT = [sb(f"kT{i}", [P, T]) for i in range(2)]
                qx = [sb(f"qx{i}", [P, CH, H0, P]) for i in range(2)]
                v = [sb(f"v{i}", [P, CH, H0 * DV0]) for i in range(2)]
                kt = sb("kt", [P, CH - 1, P])
                sg = sb("sg", [P, CH, H0 * DV0])
                sT = [sb(f"sT{i}", [P, H0, P]) for i in range(2)]
                S = [sb(f"S{i}", [P, H0 * DV0]) for i in range(2)]
                osq = sb("osq", [P, CH, H0 * DV0])
                og = sb("og", [P, CH, H0 * DV0])
                ssq = sb("ssq", [P, CH * H0])
                mse = sb("mse", [P, CH * H0])
                rms = sb("rms", [P, CH * H0])
                ogT = sb("ogT", [P, 2, T])
                r = sb("r", [P, CH, D])
                x1 = [sb(f"x1{i}", [P, CH, D]) for i in range(2)]
                norm = Norm("n", sb, sem)
                router = Router("r", sb, sem, w_r)
                T0, T1, S0, S1, U, O, A0, A1 = psum

                s_x = [sem(f"x{i}") for i in range(2)]
                s_xr = sem("xr")
                s_w = sem("w")
                s_wo = sem("wo_scaled")
                xT_mm, xT_ev = sem("xT_mm"), sem("xT_ev")
                q_mm, k_mm, v_mm, g_mm = sem("q_mm"), sem("k_mm"), sem("v_mm"), sem("g_mm")
                q_ev, k_ev, v_ev, g_ev = sem("q_ev"), sem("k_ev"), sem("v_ev"), sem("g_ev")
                qx_there, kT_there = sem("qx_there"), sem("kT_there")
                kt_mm, kt_ev = sem("kt_mm"), sem("kt_ev")
                sc_mm, sT_there = sem("sc_mm"), sem("sT_there")
                U_mm, S_there = sem("U_mm"), sem("S_there")
                o_mm, sq_there, og_there = sem("o_mm"), sem("sq_there"), sem("og_there")
                ms_there, rms_there, ogn_there = sem("ms_there"), sem("rms_there"), sem("ogn_there")
                ogT_mm, ogT_ev = sem("ogT_mm"), sem("ogT_ev")
                y_mm, r_there, x1_there, x1_kept = sem("y_mm"), sem("r_there"), sem("x1_there"), sem("x1_kept")
                ch_q, ch_ss = Chain(sem("ch_q")), Chain(sem("ch_ss"))
                lags = [0, 1, 2, 3]
                first, last = 2, SEQS // 2
                block = ph.enter_context(nc.Block())

                @block.sync
                def _(sp):
                    sp.dma_start(c_ident[:], ident).then_inc(s_const, 16)
                    small = [(w_q, wq), (w_qp, wqp), (w_k, wk), (w_kp, wkp), (w_vg, wvg), (t_q, rope_q), (t_k, rope_k),
                             (m_head, head0), (m_blk, blk0), (w_o, wo), (g_n, gnorm), (w_r, router0)]
                    consts = [(c_causal, causal), (c_iota, iota_e), (c_region, region0)]

                    def load(t):
                        wait_count(sp, xT_mm, t.n - 1)
                        sp.dma_start(xb[t.odd][:], x_seq[:, bass.ds(t.n, 1)].rearrange("p b c d -> p (b c) d")
                                     ).then_inc(s_x[t.odd], 16)

                    def body(ts):
                        if ts[0] is None:
                            return
                        load(ts[0])
                        if isinstance(ts[0].n, int) and ts[0].n == 0:
                            for to, src in small:
                                sp.dma_start(to[:], src).then_inc(s_w, 16)
                            for to, src in consts:
                                sp.dma_start(to[:], src).then_inc(s_const, 16)
                            sp.dma_start(tri_f[:], tri).then_inc(s_const, 16)
                        if isinstance(ts[0].n, int) and ts[0].n == 1:
                            for q in range(4):
                                sp.dma_start(xres[:, q * 16:(q + 1) * 16, :],
                                             x_seq[:, q * 4:(q + 1) * 4].rearrange("p b c d -> p (b c) d")
                                             ).then_inc(s_xr, 16)
                            load_experts(sp, 0, s_wx0)

                    run_steps(sp, first, last, SEQS, lags, body)

                n_w, n_const = 16 * 12, 16 * 5

                @block.gpsimd
                def _(pool):
                    nc.gpsimd.memset(c_half[:], -0.5).then_inc(s_cset, 1)
                    nc.gpsimd.memset(c_ones[:], 1.0).then_inc(s_cset, 1)
                    pool.wait_ge(s_cset, 2)

                    def body(ts):
                        _, b, c, d = ts
                        if c:
                            norm.power(pool, c)
                        if b:
                            pool.wait_ge(ms_there, b.n + 1)
                            nc.gpsimd.tensor_tensor(rms[:], mse[:], c_half[:, 0:CH * H0], ALU.pow).then_inc(rms_there, 1)
                        if d:
                            router.scatter(pool, x1[d.odd], d)

                    run_steps(pool, first, last, SEQS, lags, body)
                    for i in range(2):
                        pool.wait_ge(router.sent[i], SCATTERS * SEQS // 2)

                @block.scalar
                def _(act):
                    def body(ts):
                        a, b, c, d = ts
                        if a:
                            act.wait_ge(xT_mm, a.n + 1)
                            nc.scalar.copy(xT[a.odd][:], T0[:, :]).then_inc(xT_ev, 1)
                        if b:
                            act.wait_ge(kt_mm, b.n + 1)
                            nc.scalar.copy(kt[:], T1[:, 0:(CH - 1) * P].rearrange("p (c k) -> p c k", c=CH - 1)
                                           ).then_inc(kt_ev, 1)
                            wait_count(act, og_there, 2 * b.n)
                            act.wait_ge(g_mm, b.n + 1)
                            for j, bank in enumerate((A0, A1)):
                                nc.scalar.activation(sg[:, 2 * j:2 * j + 2, :],
                                                     bank[:].rearrange("p (c n) -> p c n", c=2),
                                                     ACT.Silu).then_inc(g_ev, 1)
                        if c:
                            act.wait_ge(ogT_mm, c.n + 1)
                            for j, bank in enumerate((A0, A1)):
                                nc.scalar.copy(ogT[:, j, :], bank[:, :]).then_inc(ogT_ev, 1)
                        if d:
                            act.wait_ge(x1_there, d.n + 1)
                            nc.scalar.copy(xres[:, bass.ds(d.n * CH, CH), :], x1[d.odd][:]).then_inc(x1_kept, 1)
                        if b:
                            wait_count(act, ms_there, b.n)
                            act.wait_ge(o_mm, 2 * b.n + 1)
                            nc.scalar.activation(osq[:, 0:2, :], O[:].rearrange("p (c n) -> p c n", c=2),
                                                 ACT.Square).then_inc(sq_there, 1)
                        if d:
                            act.wait_ge(router.tp, d.n + 1)
                            nc.scalar.copy(router.xT[:], T0[:, :]).then_inc(router.xT_there, 1)
                        if a:
                            act.wait_ge(v_mm, a.n + 1)
                            for j, bank in enumerate((A0, A1)):
                                nc.scalar.copy(v[a.odd][:, 2 * j:2 * j + 2, :],
                                               bank[:].rearrange("p (c n) -> p c n", c=2)).then_inc(v_ev, 1)
                        if b:
                            act.wait_ge(o_mm, 2 * b.n + 2)
                            nc.scalar.activation(osq[:, 2:4, :], O[:].rearrange("p (c n) -> p c n", c=2),
                                                 ACT.Square).then_inc(sq_there, 1)

                    nc.scalar.preload_act_table_set("silu_and_others")
                    run_steps(act, first, last, SEQS, lags, body)

                @block.vector
                def _(dve):
                    dve.wait_ge(s_w, n_w)
                    dve.wait_ge(s_const, n_const)
                    nc.vector.tensor_copy(base[:], c_region[:])
                    nc.vector.tensor_copy(c_tri[:], tri_f[:])
                    nc.vector.tensor_scalar(w_on[:], w_o[:], g_n[:, 0:1], None, ALU.mult).then_inc(s_wo, 1)
                    dve.wait_ge(s_wo, 1)
                    dve.wait_ge(s_xr, 64)

                    def masked_scores(b, c):
                        dve.wait_ge(sc_mm, CH * b.n + c + 1)
                        nc.vector.tensor_tensor(sT[c % 2][:], (S0, S1)[c % 2][:].rearrange("p (h t) -> p h t", h=H0),
                                                c_causal[:].unsqueeze(1).to_broadcast([P, H0, P]),
                                                ALU.mult).then_inc(sT_there, 1)

                    def state(b, c):
                        dve.wait_ge(U_mm, (CH - 1) * b.n + c + 1)
                        nc.vector.tensor_tensor(S[c % 2][:], U[:, 0:H0 * DV0], m_blk[:], ALU.mult).then_inc(S_there, 1)

                    def gated(b, j):
                        dve.wait_ge(sq_there, 2 * b.n + j + 1)
                        dve.wait_ge(g_ev, 2 * b.n + 2)
                        nc.vector.tensor_tensor(og[:, 2 * j:2 * j + 2, :], O[:].rearrange("p (c n) -> p c n", c=2),
                                                sg[:, 2 * j:2 * j + 2, :], ALU.mult).then_inc(og_there, 1)

                    def body(ts):
                        a, b, c, d = ts
                        if c:
                            dve.wait_ge(rms_there, c.n + 1)
                            nc.vector.tensor_tensor(
                                og[:].rearrange("p c (h n) -> p (c h) n", h=H0),
                                og[:].rearrange("p c (h n) -> p (c h) n", h=H0),
                                rms[:].unsqueeze(2).to_broadcast([P, CH * H0, DV0]), ALU.mult).then_inc(ogn_there, 1)
                        if b:
                            masked_scores(b, 0)
                            masked_scores(b, 1)
                            state(b, 0)
                        if c:
                            dve.wait_ge(y_mm, c.n + 1)
                            nc.vector.tensor_tensor(r[:], T0[:].rearrange("p (c d) -> p c d", c=CH),
                                                    xres[:, bass.ds(c.n * CH, CH), :], ALU.add).then_inc(r_there, 1)
                            dve.wait_ge(r_there, c.n + 1)
                            norm.statistics(dve, r, c)
                        if a:
                            dve.wait_ge(q_mm, a.n + 1)
                            for j, bank in enumerate((A0, A1)):
                                last_i = nc.vector.tensor_tensor(qm[:, j, :], bank[:], t_q[:, j, :], ALU.mult)
                            last_i.then_inc(q_ev, 1)
                            dve.wait_ge(q_ev, a.n + 1)
                            ch_q.start(dve, a)
                            ch_q.link(nc.vector.tensor_tensor(qr[a.odd][:], qm[:, 0, :], qm[:, 1, :], ALU.add))
                            ch_q.end()
                            for h in range(H0):
                                last_i = nc.vector.tensor_scalar(
                                    qx[a.odd][:, :, h, :], qr[a.odd][:].rearrange("p (c t) -> p c t", c=CH),
                                    m_head[:, h:h + 1], None, ALU.mult)
                            last_i.then_inc(qx_there, 1)
                        if b:
                            gated(b, 0)
                            state(b, 1)
                            masked_scores(b, 2)
                        if a:
                            dve.wait_ge(k_mm, a.n + 1)
                            for j, bank in enumerate((A0, A1)):
                                last_i = nc.vector.tensor_tensor(km[:, j, :], bank[:], t_k[:, j, :], ALU.mult)
                            last_i.then_inc(k_ev, 1)
                            dve.wait_ge(k_ev, a.n + 1)
                            nc.vector.tensor_tensor(kT[a.odd][:], km[:, 0, :], km[:, 1, :], ALU.add).then_inc(kT_there, 1)
                        if b:
                            state(b, 2)
                            masked_scores(b, 3)
                        if c:
                            wait_count(dve, router.sent[c.odd], SCATTERS * c.half)
                            wait_count(dve, x1_kept, c.n - 1)
                            norm.apply(dve, r, x1[c.odd], c, x1_there)
                        if d:
                            router.choose(dve, T1, d)
                        if b:
                            gated(b, 1)
                            ch_ss.start(dve, b)
                            ch_ss.link(nc.vector.tensor_reduce(ssq[:], osq[:].rearrange("p c (h n) -> p (c h) n", h=H0),
                                                               AX.X, ALU.add))
                            ch_ss.end()
                            nc.vector.tensor_scalar(mse[:], ssq[:], 1.0 / DV0, LN_EPS, ALU.mult, ALU.add
                                                    ).then_inc(ms_there, 1)
                        if d:
                            router.rows_of(dve, T1, d)

                    run_steps(dve, first, last, SEQS, lags, body)

                @block.tensor
                def _(pe):
                    pe.wait_ge(s_const, n_const)
                    pe.wait_ge(s_w, n_w)
                    pe.wait_ge(s_wo, 1)

                    def scores(b, c):
                        wait_count(pe, sT_there, CH * b.n + c - 1)
                        nc.tensor.matmul((S0, S1)[c % 2][:], kT[b.odd][:, c * P:(c + 1) * P],
                                         qx[b.odd][:, c].rearrange("p h t -> p (h t)"),
                                         start=True, stop=True).then_inc(sc_mm, 1)

                    def state(b, c):
                        wait_count(pe, S_there, (CH - 1) * b.n + c)
                        nc.tensor.matmul(U[:, 0:H0 * DV0], kt[:, c, :], v[b.odd][:, c, :],
                                         start=(c == 0), stop=(c == CH - 2), skip_group_check=True).then_inc(U_mm, 1)

                    def outputs(b, c):
                        at = (c % 2) * H0 * DV0
                        if c % 2 == 0:
                            wait_count(pe, og_there, 2 * b.n + c // 2)
                        if c:
                            pe.wait_ge(S_there, (CH - 1) * b.n + c)
                            nc.tensor.matmul(O[:, at:at + H0 * DV0], qr[b.odd][:, c * P:(c + 1) * P], S[(c - 1) % 2][:],
                                             start=(c % 2 == 0), stop=False, skip_group_check=True)
                        pe.wait_ge(sT_there, CH * b.n + c + 1)
                        for h in range(H0):
                            mm = nc.tensor.matmul(O[:, at + h * DV0:at + (h + 1) * DV0], sT[c % 2][:, h, :],
                                                  v[b.odd][:, c, h * DV0:(h + 1) * DV0],
                                                  start=(c == 0 and h == 0), stop=(h == H0 - 1), skip_group_check=True)
                        if c % 2:
                            mm.then_inc(o_mm, 1)

                    def body(ts):
                        a, b, c, d = ts
                        if a:
                            pe.wait_ge(s_x[a.odd], a.half * 16 + 16)
                            wait_count(pe, router.xT_there, a.n - 3)
                            wait_count(pe, r_there, a.n - 2)
                            wait_count(pe, xT_ev, a.n)
                            for j in range(CH):
                                mm = nc.tensor.transpose(T0[:, j * P:(j + 1) * P], xb[a.odd][:, j, :], c_ident[:])
                            mm.then_inc(xT_mm, 1)
                        if b:
                            pe.wait_ge(kT_there, b.n + 1)
                            wait_count(pe, router.idx_there, b.n - 2)
                            wait_count(pe, kt_ev, b.n)
                            for j in range(CH - 1):
                                mm = nc.tensor.transpose(T1[:, j * P:(j + 1) * P], kT[b.odd][:, j * P:(j + 1) * P],
                                                         c_ident[:])
                            mm.then_inc(kt_mm, 1)
                            pe.wait_ge(v_ev, 2 * b.n + 2)
                            for j in range(CH):
                                mm = nc.tensor.matmul((A0, A1)[j // 2][:, (j % 2) * 256:(j % 2) * 256 + 256],
                                                      xT[b.odd][:, j * P:(j + 1) * P], w_vg[:, 256:512],
                                                      start=True, stop=True)
                            mm.then_inc(g_mm, 1)
                            pe.wait_ge(qx_there, b.n + 1)
                            scores(b, 0)
                            scores(b, 1)
                        if c:
                            pe.wait_ge(ogn_there, c.n + 1)
                            if b:
                                pe.wait_ge(g_ev, 2 * b.n + 2)
                            else:
                                pe.wait_ge(ogT_ev, 2 * c.n)
                            for j in range(2):
                                for i in range(CH):
                                    mm = nc.tensor.transpose((A0, A1)[j][:, i * P:(i + 1) * P],
                                                             og[:, i, j * P:(j + 1) * P], c_ident[:])
                            mm.then_inc(ogT_mm, 1)
                        if b:
                            pe.wait_ge(kt_ev, b.n + 1)
                            state(b, 0)
                            outputs(b, 0)
                        if c:
                            pe.wait_ge(ogT_ev, 2 * c.n + 2)
                            if a:
                                pe.wait_ge(xT_ev, a.n + 1)
                            else:
                                wait_count(pe, router.xT_there, c.n - 1)
                            for i in range(CH):
                                for j in range(2):
                                    mm = nc.tensor.matmul(T0[:, i * D:(i + 1) * D], ogT[:, j, i * P:(i + 1) * P],
                                                          w_on[:, j, :], start=(j == 0), stop=(j == 1))
                            mm.then_inc(y_mm, 1)
                        if a:
                            pe.wait_ge(xT_ev, a.n + 1)
                            if c:
                                pe.wait_ge(ogT_ev, 2 * c.n + 2)
                            elif b:
                                pe.wait_ge(g_ev, 2 * b.n + 2)
                            nc.tensor.matmul(A0[:], w_q[:], xT[a.odd][:], start=True, stop=True)
                            nc.tensor.matmul(A1[:], w_qp[:], xT[a.odd][:], start=True, stop=True).then_inc(q_mm, 1)
                        if b:
                            state(b, 1)
                            outputs(b, 1)
                            scores(b, 2)
                        if a:
                            pe.wait_ge(q_ev, a.n + 1)
                            nc.tensor.matmul(A0[:], w_k[:], xT[a.odd][:], start=True, stop=True)
                            nc.tensor.matmul(A1[:], w_kp[:], xT[a.odd][:], start=True, stop=True).then_inc(k_mm, 1)
                        if d:
                            pe.wait_ge(x1_there, d.n + 1)
                            if c:
                                pe.wait_ge(r_there, c.n + 1)
                            else:
                                pe.wait_ge(router.xT_there, d.n)
                            router.transposes(pe, T0, x1[d.odd], d)
                        if b:
                            state(b, 2)
                            scores(b, 3)
                            outputs(b, 2)
                        if a:
                            pe.wait_ge(k_ev, a.n + 1)
                            for j in range(CH):
                                mm = nc.tensor.matmul((A0, A1)[j // 2][:, (j % 2) * 256:(j % 2) * 256 + 256],
                                                      xT[a.odd][:, j * P:(j + 1) * P], w_vg[:, 0:256],
                                                      start=True, stop=True)
                            mm.then_inc(v_mm, 1)
                        if d:
                            if b:
                                pe.wait_ge(kt_ev, b.n + 1)
                            else:
                                pe.wait_ge(router.idx_there, d.n)
                            router.logits_mm(pe, T1, d)
                        if b:
                            outputs(b, 3)
                        if d:
                            router.ranks_mm_(pe, T1, d)

                    run_steps(pe, first, last, SEQS, lags, body)

        def experts(layer):
            F = (F0, F1)[layer]
            FC = F // P
            PAIRS = FC // 2
            ph = ExitStack()
            with ph:
                def sb(name, shape, dt=F32):
                    return ph.enter_context(nc.sbuf_tensor(f"e{layer}_" + name, shape, dt))

                def sem(name):
                    return new_sem(ph, f"e{layer}_" + name)

                zero = sb("zero", [P, ROWS // P, D])
                c_steps = sb("c_steps", [1, STEPS])
                cnt = sb("cnt", [P, E])
                cnt_i = sb("cnt_i", [P, E], I32)
                til_i = sb("til_i", [P, E], I32)
                til = sb("til", [P, E])
                one = sb("one", [P, E])
                cum = sb("cum", [P, E])
                delta = sb("delta", [P, E])
                free_i = sb("free_i", [1, E], I32)
                past = sb("past", [1, STEPS, E])
                past_n = sb("past_n", [1, STEPS, E])
                ex = sb("ex", [1, STEPS])
                before = sb("before", [1, STEPS])
                valid = sb("valid", [1, STEPS])
                rowf = sb("rowf", [1, STEPS])
                rowf2 = sb("rowf2", [1, STEPS])
                exc = sb("exc", [1, STEPS])
                t_ex = sb("t_ex", [1, STEPS], I32)
                t_row = sb("t_row", [1, STEPS], I32)
                pick = sb("pick", [P, SEQS * TOPK * CH, E])
                shift = sb("shift", [P, SEQS * TOPK * CH])
                ex_l = sb("ex_l", [P, TILES, E])
                zsum = sb("zsum", [P, TILES])
                p2 = sb("p2", [P, SEQS, CH])
                dif = sb("dif", [P, SEQS, CH])
                thn = sb("thn", [P, SEQS, CH])

                xg = [sb(f"xg{i}", [P, ROWS // P, D]) for i in range(2)]
                xgT = [sb(f"xgT{i}", [P, ROWS]) for i in range(2)]
                wst = [sb(f"wst{i}", [P, 2, F]) for i in range(2)]
                sgl = [sb(f"sgl{j}", [P, 2, ROWS]) for j in range(2)]
                h = [sb(f"h{i}", [P, FC, ROWS]) for i in range(2)]
                ysb = [sb(f"ysb{i}", [P, ROWS // P, D]) for i in range(2)]
                TP, GB, UB, YB = psum[0:2], psum[2:4], psum[4:6], psum[6:8]

                s_zero, s_steps = sem("zero_set"), sem("steps")
                s_tab, s_free, s_filled = sem("tab"), sem("free"), sem("filled")
                ch_t = Chain(sem("ch_t"))
                ld = [sem(f"ld{i}") for i in range(2)]
                st = [sem(f"st{i}") for i in range(2)]
                x_mm, x_ev, w_there = sem("x_mm"), sem("x_ev"), sem("w_there")
                g_mm, u_mm, sg_there, h_there = sem("g_mm"), sem("u_mm"), sem("sg_there"), sem("h_there")
                y_mm, y_there = sem("y_mm"), sem("y_there")
                s_lx, s_ex, s_dif, s_th = sem("lx"), sem("ex_there"), sem("dif"), sem("th")
                lags = [0, 1, 2, 3]
                first, last = 3, STEPS // 2
                block = ph.enter_context(nc.Block())

                def bank_of(j, t):
                    return j if PAIRS == 2 else t.odd

                def banks_before(t, j):
                    return t.n * PAIRS + j - 1 if PAIRS == 2 else t.n - 1

                @block.sync
                def _(sp):
                    sp.dma_start(c_steps[:], iota_s).then_inc(s_steps, 16)
                    sp.wait_ge(s_zero, 1)
                    sp.dma_start(scattered[E * REGION:E * REGION + ROWS, :].rearrange("(r p) d -> p r d", p=P),
                                 zero[:]).then_inc(s_filled, 16)
                    sp.wait_ge(s_free, 1)
                    for e in range(E):
                        row = sp.value_load(free_i[0:1, e:e + 1], min_val=0, max_val=E * REGION - ROWS)
                        sp.dma_start(scattered[bass.ds(row, ROWS), :].rearrange("(r p) d -> p r d", p=P),
                                     zero[:]).then_inc(s_filled, 16)
                    sp.wait_ge(s_filled, 16 * (E + 1))
                    sp.wait_ge(s_tab, 1)

                    def body(ts):
                        a, _, _, d = ts
                        if a:
                            wait_count(sp, x_mm, a.n - 1)
                            row = sp.value_load(t_row[0:1, bass.ds(a.n, 1)], min_val=0, max_val=E * REGION)
                            sp.dma_start(xg[a.odd][:], scattered[bass.ds(row, ROWS), :].rearrange("(r p) d -> p r d", p=P)
                                         ).then_inc(ld[a.odd], 16)
                        if d:
                            sp.wait_ge(y_there, d.n + 1)
                            sp.dma_start(expert_out[bass.ds(d.n * ROWS, ROWS), :].rearrange("(r p) d -> p r d", p=P),
                                         ysb[d.odd][:]).then_inc(st[d.odd], 16)

                    run_steps(sp, first, last, STEPS, lags, body)
                    for i in range(2):
                        sp.wait_ge(st[i], 16 * STEPS // 2)

                @block.gpsimd
                def _(pool):
                    nc.gpsimd.memset(zero[:], 0.0).then_inc(s_zero, 1)
                    pool.wait_ge(s_tab, 1)
                    pool.wait_ge((s_wx0, s_wx1)[layer], 16 * 3 * E)

                    def body(ts):
                        b = ts[1]
                        if b:
                            wait_count(pool, u_mm, PAIRS * (b.n - 1))
                            e = pool.value_load(t_ex[0:1, bass.ds(b.n, 1)], min_val=0, max_val=E - 1)
                            nc.gpsimd.tensor_copy(wst[b.odd][:], w_gu[:, bass.ds(e, 1), :, 0:F].rearrange(
                                "p o g f -> p (o g) f")).then_inc(w_there, 1)

                    run_steps(pool, first, last, STEPS, lags, body)

                @block.scalar
                def _(act):
                    def body(ts):
                        _, b, c, _ = ts
                        if b:
                            act.wait_ge(x_mm, b.n + 1)
                            nc.scalar.copy(xgT[b.odd][:], TP[b.odd][:, 0:ROWS]).then_inc(x_ev, 1)
                        if c:
                            for j in range(PAIRS):
                                act.wait_ge(g_mm, PAIRS * c.n + j + 1)
                                wait_count(act, h_there, banks_before(c, j))
                                nc.scalar.activation(sgl[bank_of(j, c)][:],
                                                     GB[bank_of(j, c)][:].rearrange("p (k n) -> p k n", k=2),
                                                     ACT.Silu).then_inc(sg_there, 1)

                    if layer == 0:
                        act.wait_ge(s_lx, 1)
                        nc.scalar.activation(ex_l[:], ex_l[:], ACT.Exp)
                        nc.scalar.activation(p2[:], p2[:], ACT.Exp).then_inc(s_ex, 1)
                    act.wait_ge(s_dif, 1)
                    nc.scalar.activation(thn[:], dif[:], ACT.Tanh, scale=0.5).then_inc(s_th, 1)
                    nc.scalar.preload_act_table_set("silu_and_others")
                    run_steps(act, first, last, STEPS, lags, body)

                @block.vector
                def _(dve):
                    L = ch_t.link
                    ch_t.start(dve, Turn(0, 0, 0))
                    nc.vector.memset(one[:], 1.0)
                    nc.vector.tensor_copy(free_i[:], base[0:1, :]).then_inc(s_free, 1)
                    L(nc.vector.tensor_tensor(cnt[:], base[:], c_region[:], ALU.subtract))
                    L(nc.vector.tensor_scalar(cnt_i[:], cnt[:], float(ROWS - 1), None, ALU.add))
                    L(nc.vector.tensor_scalar(til_i[:], cnt_i[:], ROWS.bit_length() - 1, None, ALU.arith_shift_right))
                    L(nc.vector.tensor_copy(til[:], til_i[:]))
                    L(nc.vector.tensor_tensor_scan(cum[:], one[:], til[:], 0.0, ALU.mult, ALU.add))
                    dve.wait_ge(s_steps, 16)
                    L(nc.vector.tensor_tensor(past[:], c_steps[:].unsqueeze(2).to_broadcast([1, STEPS, E]),
                                              cum[0:1, :].unsqueeze(1).to_broadcast([1, STEPS, E]), ALU.is_ge))
                    nc.vector.tensor_reduce(ex[:], past[:], AX.X, ALU.add)
                    L(nc.vector.tensor_tensor(past_n[:], past[:], til[0:1, :].unsqueeze(1).to_broadcast([1, STEPS, E]),
                                              ALU.mult))
                    nc.vector.tensor_scalar(valid[:], ex[:], float(E), None, ALU.is_lt)
                    nc.vector.tensor_scalar(exc[:], ex[:], float(E - 1), None, ALU.min)
                    L(nc.vector.tensor_reduce(before[:], past_n[:], AX.X, ALU.add))
                    L(nc.vector.tensor_tensor(rowf[:], c_steps[:], before[:], ALU.subtract))
                    L(nc.vector.tensor_scalar(rowf[:], rowf[:], float(ROWS), float(-E * REGION), ALU.mult, ALU.add))
                    L(nc.vector.scalar_tensor_tensor(rowf2[:], exc[:], float(REGION), rowf[:], ALU.mult, ALU.add))
                    L(nc.vector.tensor_tensor(rowf2[:], rowf2[:], valid[:], ALU.mult))
                    nc.vector.tensor_copy(t_ex[:], exc[:])
                    nc.vector.tensor_scalar(t_row[:], rowf2[:], float(E * REGION), None, ALU.add).then_inc(s_tab, 1)
                    L(nc.vector.tensor_tensor(delta[:], cum[:], til[:], ALU.subtract))
                    L(nc.vector.scalar_tensor_tensor(delta[:], delta[:], float(ROWS), c_region[:], ALU.mult, ALU.subtract))
                    n = SEQS * TOPK * CH
                    L(nc.vector.tensor_tensor(
                        pick[:], c_iota[:].unsqueeze(1).to_broadcast([P, n, E]),
                        top_i[:].rearrange("p b n -> p (b n)").unsqueeze(2).to_broadcast([P, n, E]), ALU.is_equal))
                    L(nc.vector.tensor_tensor(pick[:], pick[:], delta[:].unsqueeze(1).to_broadcast([P, n, E]), ALU.mult))
                    L(nc.vector.tensor_reduce(shift[:], pick[:], AX.X, ALU.add))
                    L(nc.vector.tensor_tensor(row_c[:].rearrange("p b n -> p (b n)"),
                                              row_r[:].rearrange("p b n -> p (b n)"), shift[:], ALU.add))
                    l1, l2 = top_l[:, :, 0:CH], top_l[:, :, CH:]
                    if layer == 0:
                        nc.vector.tensor_tensor(p2[:], l2, l1, ALU.subtract)
                        def by_seq(a):
                            return a[:].rearrange("p (b c) e -> p b c e", b=SEQS)

                        nc.vector.tensor_tensor(by_seq(ex_l), by_seq(logits), l1.unsqueeze(3).to_broadcast(
                            [P, SEQS, CH, E]), ALU.subtract).then_inc(s_lx, 1)
                        dve.wait_ge(s_ex, 1)
                        nc.vector.tensor_scalar(dif[:], p2[:], -1.0, 1.0, ALU.mult, ALU.add)
                        L(nc.vector.tensor_reduce(zsum[:], ex_l[:], AX.X, ALU.add))
                        L(nc.vector.reciprocal(zsum[:], zsum[:]))
                        nc.vector.tensor_tensor(dif[:], dif[:], zsum[:].rearrange("p (b c) -> p b c", b=SEQS),
                                                ALU.mult).then_inc(s_dif, 1)
                    else:
                        nc.vector.tensor_tensor(dif[:], l1, l2, ALU.subtract).then_inc(s_dif, 1)
                    dve.wait_ge(s_th, 1)
                    nc.vector.tensor_scalar(w_top[:, :, 0:CH], thn[:], 0.5, 0.5, ALU.mult, ALU.add)
                    L(nc.vector.tensor_scalar(w_top[:, :, CH:], thn[:], -0.5, 0.5, ALU.mult, ALU.add))
                    L(nc.vector.tensor_copy(base[:], c_region[:]))
                    ch_t.end()

                    def body(ts):
                        _, _, c, d = ts
                        if c:
                            for j in range(PAIRS):
                                dve.wait_ge(u_mm, PAIRS * c.n + j + 1)
                                dve.wait_ge(sg_there, PAIRS * c.n + j + 1)
                                nc.vector.tensor_tensor(h[c.odd][:, 2 * j:2 * j + 2, :],
                                                        UB[bank_of(j, c)][:].rearrange("p (k n) -> p k n", k=2),
                                                        sgl[bank_of(j, c)][:], ALU.mult).then_inc(h_there, 1)
                        if d:
                            dve.wait_ge(y_mm, d.n + 1)
                            wait_count(dve, st[d.odd], 16 * d.half)
                            nc.vector.tensor_copy(ysb[d.odd][:], YB[d.odd][:, 0:ROWS].rearrange("p (r d) -> p r d", d=D)
                                                  ).then_inc(y_there, 1)

                    run_steps(dve, first, last, STEPS, lags, body)

                @block.tensor
                def _(pe):
                    pe.wait_ge(s_tab, 1)
                    pe.wait_ge((s_wx0, s_wx1)[layer], 16 * 3 * E)

                    def body(ts):
                        _, b, c, d = ts
                        if b:
                            pe.wait_ge(ld[b.odd], b.half * 16 + 16)
                            wait_count(pe, x_ev, b.n - 1)
                            for i in range(ROWS // P):
                                mm = nc.tensor.transpose(TP[b.odd][:, i * P:(i + 1) * P], xg[b.odd][:, i, :], c_ident[:])
                            mm.then_inc(x_mm, 1)
                        if c:
                            pe.wait_ge(w_there, c.n + 1)
                            pe.wait_ge(x_ev, c.n + 1)
                            for j in range(PAIRS):
                                wait_count(pe, h_there, banks_before(c, j))
                                for g, banks, done in ((0, GB, g_mm), (1, UB, u_mm)):
                                    for i in range(2):
                                        f = (2 * j + i) * P
                                        mm = nc.tensor.matmul(banks[bank_of(j, c)][:, i * ROWS:(i + 1) * ROWS],
                                                              wst[c.odd][:, g, f:f + P], xgT[c.odd][:],
                                                              start=True, stop=True)
                                    mm.then_inc(done, 1)
                        if d:
                            pe.wait_ge(h_there, PAIRS * d.n + PAIRS)
                            wait_count(pe, y_there, d.n - 1)
                            e = pe.value_load(t_ex[0:1, bass.ds(d.n, 1)], min_val=0, max_val=E - 1)
                            for i in range(ROWS // P):
                                for f in range(FC):
                                    mm = nc.tensor.matmul(YB[d.odd][:, i * D:(i + 1) * D],
                                                          h[d.odd][:, f, i * P:(i + 1) * P],
                                                          w_dn[:, bass.ds(e, 1), f, :].rearrange("p o d -> p (o d)"),
                                                          start=(f == 0), stop=(f == FC - 1))
                            mm.then_inc(y_mm, 1)

                    run_steps(pe, first, last, STEPS, lags, body)

        class Combine:

            def __init__(self, sb, sem):
                self.idx = [sb(f"ci{i}", [P, TOPK * CH], U32) for i in range(2)]
                self.wt = [sb(f"cw{i}", [P, TOPK * CH]) for i in range(2)]
                self.y = [sb(f"cy{i}", [P, TOPK * CH, D]) for i in range(2)]
                self.r = sb("cr", [P, CH, D])
                self.norm = Norm("cn", sb, sem)
                self.chain = Chain(sem("cchain"))
                self.idx_there = sem("cidx")
                self.got = [sem(f"cgot{i}") for i in range(2)]
                self.used = sem("cused")

            def indices(self, dve, t):
                wait_count(dve, self.got[t.odd], SCATTERS * t.half)
                nc.vector.tensor_copy(self.wt[t.odd][:], w_top[:, bass.ds(t.n, 1), :].rearrange("p o n -> p (o n)"))
                nc.vector.tensor_copy(self.idx[t.odd][:], row_c[:, bass.ds(t.n, 1), :].rearrange("p o n -> p (o n)")
                                      ).then_inc(self.idx_there, 1)

            def gather(self, pool, t):
                pool.wait_ge(self.idx_there, t.n + 1)
                wait_count(pool, self.used, t.n - 1)
                wait_apart(pool, 2 + t.odd)
                for j in range(TOPK * CH):
                    nc.gpsimd.indirect_dma_start(
                        out=self.y[t.odd][:, j, :], out_offset=None, in_=expert_out,
                        in_offset=bass.IndirectOffsetOnAxis(ap=self.idx[t.odd][:, j:j + 1], axis=0)
                    ).then_inc(self.got[t.odd], 16)

            def add(self, dve, t):
                dve.wait_ge(self.got[t.odd], SCATTERS * t.half + SCATTERS)
                dve.wait_ge(self.idx_there, t.n + 1)
                y, w = self.y[t.odd], self.wt[t.odd]
                self.chain.start(dve, t)
                for c in range(CH):
                    last = nc.vector.scalar_tensor_tensor(
                        self.r[:, c, :], y[:, c, :], w[:, c:c + 1],
                        xres[:, bass.ds(t.n * CH + c, 1), :].rearrange("p o d -> p (o d)"), ALU.mult, ALU.add)
                self.chain.link(last)
                for c in range(CH):
                    last = nc.vector.scalar_tensor_tensor(self.r[:, c, :], y[:, CH + c, :], w[:, CH + c:CH + c + 1],
                                                          self.r[:, c, :], ALU.mult, ALU.add)
                last.then_inc(self.used, 1)
                self.chain.end()
                dve.wait_ge(self.used, t.n + 1)
                self.norm.statistics(dve, self.r, t)

        def retention1():
            ph = ExitStack()
            with ph:
                def sb(name, shape, dt=F32):
                    return ph.enter_context(nc.sbuf_tensor("b_" + name, shape, dt))

                def sem(name):
                    return new_sem(ph, "b_" + name)

                w_q, w_k = sb("wq", [P, P]), sb("wk", [P, P])
                w_kv = sb("wkv", [P, 2 * P])
                w_1, w_2 = sb("w1", [P, P]), sb("w2", [P, P])
                g_w, g_b = sb("gw", [P, 1]), sb("gb", [P, 1])
                t_q, t_k = sb("tq", [P, T]), sb("tk", [P, T])
                t_kt = sb("tkt", [P, CH, P])
                m_head = sb("m_head", [P, H1])
                m_blk = sb("m_blk", [P, P])
                w_r = sb("wr", [P, E])
                xb = [sb(f"xb{i}", [P, CH, D]) for i in range(2)]
                xT = [sb(f"xT{i}", [P, T]) for i in range(2)]
                qr = [sb(f"qr{i}", [P, T]) for i in range(2)]
                kT = [sb(f"kT{i}", [P, T]) for i in range(2)]
                qx = [sb(f"qx{i}", [P, CH, H1, P]) for i in range(1)] * 2
                kt = [sb(f"kt{i}", [P, CH, P]) for i in range(2)]
                v = [sb(f"v{i}", [P, CH, P]) for i in range(2)]
                sT = [sb(f"sT{i}", [P, H1, P]) for i in range(2)]
                S = [sb(f"S{i}", [P, P]) for i in range(2)]
                mean = sb("mean", [P, CH * H1])
                mean2 = sb("mean2", [P, CH * H1])
                oc = sb("oc", [P, CH, D])
                osq = sb("osq", [P, CH, D])
                ssq = sb("ssq", [P, CH * H1])
                var = sb("var", [P, CH * H1])
                rstd = sb("rstd", [P, CH * H1])
                sgT = [sb(f"sgT{i}", [P, T]) for i in range(2)]
                sgb = [sb(f"sgb{i}", [P, T]) for i in range(2)]
                oT = sb("oT", [P, T])
                r = sb("r", [P, CH, D])
                x3 = [sb(f"x3{i}", [P, CH, D]) for i in range(2)]
                comb = Combine(sb, sem)
                norm = Norm("n", sb, sem)
                router = Router("r", sb, sem, w_r)
                T0, T1, S0, S1, U, O, A0, A1 = psum
                CHT = CH * H1

                s_w = sem("w")
                x2_there, x2_kept = sem("x2_there"), sem("x2_kept")
                xT_mm, xT_ev = sem("xT_mm"), sem("xT_ev")
                qk_mm, qk_ev, kv_mm, kt_there, v_ev = sem("qk_mm"), sem("qk_ev"), sem("kv_mm"), sem("kt_there"), sem("v_ev")
                qx_dve, qx_act = sem("qx_dve"), sem("qx_act")
                sc_mm, sT_there = sem("sc_mm"), sem("sT_there")
                U_mm, S_there = sem("U_mm"), sem("S_there")
                g_mm, g_ev, gb_there = sem("g_mm"), sem("g_ev"), sem("gb_there")
                o_mm, oc_there, sq_there = sem("o_mm"), sem("oc_there"), sem("sq_there")
                var_there, rstd_there, ocn_there = sem("var_there"), sem("rstd_there"), sem("ocn_there")
                oT_mm, oT_there = sem("oT_mm"), sem("oT_there")
                y_mm, r_there, x3_there, x3_kept = sem("y_mm"), sem("r_there"), sem("x3_there"), sem("x3_kept")
                ch_o, ch_v = Chain(sem("ch_o")), Chain(sem("ch_v"))
                lags = [0, 1, 2, 3, 4, 5]
                first, last = 3, SEQS // 2
                block = ph.enter_context(nc.Block())
                small = [(w_q, bd_q), (w_k, bd_k), (w_kv, bd_kv), (w_1, w1), (w_2, w2), (g_w, gn_w), (g_b, gn_b),
                         (t_q, dec_q), (t_k, dec_k), (t_kt, dec_kt), (m_head, head1), (m_blk, blk1), (w_r, router1)]
                n_w = 16 * len(small)

                @block.sync
                def _(sp):
                    for to, src in small:
                        sp.dma_start(to[:], src).then_inc(s_w, 16)
                    load_experts(sp, 1, s_wx1)

                @block.gpsimd
                def _(pool):
                    def body(ts):
                        z, y, a, b, c, d = ts
                        if y:
                            comb.norm.power(pool, y)
                        if c:
                            norm.power(pool, c)
                        if b:
                            pool.wait_ge(var_there, b.n + 1)
                            nc.gpsimd.tensor_tensor(rstd[:], var[:], c_half[:, 0:CHT], ALU.pow).then_inc(rstd_there, 1)
                        if z:
                            comb.gather(pool, z)
                        if d:
                            router.scatter(pool, x3[d.odd], d)

                    run_steps(pool, first, last, SEQS, lags, body)
                    for i in range(2):
                        pool.wait_ge(router.sent[i], SCATTERS * SEQS // 2)

                @block.scalar
                def _(act):
                    act.wait_ge(s_w, n_w)

                    def body(ts):
                        z, y, a, b, c, d = ts
                        if a:
                            act.wait_ge(xT_mm, a.n + 1)
                            nc.scalar.copy(xT[a.odd][:], T0[:, :]).then_inc(xT_ev, 1)
                            nc.scalar.copy(xres[:, bass.ds(a.n * CH, CH), :], xb[a.odd][:]).then_inc(x2_kept, 1)
                        if b:
                            act.wait_ge(g_mm, b.n + 1)
                            wait_count(act, gb_there, b.n - 1)
                            nc.scalar.activation(sgT[b.odd][:], T1[:, :], ACT.Silu).then_inc(g_ev, 1)
                        if d:
                            act.wait_ge(x3_there, d.n + 1)
                            nc.scalar.copy(xres[:, bass.ds(d.n * CH, CH), :], x3[d.odd][:]).then_inc(x3_kept, 1)
                            act.wait_ge(router.tp, d.n + 1)
                            nc.scalar.copy(router.xT[:], T0[:, :]).then_inc(router.xT_there, 1)
                        if a:
                            act.wait_ge(kv_mm, a.n + 1)
                            for j, bank in enumerate((A0, A1)):
                                act.wait_ge(kt_there, 2 * a.n + j + 1)
                                nc.scalar.copy(v[a.odd][:, 2 * j:2 * j + 2, :],
                                               bank[:].rearrange("p (c n) -> p c n", c=2)[:, :, P:2 * P]).then_inc(v_ev, 1)
                        if b:
                            act.wait_ge(oc_there, b.n + 1)
                            nc.scalar.activation(osq[:], oc[:], ACT.Square).then_inc(sq_there, 1)
                        if a:
                            act.wait_ge(qk_ev, 2 * a.n + 2)
                            wait_count(act, sc_mm, 2 * CH * a.n)
                            for hd in range(H1 // 2, H1):
                                li = nc.scalar.activation(qx[a.odd][:, :, hd, :],
                                                          qr[a.odd][:].rearrange("p (c t) -> p c t", c=CH),
                                                          ACT.Copy, scale=m_head[:, hd:hd + 1])
                            li.then_inc(qx_act, 1)

                    nc.scalar.preload_act_table_set("silu_and_others")
                    run_steps(act, first, last, SEQS, lags, body)

                @block.vector
                def _(dve):
                    dve.wait_ge(s_w, n_w)

                    def masked_scores(b, c):
                        for j, bank in enumerate((S0, S1)):
                            dve.wait_ge(sc_mm, 2 * CH * b.n + 2 * c + j + 1)
                            nc.vector.tensor_tensor(sT[c % 2][:, 4 * j:4 * j + 4, :],
                                                    bank[:].rearrange("p (h t) -> p h t", h=4),
                                                    c_causal[:].unsqueeze(1).to_broadcast([P, 4, P]),
                                                    ALU.mult).then_inc(sT_there, 1)

                    def state(b, c):
                        dve.wait_ge(U_mm, (CH - 1) * b.n + c + 1)
                        nc.vector.tensor_tensor(S[c % 2][:], U[:, 0:P], m_blk[:], ALU.mult).then_inc(S_there, 1)

                    def body(ts):
                        z, y, a, b, c, d = ts
                        if c:
                            dve.wait_ge(rstd_there, c.n + 1)
                            nc.vector.tensor_tensor(
                                oc[:].rearrange("p c (h n) -> p (c h) n", h=H1),
                                oc[:].rearrange("p c (h n) -> p (c h) n", h=H1),
                                rstd[:].unsqueeze(2).to_broadcast([P, CHT, DH1]), ALU.mult).then_inc(ocn_there, 1)
                        if z:
                            comb.indices(dve, z)
                        if b:
                            masked_scores(b, 0)
                            state(b, 0)
                            dve.wait_ge(g_ev, b.n + 1)
                            nc.vector.tensor_scalar(sgb[b.odd][:], sgT[b.odd][:], g_b[:, 0:1], None, ALU.add
                                                    ).then_inc(gb_there, 1)
                        if c:
                            dve.wait_ge(oT_mm, c.n + 1)
                            dve.wait_ge(gb_there, c.n + 1)
                            nc.vector.scalar_tensor_tensor(oT[:], T1[:], g_w[:, 0:1], sgb[c.odd][:], ALU.mult, ALU.add
                                                           ).then_inc(oT_there, 1)
                        if y:
                            wait_count(dve, x2_there, y.n)
                            comb.add(dve, y)
                        if b:
                            masked_scores(b, 1)
                        if c:
                            dve.wait_ge(y_mm, c.n + 1)
                            dve.wait_ge(x2_kept, c.n + 1)
                            nc.vector.tensor_tensor(r[:], T0[:].rearrange("p (c d) -> p c d", c=CH),
                                                    xres[:, bass.ds(c.n * CH, CH), :], ALU.add).then_inc(r_there, 1)
                            dve.wait_ge(r_there, c.n + 1)
                            norm.statistics(dve, r, c)
                        if a:
                            dve.wait_ge(qk_mm, a.n + 1)
                            nc.vector.tensor_tensor(qr[a.odd][:], A0[:], t_q[:], ALU.mult).then_inc(qk_ev, 1)
                            nc.vector.tensor_tensor(kT[a.odd][:], A1[:], t_k[:], ALU.mult).then_inc(qk_ev, 1)
                        if b:
                            state(b, 1)
                            masked_scores(b, 2)
                        if y:
                            wait_count(dve, xT_mm, y.n - 1)
                            wait_count(dve, x2_kept, y.n - 1)
                            comb.norm.apply(dve, comb.r, xb[y.odd], y, x2_there)
                        if b:
                            state(b, 2)
                        if c:
                            wait_count(dve, router.sent[c.odd], SCATTERS * c.half)
                            wait_count(dve, x3_kept, c.n - 1)
                            norm.apply(dve, r, x3[c.odd], c, x3_there)
                        if d:
                            router.choose(dve, T1, d)
                        if b:
                            masked_scores(b, 3)
                        if a:
                            dve.wait_ge(kv_mm, a.n + 1)
                            for j, bank in enumerate((A0, A1)):
                                nc.vector.tensor_tensor(kt[a.odd][:, 2 * j:2 * j + 2, :],
                                                        bank[:].rearrange("p (c n) -> p c n", c=2)[:, :, 0:P],
                                                        t_kt[:, 2 * j:2 * j + 2, :], ALU.mult).then_inc(kt_there, 1)
                        if b:
                            dve.wait_ge(o_mm, b.n + 1)
                            ch_o.start(dve, b)
                            o_v = O[:].rearrange("p (g n) -> p g n", n=DH1)
                            ch_o.link(nc.vector.tensor_reduce(mean[:], o_v, AX.X, ALU.add))
                            ch_o.link(nc.vector.tensor_scalar(mean2[:], mean[:], 1.0 / DH1, None, ALU.mult))
                            ch_o.end()
                            nc.vector.tensor_tensor(oc[:].rearrange("p c (h n) -> p (c h) n", h=H1), o_v,
                                                    mean2[:].unsqueeze(2).to_broadcast([P, CHT, DH1]),
                                                    ALU.subtract).then_inc(oc_there, 1)
                        if d:
                            router.rows_of(dve, T1, d)
                        if a:
                            wait_count(dve, sc_mm, 2 * CH * a.n)
                            for hd in range(H1 // 2):
                                li = nc.vector.tensor_scalar(qx[a.odd][:, :, hd, :],
                                                             qr[a.odd][:].rearrange("p (c t) -> p c t", c=CH),
                                                             m_head[:, hd:hd + 1], None, ALU.mult)
                            li.then_inc(qx_dve, 1)
                        if b:
                            dve.wait_ge(sq_there, b.n + 1)
                            ch_v.start(dve, b)
                            ch_v.link(nc.vector.tensor_reduce(ssq[:], osq[:].rearrange("p c (h n) -> p (c h) n", h=H1),
                                                              AX.X, ALU.add))
                            ch_v.end()
                            nc.vector.tensor_scalar(var[:], ssq[:], 1.0 / DH1, LN_EPS, ALU.mult, ALU.add
                                                    ).then_inc(var_there, 1)

                    run_steps(dve, first, last, SEQS, lags, body)

                @block.tensor
                def _(pe):
                    pe.wait_ge(s_w, n_w)

                    def scores(b, c):
                        for j, bank in enumerate((S0, S1)):
                            wait_count(pe, sT_there, 2 * CH * b.n + 2 * c + j - 1)
                            nc.tensor.matmul(bank[:], kT[b.odd][:, c * P:(c + 1) * P],
                                             qx[b.odd][:, c, 4 * j:4 * j + 4, :].rearrange("p h t -> p (h t)"),
                                             start=True, stop=True).then_inc(sc_mm, 1)

                    def state(b, c):
                        wait_count(pe, S_there, (CH - 1) * b.n + c)
                        nc.tensor.matmul(U[:, 0:P], kt[b.odd][:, c, :], v[b.odd][:, c, :],
                                         start=(c == 0), stop=(c == CH - 2), skip_group_check=True).then_inc(U_mm, 1)

                    def outputs(b, c):
                        at = c * D
                        if c == 0:
                            wait_count(pe, oc_there, b.n)
                        else:
                            pe.wait_ge(S_there, (CH - 1) * b.n + c)
                            nc.tensor.matmul(O[:, at:at + D], qr[b.odd][:, c * P:(c + 1) * P], S[(c - 1) % 2][:],
                                             start=False, stop=False, skip_group_check=True)
                        pe.wait_ge(sT_there, 2 * CH * b.n + 2 * c + 2)
                        for hd in range(H1):
                            mm = nc.tensor.matmul(O[:, at + hd * DH1:at + (hd + 1) * DH1], sT[c % 2][:, hd, :],
                                                  v[b.odd][:, c, hd * DH1:(hd + 1) * DH1],
                                                  start=(c == 0 and hd == 0), stop=(hd == H1 - 1), skip_group_check=True)
                        if c == CH - 1:
                            mm.then_inc(o_mm, 1)

                    def body(ts):
                        z, y, a, b, c, d = ts
                        if a:
                            pe.wait_ge(x2_there, a.n + 1)
                            wait_count(pe, router.xT_there, a.n - 3)
                            wait_count(pe, r_there, a.n - 2)
                            wait_count(pe, xT_ev, a.n)
                            for j in range(CH):
                                mm = nc.tensor.transpose(T0[:, j * P:(j + 1) * P], xb[a.odd][:, j, :], c_ident[:])
                            mm.then_inc(xT_mm, 1)
                        if b:
                            pe.wait_ge(qx_dve, b.n + 1)
                            pe.wait_ge(qx_act, b.n + 1)
                            scores(b, 0)
                            wait_count(pe, router.idx_there, b.n - 2)
                            wait_count(pe, oT_there, b.n - 1)
                            wait_count(pe, g_ev, b.n)
                            nc.tensor.matmul(T1[:], w_1[:], xT[b.odd][:], start=True, stop=True).then_inc(g_mm, 1)
                            pe.wait_ge(v_ev, 2 * b.n + 2)
                            state(b, 0)
                        if c:
                            pe.wait_ge(ocn_there, c.n + 1)
                            if b:
                                pe.wait_ge(g_ev, b.n + 1)
                            else:
                                pe.wait_ge(router.idx_there, c.n - 1)
                            for i in range(CH):
                                mm = nc.tensor.transpose(T1[:, i * P:(i + 1) * P], oc[:, i, :], c_ident[:])
                            mm.then_inc(oT_mm, 1)
                        if b:
                            scores(b, 1)
                            outputs(b, 0)
                        if c:
                            pe.wait_ge(oT_there, c.n + 1)
                            if a:
                                pe.wait_ge(xT_ev, a.n + 1)
                            else:
                                wait_count(pe, router.xT_there, c.n - 1)
                            for i in range(CH):
                                mm = nc.tensor.matmul(T0[:, i * D:(i + 1) * D], oT[:, i * P:(i + 1) * P], w_2[:],
                                                      start=True, stop=True)
                            mm.then_inc(y_mm, 1)
                        if a:
                            pe.wait_ge(xT_ev, a.n + 1)
                            wait_count(pe, v_ev, 2 * a.n)
                            nc.tensor.matmul(A0[:], w_q[:], xT[a.odd][:], start=True, stop=True)
                            nc.tensor.matmul(A1[:], w_k[:], xT[a.odd][:], start=True, stop=True).then_inc(qk_mm, 1)
                        if b:
                            state(b, 1)
                            scores(b, 2)
                            outputs(b, 1)
                        if d:
                            pe.wait_ge(x3_there, d.n + 1)
                            if c:
                                pe.wait_ge(r_there, c.n + 1)
                            else:
                                pe.wait_ge(router.xT_there, d.n)
                            router.transposes(pe, T0, x3[d.odd], d)
                        if b:
                            state(b, 2)
                            outputs(b, 2)
                        if d:
                            if c:
                                pe.wait_ge(oT_there, c.n + 1)
                            else:
                                pe.wait_ge(router.idx_there, d.n)
                            router.logits_mm(pe, T1, d)
                        if b:
                            scores(b, 3)
                        if a:
                            pe.wait_ge(qk_ev, 2 * a.n + 2)
                            for j in range(CH):
                                mm = nc.tensor.matmul((A0, A1)[j // 2][:, (j % 2) * 256:(j % 2) * 256 + 256],
                                                      xT[a.odd][:, j * P:(j + 1) * P], w_kv[:],
                                                      start=True, stop=True)
                            mm.then_inc(kv_mm, 1)
                        if b:
                            outputs(b, 3)
                        if d:
                            router.ranks_mm_(pe, T1, d)

                    run_steps(pe, first, last, SEQS, lags, body)

        def finish():
            ph = ExitStack()
            with ph:
                def sb(name, shape, dt=F32):
                    return ph.enter_context(nc.sbuf_tensor("f_" + name, shape, dt))

                def sem(name):
                    return new_sem(ph, "f_" + name)

                x4 = [sb(f"x4{i}", [P, CH, D]) for i in range(2)]
                comb = Combine(sb, sem)
                x4_there = sem("x4_there")
                stored = [sem(f"stored{i}") for i in range(2)]
                lags = [0, 1, 2]
                first, last = 2, SEQS // 2
                block = ph.enter_context(nc.Block())

                @block.gpsimd
                def _(pool):
                    def body(ts):
                        z, y, w = ts
                        if z:
                            comb.gather(pool, z)
                        if y:
                            comb.norm.power(pool, y)

                    run_steps(pool, first, last, SEQS, lags, body)

                @block.vector
                def _(dve):
                    def body(ts):
                        z, y, w = ts
                        if z:
                            comb.indices(dve, z)
                        if y:
                            wait_count(dve, x4_there, y.n)
                            comb.add(dve, y)
                            wait_count(dve, stored[y.odd], 16 * y.half)
                            comb.norm.apply(dve, comb.r, x4[y.odd], y, x4_there)

                    run_steps(dve, first, last, SEQS, lags, body)

                @block.sync
                def _(sp):
                    def body(ts):
                        y = ts[1]
                        if y:
                            sp.wait_ge(x4_there, y.n + 1)
                            sp.dma_start(out_seq[:, bass.ds(y.n, 1)].rearrange("p b c d -> p (b c) d"),
                                         x4[y.odd][:]).then_inc(stored[y.odd], 16)

                    run_steps(sp, first, last, SEQS, lags, body)
                    for i in range(2):
                        sp.wait_ge(stored[i], 16 * SEQS // 2)

        for phase in (retention0, lambda: experts(0), retention1, lambda: experts(1)):
            phase()
            clear_semaphores()
        finish()


def constants():
    import numpy as np

    f = np.float32
    t = np.arange(T, dtype=f)
    inv = (f(1.0) / np.power(f(10000.0), np.arange(0, DK0, 2, dtype=f) / f(DK0))).astype(f)
    ang = (t[:, None] * inv[None, :]).astype(f).astype(np.float64)
    half = DK0 // 2
    log0 = np.log1p(-np.exp2(-5.0 - np.arange(H0)))
    hd = np.arange(P)
    j = hd % DK0
    cos = np.cos(ang).T[j % half]
    sin = np.sin(ang).T[j % half] * np.where(j < half, -1.0, 1.0)[:, None]
    fall = np.exp(log0[hd // DK0][:, None] * t[None, :].astype(np.float64))
    rope_q = np.stack([cos, sin], 1) * (fall * DK0 ** -0.5)[:, None, :]
    rope_k = np.stack([cos, sin], 1) / fall[:, None, :]
    lin = np.linspace(np.log(1.0 / 512.0), np.log(1.0 / 32.0), H1)
    gam = (1.0 - np.exp(lin)).astype(f).astype(np.float64)[hd // DH1]
    dec_q = gam[:, None] ** t[None, :].astype(np.float64)
    dec_k = 1.0 / dec_q
    dec_kt = dec_k.T.reshape(CH, P, P).transpose(1, 0, 2)
    ins = {
        "rope_q": rope_q, "rope_k": rope_k, "dec_q": dec_q, "dec_k": dec_k, "dec_kt": dec_kt,
        "ident": np.eye(P), "causal": hd[None, :] >= hd[:, None],
        "head0": (hd // DK0)[:, None] == np.arange(H0)[None, :],
        "head1": (hd // DH1)[:, None] == np.arange(H1)[None, :],
        "blk0": (hd // DK0)[:, None] == (np.arange(H0 * DV0) // DV0)[None, :],
        "blk1": (hd // DH1)[:, None] == (hd // DH1)[None, :],
        "iota_e": np.tile(np.arange(E), (P, 1)), "region0": np.tile(np.arange(E) * REGION, (P, 1)),
        "iota_s": np.arange(STEPS)[None, :], "tri": hd[:, None] < hd[None, :],
    }
    out = {k: np.ascontiguousarray(a, dtype=f) for k, a in ins.items()}
    return out


def block_diagonal(w):
    import numpy as np

    n, a, b = w.shape
    full = np.zeros((n * a, n * b), w.dtype)
    for i in range(n):
        full[i * a:(i + 1) * a, i * b:(i + 1) * b] = w[i]
    return full


def kernel(**inputs):
    import numpy as np
    import concourse.bacc as bacc
    from concourse.bass_utils import run_bass_kernel_spmd

    g = {k: np.asarray(v) for k, v in inputs.items()}
    swap = (np.arange(P) // DK0) * DK0 + (np.arange(P) + DK0 // 2) % DK0
    wq, wk = g["L0_attn_Wq"], g["L0_attn_Wk"]
    bd_k, bd_v = block_diagonal(g["L1_attn_Wk"]), block_diagonal(g["L1_attn_Wv"])
    arrays = {
        "x": g["L0_attn_x"], "wq": wq.T, "wqp": wq[swap].T, "wk": wk.T, "wkp": wk[swap].T,
        "wvg": np.concatenate([g["L0_attn_Wv"].T, g["L0_attn_Wg"].T], 1),
        "wo": g["L0_attn_Wo"].T.reshape(2, P, D).transpose(1, 0, 2),
        "gnorm": np.tile(g["L0_attn_g_norm_w"], 2)[:, None],
        "router0": g["L0_ffn_router_kernel_DE"], "gate0": g["L0_ffn_kernel_gating_EDF"],
        "up0": g["L0_ffn_kernel_up_EDF"], "down0": g["L0_ffn_kernel_down_EFD"],
        "bd_q": block_diagonal(g["L1_attn_Wq"]), "bd_k": bd_k, "bd_kv": np.concatenate([bd_k, bd_v], 1),
        "w1": g["L1_attn_W1"], "w2": g["L1_attn_W2"],
        "gn_w": g["L1_attn_gn_w"][:, None], "gn_b": g["L1_attn_gn_b"][:, None],
        "router1": g["L1_ffn_Wg"], "gate1": g["L1_ffn_W1"], "up1": g["L1_ffn_W3"], "down1": g["L1_ffn_W2"],
        **constants(),
    }
    order = ["x", "wq", "wqp", "wk", "wkp", "wvg", "wo", "gnorm", "rope_q", "rope_k", "router0", "gate0", "up0",
             "down0", "bd_q", "bd_k", "bd_kv", "w1", "w2", "gn_w", "gn_b", "dec_q", "dec_k", "dec_kt", "router1",
             "gate1", "up1", "down1", "ident", "causal", "tri", "head0", "head1", "blk0", "blk1", "iota_e",
             "region0", "iota_s"]
    nc = bacc.Bacc("TRN2", target_bir_lowering=False, num_devices=1)
    given, args = {}, []
    for name in order:
        a = np.ascontiguousarray(arrays[name])
        given[f"in_{name}"] = a
        args.append(nc.dram_tensor(f"in_{name}", a.shape, mybir.dt.from_np(a.dtype), kind="ExternalInput").ap())
    args.append(nc.dram_tensor("out_0", (SEQS, T, D), F32, kind="ExternalOutput").ap())
    build(nc, *args)
    r = run_bass_kernel_spmd(nc, [given], core_ids=[0])
    return r.results[0]["out_0"]
```

```python
import concourse.bass as bass
from concourse import mybir
from contextlib import ExitStack

P = 128
SEQS, T, D = 16, 512, 128
CH = T // P
TILES = SEQS * CH
TOKENS = SEQS * T
E, TOPK = 8, 2
ROWS = 256
STEPS = TOKENS * TOPK // ROWS + E
REGION = TOKENS + ROWS
LN_EPS = 1e-5
H0, DK0, DV0 = 4, 32, 64
H1, DH1 = 8, 16
F0, F1 = 256, 512

F32 = mybir.dt.float32
F32R = mybir.dt.float32r
BF16 = mybir.dt.bfloat16
I32 = mybir.dt.int32
U32 = mybir.dt.uint32
ALU = mybir.AluOpType
ACT = mybir.ActivationFunctionType
AX = mybir.AxisListType


class Turn:

    def __init__(self, n, half, odd):
        self.n, self.half, self.odd = n, half, odd


def turn(i, sub, lag, count):
    k = sub - lag
    if isinstance(i, int):
        n = 2 * i + k
        return Turn(n, n // 2, n % 2) if 0 <= n < count else None
    return Turn(i * 2 + k, i + k // 2, k % 2)


def wait_count(eng, sem, n):
    if isinstance(n, int) and n <= 0:
        return
    eng.wait_ge(sem, n)


class Chain:

    def __init__(self, sem):
        self.sem, self.per, self.k = sem, 0, 0

    def start(self, eng, t):
        self.eng, self.t, self.k = eng, t, 0

    def link(self, ins):
        self.k += 1
        ins.then_inc(self.sem, 1)
        self.eng.wait_ge(self.sem, self.t.n * self.per + self.k)

    def end(self):
        assert self.per in (0, self.k)
        self.per = self.k


def run_steps(eng, first, last, count, lags, body, between=()):
    total = count + max(lags)
    for s in range(2 * first):
        body([turn(s // 2, s % 2, lag, count) for lag in lags])
        if s < len(between):
            between[s]()
    with eng.Fori(first, last) as i:
        for sub in range(2):
            body([turn(i, sub, lag, count) for lag in lags])
    for s in range(2 * last, total):
        body([turn(s // 2, s % 2, lag, count) for lag in lags])


def build(nc, x, wq, wqp, wk, wkp, wvg, wo, gnorm, rope_q, rope_k, router0, gate0, up0, down0,
          bd_q, bd_k, bd_vT, center, w1, w2, gn_w, gn_b, dec_q, dec_k, router1, gate1, up1, down1,
          ident, causal, tri, head0, head1, blk0, blk1, iota_e, region0, iota_s, out):
    scattered = nc.dram_tensor("scattered", ((E + 1) * REGION, D), F32, kind="Internal").ap()
    expert_out = nc.dram_tensor("expert_out", (STEPS * ROWS, D), F32, kind="Internal").ap()
    x_seq = x.rearrange("b (c p) d -> p b c d", p=P)
    out_seq = out.rearrange("b (c p) d -> p b c d", p=P)

    whole = ExitStack()
    with whole:
        def keep(name, shape, dt=F32):
            return whole.enter_context(nc.sbuf_tensor(name, shape, dt))

        c_ident = keep("c_ident", [P, P])
        c_causal = keep("c_causal", [P, P])
        c_tri = keep("c_tri", [P, P], BF16)
        c_ones = keep("c_ones", [P, P], BF16)
        c_iota = keep("c_iota", [P, E])
        c_region = keep("c_region", [P, E])
        c_half = keep("c_half", [P, 2 * T // 16])
        xres = keep("xres", [P, TILES, D])
        top_l = keep("top_l", [P, SEQS, TOPK * CH])
        top_i = keep("top_i", [P, SEQS, TOPK * CH])
        row_r = keep("row_r", [P, SEQS, TOPK * CH])
        logits = keep("logits", [P, TILES, E])
        row_c = keep("row_c", [P, SEQS, TOPK * CH], U32)
        w_top = keep("w_top", [P, SEQS, TOPK * CH])
        base = keep("base", [P, E])
        c_steps = keep("c_steps", [1, STEPS])
        zero = keep("zero", [P, ROWS // P, D])
        t_ex = keep("t_ex", [1, STEPS], I32)
        t_row = keep("t_row", [1, STEPS], I32)
        delta = keep("delta", [P, E])
        psum = [whole.enter_context(nc.psum_tensor(f"bank{i}", [P, 512], F32)) for i in range(8)]
        s_const = whole.enter_context(nc.semaphore("s_const"))
        s_cset = whole.enter_context(nc.semaphore("s_cset"))
        w_gu = keep("w_gu", [P, E, 2, F1])
        w_dn = keep("w_dn", [P, E, F1 // P, D])
        s_wx0 = whole.enter_context(nc.semaphore("s_wx0"))
        s_wx1 = whole.enter_context(nc.semaphore("s_wx1"))

        def load_expert(sp, layer, e, sem):
            g, u, dn, f = ((gate0, up0, down0, F0), (gate1, up1, down1, F1))[layer]
            sp.dma_start(w_gu[:, e, 0, 0:f], g[e]).then_inc(sem, 16)
            sp.dma_start(w_gu[:, e, 1, 0:f], u[e]).then_inc(sem, 16)
            sp.dma_start(w_dn[:, e, 0:f // P, :], dn[e].rearrange("(j p) d -> p j d", p=P)).then_inc(sem, 16)

        used = []

        def new_sem(phase, name):
            used.append(phase.enter_context(nc.semaphore(name)))
            return used[-1]

        def clear_semaphores():
            with nc.Block() as between:
                @between.gpsimd
                def _(pool):
                    numbers = sorted(s.num for s in used)
                    at = 0
                    while at < len(numbers):
                        to = at
                        while to + 1 < len(numbers) and numbers[to + 1] == numbers[to] + 1:
                            to += 1
                        pool.sem_clear(range(numbers[at], numbers[to] + 1))
                        at = to + 1
            used.clear()

        mark = keep("mark", [1, 5])

        def wait_apart(eng, at=4):
            if eng is nc.gpsimd:
                return nc.gpsimd.tensor_tensor(mark[:, at:at + 1], c_half[0:1, 0:1], c_half[0:1, 0:1], ALU.add)
            return nc.vector.memset(mark[:, at:at + 1], 0.0)

        class InverseRoot:

            def __init__(self, name, sb, sem, n):
                self.half = sb(name + "_half", [P, n])
                self.bits = sb(name + "_bits", [P, n], I32)
                self.sq = sb(name + "_sq", [P, n])
                self.y = sb(name + "_y", [P, n])
                self.chain = Chain(sem(name + "_chain"))

            def compute(self, dve, v, t):
                L = self.chain.link
                self.chain.start(dve, t)
                nc.vector.tensor_scalar(self.half[:], v[:], -0.5, None, ALU.mult)
                L(nc.vector.tensor_scalar(self.bits[:], v[:].bitcast(I32), 1, None, ALU.arith_shift_right))
                L(nc.vector.tensor_scalar(self.y[:].bitcast(I32), self.bits[:], -1.0, float(0x5F3759DF),
                                          ALU.mult, ALU.add))
                for _ in range(3):
                    L(nc.vector.tensor_tensor(self.sq[:], self.y[:], self.y[:], ALU.mult))
                    L(nc.vector.tensor_tensor(self.sq[:], self.sq[:], self.half[:], ALU.mult))
                    L(nc.vector.scalar_tensor_tensor(self.y[:], self.sq[:], 1.5, self.y[:], ALU.add, ALU.mult))
                self.chain.end()

        class Norm:

            def __init__(self, name, sb, sem):
                self.neg = sb(name + "_neg", [P, CH])
                self.bias = sb(name + "_bias", [P, CH])
                self.powed = Chain(sem(name + "_powed"))
                self.stats = sb(name + "_stats", [P, CH, 6])
                self.mv = sb(name + "_mv", [P, CH, 2])
                self.ve = sb(name + "_ve", [P, CH])
                self.rstd = sb(name + "_rstd", [P, CH])
                self.chain = Chain(sem(name + "_chain"))
                self.var = sem(name + "_var")
                self.inv = sem(name + "_inv")

            def statistics(self, dve, r, t):
                for c in range(CH):
                    last = nc.vector.bn_stats(self.stats[:, c, :], r[:, c, :])
                self.chain.start(dve, t)
                self.chain.link(last)
                wait_apart(dve)
                for c in range(CH):
                    last = nc.vector.bn_aggr(self.mv[:, c, :], self.stats[:, c, :])
                self.chain.link(last)
                self.chain.end()
                nc.vector.tensor_scalar(self.neg[:], self.mv[:, :, 0], -1.0, None, ALU.mult)
                nc.vector.tensor_scalar(self.ve[:], self.mv[:, :, 1], LN_EPS, None, ALU.add).then_inc(self.var, 1)

            def power(self, pool, t):
                pool.wait_ge(self.var, t.n + 1)
                self.powed.start(pool, t)
                self.powed.link(nc.gpsimd.tensor_tensor(self.rstd[:], self.ve[:], c_half[:, 0:CH], ALU.pow))
                self.powed.end()
                nc.gpsimd.tensor_tensor(self.bias[:], self.neg[:], self.rstd[:], ALU.mult).then_inc(self.inv, 1)

            def apply(self, act, r, to, t, done):
                act.wait_ge(self.inv, t.n + 1)
                for c in range(CH):
                    last = nc.scalar.activation(to[:, c, :], r[:, c, :], ACT.Identity, bias=self.bias[:, c:c + 1],
                                                scale=self.rstd[:, c:c + 1])
                last.then_inc(done, 1)

        class NormDve(Norm):

            def __init__(self, name, sb, sem):
                super().__init__(name, sb, sem)
                self.root = InverseRoot(name + "_root", sb, sem, CH)

            def apply(self, dve, r, to, t, done):
                dve.wait_ge(self.var, t.n + 1)
                self.root.compute(dve, self.ve, t)
                for c in range(CH):
                    last = nc.vector.tensor_scalar(to[:, c, :], r[:, c, :], self.mv[:, c, 0:1],
                                                   self.root.y[:, c:c + 1], ALU.subtract, ALU.mult)
                last.then_inc(done, 1)

        class Router:

            def __init__(self, name, sb, sem, w_router):
                self.w = w_router
                self.xT = sb(name + "_xT", [P, T])
                self.lg = sb(name + "_lg", [P, CH, E])
                self.mx = sb(name + "_mx", [P, CH, 8])
                self.mi = sb(name + "_mi", [P, CH, 8], U32)
                self.ix = sb(name + "_ix", [P, TOPK, CH])
                self.pick = sb(name + "_pick", [P, TOPK * CH, E])
                self.picked = sb(name + "_picked", [P, CH, E], BF16)
                self.rows = sb(name + "_rows", [P, CH, E])
                self.rowk = sb(name + "_rowk", [P, TOPK * CH, E])
                self.dst = sb(name + "_dst", [P, TOPK * CH])
                self.idx = [sb(f"{name}_idx{i}", [P, TOPK * CH], U32) for i in range(2)]
                self.chain = Chain(sem(name + "_chain"))
                self.chain2 = Chain(sem(name + "_chain2"))
                self.tp = sem(name + "_tp")
                self.xT_there = sem(name + "_xT_there")
                self.lg_mm = sem(name + "_lg_mm")
                self.picks = sem(name + "_picks")
                self.ranks_mm = sem(name + "_ranks_mm")
                self.idx_there = sem(name + "_idx_there")
                self.sent = [sem(f"{name}_sent{i}") for i in range(2)]

            def transposes(self, pe, bank, xb, t):
                for c in range(CH):
                    last = nc.tensor.transpose(bank[:, c * P:(c + 1) * P], xb[:, c, :], c_ident[:])
                last.then_inc(self.tp, 1)

            def logits_mm(self, pe, bank, t):
                pe.wait_ge(self.xT_there, t.n + 1)
                wait_count(pe, self.idx_there, t.n)
                for c in range(CH):
                    last = nc.tensor.matmul(bank[:, c * E:(c + 1) * E], self.xT[:, c * P:(c + 1) * P],
                                            self.w[:], start=True, stop=True)
                last.then_inc(self.lg_mm, 1)

            def choose(self, dve, bank, t):
                ch = self.chain
                dve.wait_ge(self.lg_mm, t.n + 1)
                ch.start(dve, t)
                lg = bank[:, 0:CH * E].rearrange("p (c e) -> p c e", c=CH)
                nc.vector.tensor_copy(logits[:, bass.ds(t.n * CH, CH), :], lg)
                ch.link(nc.vector.tensor_copy(self.lg[:], lg))
                wait_apart(dve)
                for c in range(CH):
                    last = nc.vector.max(self.mx[:, c, :], self.lg[:, c, :])
                ch.link(last)
                wait_apart(dve)
                for c in range(CH):
                    last = nc.vector.max_index(self.mi[:, c, :], self.mx[:, c, :], self.lg[:, c, :])
                ch.link(last)
                nc.vector.tensor_copy(top_l[:, bass.ds(t.n, 1), :].rearrange("p o (k c) -> p (o k) c", k=TOPK),
                                      self.mx[:, :, 0:TOPK].rearrange("p c k -> p k c"))
                ch.link(nc.vector.tensor_copy(self.ix[:], self.mi[:, :, 0:TOPK].rearrange("p c k -> p k c")))
                nc.vector.tensor_copy(top_i[:, bass.ds(t.n, 1), :].rearrange("p o n -> p (o n)"),
                                      self.ix[:].rearrange("p k c -> p (k c)"))
                ch.link(nc.vector.tensor_tensor(
                    self.pick[:], c_iota[:].unsqueeze(1).to_broadcast([P, TOPK * CH, E]),
                    self.ix[:].rearrange("p k c -> p (k c)").unsqueeze(2).to_broadcast([P, TOPK * CH, E]),
                    ALU.is_equal))
                ch.end()
                nc.vector.tensor_tensor(self.picked[:], self.pick[:, 0:CH, :], self.pick[:, CH:, :],
                                        ALU.add).then_inc(self.picks, 1)

            def ranks_mm_(self, pe, bank, t):
                pe.wait_ge(self.picks, t.n + 1)
                m = self.picked
                nc.tensor.matmul(bank[:, 0:CH * E], c_tri[:], m[:].rearrange("p c e -> p (c e)"),
                                 start=True, stop=False, skip_group_check=True)
                for c in range(CH - 1):
                    later = CH - 1 - c
                    nc.tensor.matmul(bank[:, (c + 1) * E:CH * E].rearrange("p (c e) -> p c e", e=E), c_ones[:],
                                     m[:, c:c + 1, :].to_broadcast([P, later, E]),
                                     start=False, stop=False, skip_group_check=True)
                for c in range(CH):
                    last = nc.tensor.matmul(bank[:, CH * E:CH * E + E], c_ones[:], m[:, c, :],
                                            start=False, stop=(c == CH - 1), skip_group_check=True)
                last.then_inc(self.ranks_mm, 1)

            def rows_of(self, dve, bank, t):
                ch = self.chain2
                dve.wait_ge(self.ranks_mm, t.n + 1)
                ch.start(dve, t)
                ch.link(nc.vector.tensor_tensor(
                    self.rows[:], bank[:, 0:CH * E].rearrange("p (c e) -> p c e", c=CH),
                    base[:].unsqueeze(1).to_broadcast([P, CH, E]), ALU.add))
                nc.vector.tensor_tensor(base[:], bank[:, CH * E:CH * E + E], base[:], ALU.add)
                for k in range(TOPK):
                    last = nc.vector.tensor_tensor(self.rowk[:, k * CH:(k + 1) * CH, :],
                                                   self.pick[:, k * CH:(k + 1) * CH, :], self.rows[:], ALU.mult)
                ch.link(last)
                ch.link(nc.vector.tensor_reduce(self.dst[:], self.rowk[:], AX.X, ALU.add))
                nc.vector.tensor_copy(row_r[:, bass.ds(t.n, 1), :].rearrange("p o n -> p (o n)"), self.dst[:])
                ch.end()
                nc.vector.tensor_copy(self.idx[t.odd][:], self.dst[:]).then_inc(self.idx_there, 1)

            def scatter(self, pool, xb, t):
                pool.wait_ge(self.idx_there, t.n + 1)
                wait_apart(pool, t.odd)
                for k in range(TOPK):
                    for c in range(CH):
                        j = k * CH + c
                        nc.gpsimd.indirect_dma_start(
                            out=scattered[0:E * REGION, :],
                            out_offset=bass.IndirectOffsetOnAxis(ap=self.idx[t.odd][:, j:j + 1], axis=0),
                            in_=xb[:, c, :], in_offset=None).then_inc(self.sent[t.odd], 16)

        class Tiles:

            def __init__(self, sb, sem):
                self.cnt, self.til, self.one, self.cum = (sb("t_" + n, [P, E]) for n in ("cnt", "til", "one", "cum"))
                self.cnt_i, self.til_i = sb("t_cnt_i", [P, E], I32), sb("t_til_i", [P, E], I32)
                self.free_i = sb("t_free_i", [1, E], I32)
                self.past, self.past_n = sb("t_past", [1, STEPS, E]), sb("t_past_n", [1, STEPS, E])
                self.ex, self.exc, self.before, self.valid, self.rowf, self.rowf2 = (
                    sb("t_" + n, [1, STEPS]) for n in ("ex", "exc", "before", "valid", "rowf", "rowf2"))
                self.free, self.filled = sem("t_free"), sem("t_filled")
                self.chain = Chain(sem("t_chain"))

            def fill(self, sp):
                sp.dma_start(scattered[E * REGION:E * REGION + ROWS, :].rearrange("(r p) d -> p r d", p=P),
                             zero[:]).then_inc(self.filled, 16)
                sp.wait_ge(self.free, 1)
                for e in range(E):
                    row = sp.value_load(self.free_i[0:1, e:e + 1], min_val=0, max_val=E * REGION - ROWS)
                    sp.dma_start(scattered[bass.ds(row, ROWS), :].rearrange("(r p) d -> p r d", p=P),
                                 zero[:]).then_inc(self.filled, 16)
                sp.wait_ge(self.filled, 16 * (E + 1))

            def table(self, dve):
                L = self.chain.link
                self.chain.start(dve, Turn(0, 0, 0))
                cnt, til, cum, ex, exc, rowf, rowf2 = (
                    self.cnt, self.til, self.cum, self.ex, self.exc, self.rowf, self.rowf2)
                L(nc.vector.memset(self.one[:], 1.0))
                nc.vector.tensor_copy(self.free_i[:], base[0:1, :]).then_inc(self.free, 1)
                L(nc.vector.tensor_tensor(cnt[:], base[:], c_region[:], ALU.subtract))
                L(nc.vector.tensor_scalar(self.cnt_i[:], cnt[:], float(ROWS - 1), None, ALU.add))
                L(nc.vector.tensor_scalar(self.til_i[:], self.cnt_i[:], ROWS.bit_length() - 1, None,
                                          ALU.arith_shift_right))
                L(nc.vector.tensor_copy(til[:], self.til_i[:]))
                L(nc.vector.tensor_tensor_scan(cum[:], self.one[:], til[:], 0.0, ALU.mult, ALU.add))
                L(nc.vector.tensor_tensor(self.past[:], c_steps[:].unsqueeze(2).to_broadcast([1, STEPS, E]),
                                          cum[0:1, :].unsqueeze(1).to_broadcast([1, STEPS, E]), ALU.is_ge))
                nc.vector.tensor_reduce(ex[:], self.past[:], AX.X, ALU.add)
                L(nc.vector.tensor_tensor(self.past_n[:], self.past[:],
                                          til[0:1, :].unsqueeze(1).to_broadcast([1, STEPS, E]), ALU.mult))
                nc.vector.tensor_scalar(self.valid[:], ex[:], float(E), None, ALU.is_lt)
                nc.vector.tensor_scalar(exc[:], ex[:], float(E - 1), None, ALU.min)
                L(nc.vector.tensor_reduce(self.before[:], self.past_n[:], AX.X, ALU.add))
                L(nc.vector.tensor_tensor(rowf[:], c_steps[:], self.before[:], ALU.subtract))
                L(nc.vector.tensor_scalar(rowf[:], rowf[:], float(ROWS), float(-E * REGION), ALU.mult, ALU.add))
                L(nc.vector.scalar_tensor_tensor(rowf2[:], exc[:], float(REGION), rowf[:], ALU.mult, ALU.add))
                L(nc.vector.tensor_tensor(rowf2[:], rowf2[:], self.valid[:], ALU.mult))
                nc.vector.tensor_copy(t_ex[:], exc[:])
                nc.vector.tensor_scalar(t_row[:], rowf2[:], float(E * REGION), None, ALU.add)
                L(nc.vector.tensor_tensor(delta[:], cum[:], til[:], ALU.subtract))
                nc.vector.scalar_tensor_tensor(delta[:], delta[:], float(ROWS), c_region[:], ALU.mult, ALU.subtract)

        SCATTERS = 16 * TOPK * CH

        def retention0():
            ph = ExitStack()
            with ph:
                def sb(name, shape, dt=F32):
                    return ph.enter_context(nc.sbuf_tensor("a_" + name, shape, dt))

                def sem(name):
                    return new_sem(ph, "a_" + name)

                w_q, w_qp, w_k, w_kp = (sb(n, [P, P]) for n in ("wq", "wqp", "wk", "wkp"))
                w_vg = sb("wvg", [P, 2 * H0 * DV0])
                w_o = sb("wo", [P, 2, D])
                w_on = sb("won", [P, 2, D])
                tri_f = sb("tri_f", [P, P])
                g_n = sb("gn", [P, 1])
                t_q = sb("rope_q", [P, 2, T])
                t_k = sb("rope_k", [P, 2, T])
                m_head = sb("m_head", [P, H0])
                m_blk = sb("m_blk", [P, H0 * DV0])
                w_r = sb("wr", [P, E])
                xb = [sb(f"xb{i}", [P, CH, D]) for i in range(2)]
                xT = [sb(f"xT{i}", [P, T]) for i in range(2)]
                qm = sb("qm", [P, 2, T])
                km = sb("km", [P, 2, T])
                qr = [sb(f"qr{i}", [P, T]) for i in range(2)]
                kT = [sb(f"kT{i}", [P, T]) for i in range(2)]
                qx = [sb(f"qx{i}", [P, CH, H0, P]) for i in range(2)]
                v = [sb(f"v{i}", [P, CH, H0 * DV0]) for i in range(2)]
                kt = sb("kt", [P, CH - 1, P])
                sg = sb("sg", [P, CH, H0 * DV0])
                sT = [sb(f"sT{i}", [P, H0, P]) for i in range(2)]
                S = [sb(f"S{i}", [P, H0 * DV0]) for i in range(2)]
                osq = sb("osq", [P, CH, H0 * DV0])
                og = sb("og", [P, CH, H0 * DV0])
                ssq = sb("ssq", [P, CH * H0])
                mse = sb("mse", [P, CH * H0])
                root = InverseRoot("rms", sb, sem, CH * H0)
                ogT = sb("ogT", [P, 2, T])
                r = sb("r", [P, CH, D])
                x1 = [sb(f"x1{i}", [P, CH, D]) for i in range(2)]
                norm = Norm("n", sb, sem)
                router = Router("r", sb, sem, w_r)
                tiles = Tiles(sb, sem)
                T0, T1, S0, S1, U, O, A0, A1 = psum
                LG, RK = U[:, 256:256 + CH * E], U[:, 384:384 + CH * E + E]

                s_x = [sem(f"x{i}") for i in range(2)]
                s_xr = sem("xr")
                s_w = sem("w")
                s_wo = sem("wo_scaled")
                xT_mm, xT_ev = sem("xT_mm"), sem("xT_ev")
                q_mm, k_mm, v_mm, g_mm = sem("q_mm"), sem("k_mm"), sem("v_mm"), sem("g_mm")
                q_ev, k_ev, v_ev, g_ev = sem("q_ev"), sem("k_ev"), sem("v_ev"), sem("g_ev")
                qr_there, qx_there, kT_there = sem("qr_there"), sem("qx_there"), sem("kT_there")
                kt_mm, kt_ev = sem("kt_mm"), sem("kt_ev")
                sc_mm, sT_there = sem("sc_mm"), sem("sT_there")
                U_mm, S_there = sem("U_mm"), sem("S_there")
                o_mm, sq_there, og_there = sem("o_mm"), sem("sq_there"), sem("og_there")
                ogn_there = sem("ogn_there")
                ogT_mm, ogT_ev = sem("ogT_mm"), sem("ogT_ev")
                y_mm, r_there, x1_there, x1_kept = sem("y_mm"), sem("r_there"), sem("x1_there"), sem("x1_kept")
                ch_ss = Chain(sem("ch_ss"))
                lags = [0, 1, 2, 3]
                first, last = 2, SEQS // 2
                block = ph.enter_context(nc.Block())

                @block.sync
                def _(sp):
                    sp.dma_start(c_ident[:], ident).then_inc(s_const, 16)
                    small = [(w_q, wq), (w_qp, wqp), (w_k, wk), (w_kp, wkp), (w_vg, wvg), (t_q, rope_q), (t_k, rope_k),
                             (m_head, head0), (m_blk, blk0), (w_o, wo), (g_n, gnorm), (w_r, router0)]
                    consts = [(c_causal, causal), (c_iota, iota_e), (c_region, region0), (c_steps, iota_s)]

                    def load(t):
                        wait_count(sp, xT_mm, t.n - 1)
                        sp.dma_start(xb[t.odd][:], x_seq[:, bass.ds(t.n, 1)].rearrange("p b c d -> p (b c) d")
                                     ).then_inc(s_x[t.odd], 16)

                    def body(ts):
                        if ts[0] is None:
                            return
                        load(ts[0])
                        if isinstance(ts[0].n, int) and ts[0].n == 0:
                            for to, src in small:
                                sp.dma_start(to[:], src).then_inc(s_w, 16)
                            for to, src in consts:
                                sp.dma_start(to[:], src).then_inc(s_const, 16)
                            sp.dma_start(tri_f[:], tri).then_inc(s_const, 16)
                        if isinstance(ts[0].n, int) and ts[0].n == 1:
                            for q in range(4):
                                sp.dma_start(xres[:, q * 16:(q + 1) * 16, :],
                                             x_seq[:, q * 4:(q + 1) * 4].rearrange("p b c d -> p (b c) d")
                                             ).then_inc(s_xr, 16)
                        if isinstance(ts[0].n, int) and 2 <= ts[0].n < 2 + E:
                            load_expert(sp, 0, ts[0].n - 2, s_wx0)

                    run_steps(sp, (2 + E) // 2, last, SEQS, [0], body)
                    sp.wait_ge(s_cset, 3)
                    tiles.fill(sp)

                n_w, n_const = 16 * 12, 16 * 6

                @block.gpsimd
                def _(pool):
                    nc.gpsimd.memset(c_half[:], -0.5).then_inc(s_cset, 1)
                    nc.gpsimd.memset(c_ones[:], 1.0).then_inc(s_cset, 1)
                    nc.gpsimd.memset(zero[:], 0.0).then_inc(s_cset, 1)
                    pool.wait_ge(s_cset, 2)

                    def body(ts):
                        _, b, c, d = ts
                        if c:
                            norm.power(pool, c)
                        if d:
                            router.scatter(pool, x1[d.odd], d)

                    run_steps(pool, first, last, SEQS, lags, body)
                    for i in range(2):
                        pool.wait_ge(router.sent[i], SCATTERS * SEQS // 2)

                @block.scalar
                def _(act):
                    def body(ts):
                        a, b, c, d = ts
                        if a:
                            act.wait_ge(xT_mm, a.n + 1)
                            nc.scalar.copy(xT[a.odd][:], T0[:, :]).then_inc(xT_ev, 1)
                        if b:
                            wait_count(act, og_there, 2 * b.n)
                            act.wait_ge(g_mm, b.n + 1)
                            for j, bank in enumerate((A0, A1)):
                                nc.scalar.activation(sg[:, 2 * j:2 * j + 2, :],
                                                     bank[:].rearrange("p (c n) -> p c n", c=2),
                                                     ACT.Silu).then_inc(g_ev, 1)
                        if d:
                            act.wait_ge(router.tp, d.n + 1)
                            nc.scalar.copy(router.xT[:], T0[:, :]).then_inc(router.xT_there, 1)
                        if b:
                            act.wait_ge(kt_mm, b.n + 1)
                            nc.scalar.copy(kt[:], T1[:, 0:(CH - 1) * P].rearrange("p (c k) -> p c k", c=CH - 1)
                                           ).then_inc(kt_ev, 1)
                        if d:
                            act.wait_ge(x1_there, d.n + 1)
                            nc.scalar.copy(xres[:, bass.ds(d.n * CH, CH), :], x1[d.odd][:]).then_inc(x1_kept, 1)
                        if b:
                            wait_count(act, ch_ss.sem, 2 * b.n - 1)
                            act.wait_ge(o_mm, 2 * b.n + 1)
                            nc.scalar.activation(osq[:, 0:2, :], O[:].rearrange("p (c n) -> p c n", c=2),
                                                 ACT.Square).then_inc(sq_there, 1)
                        if c:
                            act.wait_ge(ogT_mm, c.n + 1)
                            for j, bank in enumerate((T0, T1)):
                                nc.scalar.copy(ogT[:, j, :], bank[:, :]).then_inc(ogT_ev, 1)
                        if a:
                            act.wait_ge(qr_there, a.n + 1)
                            wait_count(act, sc_mm, CH * (a.n - 1))
                            for h in range(H0):
                                last_i = nc.scalar.activation(
                                    qx[a.odd][:, :, h, :], qr[a.odd][:].rearrange("p (c t) -> p c t", c=CH),
                                    ACT.Copy, scale=m_head[:, h:h + 1])
                            last_i.then_inc(qx_there, 1)
                        if a:
                            act.wait_ge(v_mm, a.n + 1)
                            for j, bank in enumerate((A0, A1)):
                                nc.scalar.copy(v[a.odd][:, 2 * j:2 * j + 2, :],
                                               bank[:].rearrange("p (c n) -> p c n", c=2)).then_inc(v_ev, 1)
                        if c:
                            wait_count(act, router.sent[c.odd], SCATTERS * c.half)
                            wait_count(act, x1_kept, c.n - 1)
                            norm.apply(act, r, x1[c.odd], c, x1_there)
                        if b:
                            act.wait_ge(o_mm, 2 * b.n + 2)
                            nc.scalar.activation(osq[:, 2:4, :], O[:].rearrange("p (c n) -> p c n", c=2),
                                                 ACT.Square).then_inc(sq_there, 1)

                    act.wait_ge(s_w, n_w)
                    nc.scalar.preload_act_table_set("silu_and_others")
                    run_steps(act, first, last, SEQS, lags, body)

                @block.vector
                def _(dve):
                    dve.wait_ge(s_w, n_w)
                    dve.wait_ge(s_const, n_const)
                    nc.vector.tensor_copy(base[:], c_region[:])
                    nc.vector.tensor_copy(c_tri[:], tri_f[:])
                    nc.vector.tensor_scalar(w_on[:], w_o[:], g_n[:, 0:1], None, ALU.mult).then_inc(s_wo, 1)
                    dve.wait_ge(s_wo, 1)
                    dve.wait_ge(s_xr, 64)

                    def masked_scores(b, c):
                        dve.wait_ge(sc_mm, CH * b.n + c + 1)
                        nc.vector.tensor_tensor(sT[c % 2][:], (S0, S1)[c % 2][:].rearrange("p (h t) -> p h t", h=H0),
                                                c_causal[:].unsqueeze(1).to_broadcast([P, H0, P]),
                                                ALU.mult).then_inc(sT_there, 1)

                    def state(b, c):
                        dve.wait_ge(U_mm, (CH - 1) * b.n + c + 1)
                        nc.vector.tensor_tensor(S[c % 2][:], U[:, 0:H0 * DV0], m_blk[:], ALU.mult).then_inc(S_there, 1)

                    def gated(b, j):
                        dve.wait_ge(sq_there, 2 * b.n + j + 1)
                        dve.wait_ge(g_ev, 2 * b.n + 2)
                        nc.vector.tensor_tensor(og[:, 2 * j:2 * j + 2, :], O[:].rearrange("p (c n) -> p c n", c=2),
                                                sg[:, 2 * j:2 * j + 2, :], ALU.mult).then_inc(og_there, 1)

                    def body(ts):
                        a, b, c, d = ts
                        if b:
                            masked_scores(b, 0)
                            masked_scores(b, 1)
                            state(b, 0)
                        if c:
                            ch_ss.start(dve, c)
                            ch_ss.link(nc.vector.tensor_reduce(ssq[:], osq[:].rearrange("p c (h n) -> p (c h) n", h=H0),
                                                               AX.X, ALU.add))
                            ch_ss.link(nc.vector.tensor_scalar(mse[:], ssq[:], 1.0 / DV0, LN_EPS, ALU.mult, ALU.add))
                            ch_ss.end()
                            root.compute(dve, mse, c)
                            nc.vector.tensor_tensor(
                                og[:].rearrange("p c (h n) -> p (c h) n", h=H0),
                                og[:].rearrange("p c (h n) -> p (c h) n", h=H0),
                                root.y[:].unsqueeze(2).to_broadcast([P, CH * H0, DV0]), ALU.mult).then_inc(ogn_there, 1)
                        if b:
                            state(b, 1)
                        if a:
                            dve.wait_ge(q_mm, a.n + 1)
                            for j, bank in enumerate((A0, A1)):
                                last_i = nc.vector.tensor_tensor(qm[:, j, :], bank[:], t_q[:, j, :], ALU.mult)
                            last_i.then_inc(q_ev, 1)
                        if b:
                            masked_scores(b, 2)
                        if a:
                            dve.wait_ge(q_ev, a.n + 1)
                            nc.vector.tensor_tensor(qr[a.odd][:], qm[:, 0, :], qm[:, 1, :], ALU.add).then_inc(qr_there, 1)
                        if b:
                            if c:
                                dve.wait_ge(ogT_mm, c.n + 1)
                            gated(b, 0)
                            state(b, 2)
                        if d:
                            router.choose(dve, LG, d)
                        if a:
                            dve.wait_ge(k_mm, a.n + 1)
                            for j, bank in enumerate((A0, A1)):
                                last_i = nc.vector.tensor_tensor(km[:, j, :], bank[:], t_k[:, j, :], ALU.mult)
                            last_i.then_inc(k_ev, 1)
                        if b:
                            masked_scores(b, 3)
                        if a:
                            dve.wait_ge(k_ev, a.n + 1)
                            nc.vector.tensor_tensor(kT[a.odd][:], km[:, 0, :], km[:, 1, :], ALU.add).then_inc(kT_there, 1)
                        if c:
                            dve.wait_ge(y_mm, c.n + 1)
                            wait_count(dve, x1_there, c.n)
                            nc.vector.tensor_tensor(r[:], T0[:].rearrange("p (c d) -> p c d", c=CH),
                                                    xres[:, bass.ds(c.n * CH, CH), :], ALU.add).then_inc(r_there, 1)
                            dve.wait_ge(r_there, c.n + 1)
                            norm.statistics(dve, r, c)
                        if d:
                            router.rows_of(dve, RK, d)
                        if b:
                            gated(b, 1)

                    run_steps(dve, first, last, SEQS, lags, body)
                    tiles.table(dve)

                @block.tensor
                def _(pe):
                    pe.wait_ge(s_const, n_const)
                    pe.wait_ge(s_w, n_w)
                    pe.wait_ge(s_wo, 1)

                    def scores(b, c):
                        wait_count(pe, sT_there, CH * b.n + c - 1)
                        nc.tensor.matmul((S0, S1)[c % 2][:], kT[b.odd][:, c * P:(c + 1) * P],
                                         qx[b.odd][:, c].rearrange("p h t -> p (h t)"),
                                         start=True, stop=True).then_inc(sc_mm, 1)

                    def state(b, c):
                        wait_count(pe, S_there, (CH - 1) * b.n + c)
                        nc.tensor.matmul(U[:, 0:H0 * DV0], kt[:, c, :], v[b.odd][:, c, :],
                                         start=(c == 0), stop=(c == CH - 2), skip_group_check=True).then_inc(U_mm, 1)

                    def outputs(b, c):
                        at = (c % 2) * H0 * DV0
                        if c % 2 == 0:
                            wait_count(pe, og_there, 2 * b.n + c // 2)
                        if c:
                            pe.wait_ge(S_there, (CH - 1) * b.n + c)
                            nc.tensor.matmul(O[:, at:at + H0 * DV0], qr[b.odd][:, c * P:(c + 1) * P], S[(c - 1) % 2][:],
                                             start=(c % 2 == 0), stop=False, skip_group_check=True)
                        pe.wait_ge(sT_there, CH * b.n + c + 1)
                        for h in range(H0):
                            mm = nc.tensor.matmul(O[:, at + h * DV0:at + (h + 1) * DV0], sT[c % 2][:, h, :],
                                                  v[b.odd][:, c, h * DV0:(h + 1) * DV0],
                                                  start=(c == 0 and h == 0), stop=(h == H0 - 1), skip_group_check=True)
                        if c % 2:
                            mm.then_inc(o_mm, 1)

                    def body(ts):
                        a, b, c, d = ts
                        if a:
                            pe.wait_ge(s_x[a.odd], a.half * 16 + 16)
                            wait_count(pe, r_there, a.n - 2)
                            wait_count(pe, xT_ev, a.n)
                            for j in range(CH):
                                mm = nc.tensor.transpose(T0[:, j * P:(j + 1) * P], xb[a.odd][:, j, :], c_ident[:])
                            mm.then_inc(xT_mm, 1)
                        if b:
                            pe.wait_ge(v_ev, 2 * b.n + 2)
                            for j in range(CH):
                                mm = nc.tensor.matmul((A0, A1)[j // 2][:, (j % 2) * 256:(j % 2) * 256 + 256],
                                                      xT[b.odd][:, j * P:(j + 1) * P], w_vg[:, 256:512],
                                                      start=True, stop=True)
                            mm.then_inc(g_mm, 1)
                            pe.wait_ge(qx_there, b.n + 1)
                            pe.wait_ge(kT_there, b.n + 1)
                            scores(b, 0)
                        if d:
                            pe.wait_ge(x1_there, d.n + 1)
                            if a:
                                pe.wait_ge(xT_ev, a.n + 1)
                            router.transposes(pe, T0, x1[d.odd], d)
                        if b:
                            wait_count(pe, ogT_ev, 2 * (b.n - 1))
                            wait_count(pe, kt_ev, b.n)
                            for j in range(CH - 1):
                                mm = nc.tensor.transpose(T1[:, j * P:(j + 1) * P], kT[b.odd][:, j * P:(j + 1) * P],
                                                         c_ident[:])
                            mm.then_inc(kt_mm, 1)
                            scores(b, 1)
                        if d:
                            router.logits_mm(pe, LG, d)
                        if b:
                            pe.wait_ge(kt_ev, b.n + 1)
                            state(b, 0)
                            outputs(b, 0)
                        if a:
                            pe.wait_ge(xT_ev, a.n + 1)
                            if b:
                                pe.wait_ge(g_ev, 2 * b.n + 2)
                            nc.tensor.matmul(A0[:], w_q[:], xT[a.odd][:], start=True, stop=True)
                            nc.tensor.matmul(A1[:], w_qp[:], xT[a.odd][:], start=True, stop=True).then_inc(q_mm, 1)
                        if b:
                            state(b, 1)
                            scores(b, 2)
                            outputs(b, 1)
                        if c:
                            pe.wait_ge(ogn_there, c.n + 1)
                            if d:
                                pe.wait_ge(router.xT_there, d.n + 1)
                            else:
                                pe.wait_ge(xT_ev, a.n + 1)
                            if b:
                                pe.wait_ge(kt_ev, b.n + 1)
                            for j in range(2):
                                for i in range(CH):
                                    mm = nc.tensor.transpose((T0, T1)[j][:, i * P:(i + 1) * P],
                                                             og[:, i, j * P:(j + 1) * P], c_ident[:])
                            mm.then_inc(ogT_mm, 1)
                        if a:
                            pe.wait_ge(q_ev, a.n + 1)
                            nc.tensor.matmul(A0[:], w_k[:], xT[a.odd][:], start=True, stop=True)
                            nc.tensor.matmul(A1[:], w_kp[:], xT[a.odd][:], start=True, stop=True).then_inc(k_mm, 1)
                        if b:
                            state(b, 2)
                        if c:
                            pe.wait_ge(ogT_ev, 2 * c.n + 2)
                            for i in range(CH):
                                for j in range(2):
                                    mm = nc.tensor.matmul(T0[:, i * D:(i + 1) * D], ogT[:, j, i * P:(i + 1) * P],
                                                          w_on[:, j, :], start=(j == 0), stop=(j == 1))
                            mm.then_inc(y_mm, 1)
                        if b:
                            scores(b, 3)
                        if d:
                            router.ranks_mm_(pe, RK, d)
                        if b:
                            outputs(b, 2)
                        if a:
                            pe.wait_ge(k_ev, a.n + 1)
                            for j in range(CH):
                                mm = nc.tensor.matmul((A0, A1)[j // 2][:, (j % 2) * 256:(j % 2) * 256 + 256],
                                                      xT[a.odd][:, j * P:(j + 1) * P], w_vg[:, 0:256],
                                                      start=True, stop=True)
                            mm.then_inc(v_mm, 1)
                        if b:
                            outputs(b, 3)

                    run_steps(pe, first, last, SEQS, lags, body)

        def experts(layer):
            F = (F0, F1)[layer]
            FC = F // P
            PAIRS = FC // 2
            ph = ExitStack()
            with ph:
                def sb(name, shape, dt=F32):
                    return ph.enter_context(nc.sbuf_tensor(f"e{layer}_" + name, shape, dt))

                def sem(name):
                    return new_sem(ph, f"e{layer}_" + name)

                pick = sb("pick", [P, SEQS * TOPK * CH, E])
                shift = sb("shift", [P, SEQS * TOPK * CH])
                ex_l = sb("ex_l", [P, TILES, E])
                zsum = sb("zsum", [P, TILES])
                p2 = sb("p2", [P, SEQS, CH])
                dif = sb("dif", [P, SEQS, CH])
                thn = sb("thn", [P, SEQS, CH])

                xg = [sb(f"xg{i}", [P, ROWS // P, D]) for i in range(2)]
                x_hi = [sb(f"x_hi{i}", [P, ROWS], F32R) for i in range(2)]
                x_lo = [sb(f"x_lo{i}", [P, ROWS], F32R) for i in range(2)]
                w_hi = [sb(f"w_hi{i}", [P, 2, F], F32R) for i in range(2)]
                w_lo = [sb(f"w_lo{i}", [P, 2, F], F32R) for i in range(2)]
                sgl = [sb(f"sgl{j}", [P, 2, ROWS]) for j in range(2)]
                h = [sb(f"h{i}", [P, FC, ROWS]) for i in range(2)]
                ysb = [sb(f"ysb{i}", [P, ROWS // P, D]) for i in range(2)]
                TP, GB, UB, YB = psum[0:2], psum[2:4], psum[4:6], psum[6:8]

                ch_r = Chain(sem("ch_r"))
                n_top = SEQS * TOPK * CH
                ld = [sem(f"ld{i}") for i in range(2)]
                st = [sem(f"st{i}") for i in range(2)]
                x_mm, x_hi_there, x_ev = sem("x_mm"), sem("x_hi_there"), sem("x_ev")
                w_hi_there, w_there = sem("w_hi_there"), sem("w_there")
                g_mm, u_mm, sg_there, h_there = sem("g_mm"), sem("u_mm"), sem("sg_there"), sem("h_there")
                y_mm, y_there = sem("y_mm"), sem("y_there")
                s_lx, s_ex, s_dif, s_th = sem("lx"), sem("ex_there"), sem("dif"), sem("th")
                lags = [0, 1, 2, 3]
                first, last = 3, STEPS // 2
                block = ph.enter_context(nc.Block())

                def bank_of(j, t):
                    return j if PAIRS == 2 else t.odd

                def banks_before(t, j):
                    return t.n * PAIRS + j - 1 if PAIRS == 2 else t.n - 1

                @block.sync
                def _(sp):
                    def body(ts):
                        a, d = ts
                        if a:
                            wait_count(sp, x_mm, a.n - 1)
                            row = sp.value_load(t_row[0:1, bass.ds(a.n, 1)], min_val=0, max_val=E * REGION)
                            sp.dma_start(xg[a.odd][:], scattered[bass.ds(row, ROWS), :].rearrange("(r p) d -> p r d", p=P)
                                         ).then_inc(ld[a.odd], 16)
                        if d:
                            sp.wait_ge(y_there, d.n + 1)
                            sp.dma_start(expert_out[bass.ds(d.n * ROWS, ROWS), :].rearrange("(r p) d -> p r d", p=P),
                                         ysb[d.odd][:]).then_inc(st[d.odd], 16)

                    run_steps(sp, first, last, STEPS, [0, lags[-1] + 1], body)
                    for i in range(2):
                        sp.wait_ge(st[i], 16 * STEPS // 2)

                @block.scalar
                def _(act):
                    def body(ts):
                        _, b, c, _ = ts
                        if b:
                            wait_count(act, u_mm, PAIRS * (b.n - 1))
                            e = act.value_load(t_ex[0:1, bass.ds(b.n, 1)], min_val=0, max_val=E - 1)
                            nc.scalar.copy(w_hi[b.odd][:], w_gu[:, bass.ds(e, 1), :, 0:F].rearrange(
                                "p o g f -> p (o g) f")).then_inc(w_hi_there, 1)
                            act.wait_ge(x_mm, b.n + 1)
                            nc.scalar.copy(x_hi[b.odd][:], TP[b.odd][:, 0:ROWS]).then_inc(x_hi_there, 1)
                        if c:
                            for j in range(PAIRS):
                                act.wait_ge(g_mm, PAIRS * c.n + j + 1)
                                wait_count(act, h_there, banks_before(c, j))
                                nc.scalar.activation(sgl[bank_of(j, c)][:],
                                                     GB[bank_of(j, c)][:].rearrange("p (k n) -> p k n", k=2),
                                                     ACT.Silu).then_inc(sg_there, 1)

                    def exp_piece():
                        if layer == 0:
                            act.wait_ge(s_lx, 1)
                            nc.scalar.activation(ex_l[:], ex_l[:], ACT.Exp)
                            nc.scalar.activation(p2[:], p2[:], ACT.Exp).then_inc(s_ex, 1)
                            nc.scalar.preload_act_table_set("silu_and_others")

                    def tanh_piece():
                        act.wait_ge(s_dif, 1)
                        nc.scalar.activation(thn[:], dif[:], ACT.Tanh, scale=0.5).then_inc(s_th, 1)

                    def nothing():
                        pass

                    act.wait_ge((s_wx0, s_wx1)[layer], 16 * 3 * E)
                    nc.scalar.preload_act_table_set("silu_and_others")
                    run_steps(act, first, last, STEPS, lags, body,
                              [nothing, nothing, nothing, exp_piece, tanh_piece])

                @block.vector
                def _(dve):
                    def rows_piece():
                        ch_r.start(dve, Turn(0, 0, 0))
                        L = ch_r.link
                        L(nc.vector.tensor_tensor(
                            pick[:], c_iota[:].unsqueeze(1).to_broadcast([P, n_top, E]),
                            top_i[:].rearrange("p b n -> p (b n)").unsqueeze(2).to_broadcast([P, n_top, E]),
                            ALU.is_equal))

                    def shift_piece():
                        L = ch_r.link
                        L(nc.vector.tensor_tensor(pick[:], pick[:], delta[:].unsqueeze(1).to_broadcast([P, n_top, E]),
                                                  ALU.mult))
                        L(nc.vector.tensor_reduce(shift[:], pick[:], AX.X, ALU.add))
                        nc.vector.tensor_tensor(row_c[:].rearrange("p b n -> p (b n)"),
                                                row_r[:].rearrange("p b n -> p (b n)"), shift[:], ALU.add)

                    l1, l2 = top_l[:, :, 0:CH], top_l[:, :, CH:]

                    def difference_piece():
                        if layer:
                            nc.vector.tensor_tensor(dif[:], l1, l2, ALU.subtract).then_inc(s_dif, 1)
                            return
                        nc.vector.tensor_tensor(p2[:], l2, l1, ALU.subtract)

                        def by_seq(a):
                            return a[:].rearrange("p (b c) e -> p b c e", b=SEQS)

                        nc.vector.tensor_tensor(by_seq(ex_l), by_seq(logits), l1.unsqueeze(3).to_broadcast(
                            [P, SEQS, CH, E]), ALU.subtract).then_inc(s_lx, 1)

                    def probabilities_piece():
                        if layer:
                            return
                        L = ch_r.link
                        dve.wait_ge(s_ex, 1)
                        nc.vector.tensor_scalar(dif[:], p2[:], -1.0, 1.0, ALU.mult, ALU.add)
                        L(nc.vector.tensor_reduce(zsum[:], ex_l[:], AX.X, ALU.add))
                        L(nc.vector.reciprocal(zsum[:], zsum[:]))
                        nc.vector.tensor_tensor(dif[:], dif[:], zsum[:].rearrange("p (b c) -> p b c", b=SEQS),
                                                ALU.mult).then_inc(s_dif, 1)

                    def weights_piece():
                        dve.wait_ge(s_th, 1)
                        nc.vector.tensor_scalar(w_top[:, :, 0:CH], thn[:], 0.5, 0.5, ALU.mult, ALU.add)
                        nc.vector.tensor_scalar(w_top[:, :, CH:], thn[:], -0.5, 0.5, ALU.mult, ALU.add)
                        nc.vector.tensor_copy(base[:], c_region[:])

                    def nothing():
                        pass

                    between = [nothing, rows_piece, shift_piece, difference_piece, probabilities_piece, weights_piece]

                    def body(ts):
                        _, b, c, d = ts
                        if b:
                            e = dve.value_load(t_ex[0:1, bass.ds(b.n, 1)], min_val=0, max_val=E - 1)
                            dve.wait_ge(w_hi_there, b.n + 1)
                            nc.vector.tensor_tensor(
                                w_lo[b.odd][:], w_gu[:, bass.ds(e, 1), :, 0:F].rearrange("p o g f -> p (o g) f"),
                                w_hi[b.odd][:].bitcast(F32), ALU.subtract).then_inc(w_there, 1)
                            dve.wait_ge(x_hi_there, b.n + 1)
                            nc.vector.tensor_tensor(x_lo[b.odd][:], TP[b.odd][:, 0:ROWS], x_hi[b.odd][:].bitcast(F32),
                                                    ALU.subtract).then_inc(x_ev, 1)
                        if c:
                            for j in range(PAIRS):
                                dve.wait_ge(u_mm, PAIRS * c.n + j + 1)
                                dve.wait_ge(sg_there, PAIRS * c.n + j + 1)
                                nc.vector.tensor_tensor(h[c.odd][:, 2 * j:2 * j + 2, :],
                                                        UB[bank_of(j, c)][:].rearrange("p (k n) -> p k n", k=2),
                                                        sgl[bank_of(j, c)][:], ALU.mult).then_inc(h_there, 1)
                        if d:
                            dve.wait_ge(y_mm, d.n + 1)
                            wait_count(dve, st[d.odd], 16 * d.half)
                            nc.vector.tensor_copy(ysb[d.odd][:], YB[d.odd][:, 0:ROWS].rearrange("p (r d) -> p r d", d=D)
                                                  ).then_inc(y_there, 1)

                    run_steps(dve, first, last, STEPS, lags, body, between)

                @block.tensor
                def _(pe):
                    pe.wait_ge((s_wx0, s_wx1)[layer], 16 * 3 * E)

                    def body(ts):
                        _, b, c, d = ts
                        if b:
                            pe.wait_ge(ld[b.odd], b.half * 16 + 16)
                            wait_count(pe, x_ev, b.n - 1)
                            for i in range(ROWS // P):
                                mm = nc.tensor.transpose(TP[b.odd][:, i * P:(i + 1) * P], xg[b.odd][:, i, :], c_ident[:])
                            mm.then_inc(x_mm, 1)
                        if c:
                            pe.wait_ge(w_there, c.n + 1)
                            pe.wait_ge(x_ev, c.n + 1)
                            for j in range(PAIRS):
                                wait_count(pe, h_there, banks_before(c, j))
                                for g, banks, done in ((0, GB, g_mm), (1, UB, u_mm)):
                                    for i in range(2):
                                        f = (2 * j + i) * P
                                        for k, (w_, x_) in enumerate(((w_hi, x_hi), (w_hi, x_lo), (w_lo, x_hi))):
                                            mm = nc.tensor.matmul(banks[bank_of(j, c)][:, i * ROWS:(i + 1) * ROWS],
                                                                  w_[c.odd][:, g, f:f + P], x_[c.odd][:],
                                                                  start=(k == 0), stop=(k == 2))
                                    mm.then_inc(done, 1)
                        if d:
                            pe.wait_ge(h_there, PAIRS * d.n + PAIRS)
                            wait_count(pe, y_there, d.n - 1)
                            e = pe.value_load(t_ex[0:1, bass.ds(d.n, 1)], min_val=0, max_val=E - 1)
                            for i in range(ROWS // P):
                                for f in range(FC):
                                    mm = nc.tensor.matmul(YB[d.odd][:, i * D:(i + 1) * D],
                                                          h[d.odd][:, f, i * P:(i + 1) * P],
                                                          w_dn[:, bass.ds(e, 1), f, :].rearrange("p o d -> p (o d)"),
                                                          start=(f == 0), stop=(f == FC - 1))
                            mm.then_inc(y_mm, 1)

                    run_steps(pe, first, last, STEPS, lags, body)

        class Combine:

            def __init__(self, sb, sem, norm_kind):
                self.idx = [sb(f"ci{i}", [P, TOPK * CH], U32) for i in range(2)]
                self.wt = [sb(f"cw{i}", [P, TOPK * CH]) for i in range(2)]
                self.y = [sb(f"cy{i}", [P, TOPK * CH, D]) for i in range(2)]
                self.r = sb("cr", [P, CH, D])
                self.norm = norm_kind("cn", sb, sem)
                self.chain = Chain(sem("cchain"))
                self.idx_there = sem("cidx")
                self.got = [sem(f"cgot{i}") for i in range(2)]
                self.used = sem("cused")
                self.marked = sem("cmarked")

            def indices(self, dve, t):
                wait_count(dve, self.got[t.odd], SCATTERS * t.half)
                nc.vector.tensor_copy(self.wt[t.odd][:], w_top[:, bass.ds(t.n, 1), :].rearrange("p o n -> p (o n)"))
                nc.vector.tensor_copy(self.idx[t.odd][:], row_c[:, bass.ds(t.n, 1), :].rearrange("p o n -> p (o n)")
                                      ).then_inc(self.idx_there, 1)

            def gather(self, pool, t):
                pool.wait_ge(self.idx_there, t.n + 1)
                wait_count(pool, self.used, t.n - 1)
                wait_count(pool, self.marked, t.n)
                wait_apart(pool, 2 + t.odd).then_inc(self.marked, 1)
                for j in range(TOPK * CH):
                    nc.gpsimd.indirect_dma_start(
                        out=self.y[t.odd][:, j, :], out_offset=None, in_=expert_out,
                        in_offset=bass.IndirectOffsetOnAxis(ap=self.idx[t.odd][:, j:j + 1], axis=0)
                    ).then_inc(self.got[t.odd], 16)

            def add(self, dve, t):
                dve.wait_ge(self.got[t.odd], SCATTERS * t.half + SCATTERS)
                dve.wait_ge(self.idx_there, t.n + 1)
                y, w = self.y[t.odd], self.wt[t.odd]
                self.chain.start(dve, t)
                for c in range(CH):
                    last = nc.vector.scalar_tensor_tensor(
                        self.r[:, c, :], y[:, c, :], w[:, c:c + 1],
                        xres[:, bass.ds(t.n * CH + c, 1), :].rearrange("p o d -> p (o d)"), ALU.mult, ALU.add)
                self.chain.link(last)
                for c in range(CH):
                    last = nc.vector.scalar_tensor_tensor(self.r[:, c, :], y[:, CH + c, :], w[:, CH + c:CH + c + 1],
                                                          self.r[:, c, :], ALU.mult, ALU.add)
                last.then_inc(self.used, 1)
                self.chain.end()
                dve.wait_ge(self.used, t.n + 1)
                self.norm.statistics(dve, self.r, t)

        def retention1():
            ph = ExitStack()
            with ph:
                def sb(name, shape, dt=F32):
                    return ph.enter_context(nc.sbuf_tensor("b_" + name, shape, dt))

                def sem(name):
                    return new_sem(ph, "b_" + name)

                w_q, w_k = sb("wq", [P, P]), sb("wk", [P, P])
                w_vT, c_center = sb("wvT", [P, P]), sb("center", [P, P])
                w_v = sb("wv", [P, P])
                w_1, w_2 = sb("w1", [P, P]), sb("w2", [P, P])
                g_w, g_b = sb("gw", [P, 1]), sb("gb", [P, 1])
                t_q, t_k = sb("tq", [P, T]), sb("tk", [P, T])
                m_head = sb("m_head", [P, H1])
                m_blk = sb("m_blk", [P, P])
                w_r = sb("wr", [P, E])
                xb = [sb(f"xb{i}", [P, CH, D]) for i in range(2)]
                xT = [sb(f"xT{i}", [P, T]) for i in range(2)]
                qr = [sb(f"qr{i}", [P, T]) for i in range(2)]
                kT = [sb(f"kT{i}", [P, T]) for i in range(2)]
                qx = [sb(f"qx{i}", [P, CH, H1, P]) for i in range(2)]
                kt = [sb(f"kt{i}", [P, CH - 1, P]) for i in range(2)]
                v = [sb(f"v{i}", [P, CH, P]) for i in range(2)]
                sT = [sb(f"sT{i}", [P, H1, P]) for i in range(2)]
                S = [sb(f"S{i}", [P, P]) for i in range(2)]
                oc = sb("oc", [P, CH, D])
                on = sb("on", [P, CH, D])
                osq = sb("osq", [P, CH, D])
                ssq = sb("ssq", [P, CH * H1])
                var = sb("var", [P, CH * H1])
                root = InverseRoot("gn", sb, sem, CH * H1)
                sgT = sb("sgT", [P, T])
                sgb = [sb(f"sgb{i}", [P, T]) for i in range(2)]
                oT = sb("oT", [P, T])
                r = sb("r", [P, CH, D])
                x3 = [sb(f"x3{i}", [P, CH, D]) for i in range(2)]
                comb = Combine(sb, sem, Norm)
                norm = Norm("n", sb, sem)
                router = Router("r", sb, sem, w_r)
                tiles = Tiles(sb, sem)
                T0, T1, S0, S1, U, O, A0, A1 = psum
                LG, RK = U[:, 256:256 + CH * E], U[:, 384:384 + CH * E + E]
                CHT = CH * H1

                s_w = sem("w")
                wv_mm, wv_there = sem("wv_mm"), sem("wv_there")
                x2_there, x2_kept = sem("x2_there"), sem("x2_kept")
                xT_mm, xT_ev = sem("xT_mm"), sem("xT_ev")
                qk_mm, qr_there, kT_there = sem("qk_mm"), sem("qr_there"), sem("kT_there")
                v_mm, v_ev, kt_mm, kt_ev = sem("v_mm"), sem("v_ev"), sem("kt_mm"), sem("kt_ev")
                qx_there = sem("qx_there")
                sc_mm, sT_there = sem("sc_mm"), sem("sT_there")
                U_mm, S_there = sem("U_mm"), sem("S_there")
                g_mm, sg_there, sgb_there = sem("g_mm"), sem("sg_there"), sem("sgb_there")
                o_mm, sq_there, oc_there, on_there = sem("o_mm"), sem("sq_there"), sem("oc_there"), sem("on_there")
                oT_mm, oT_there = sem("oT_mm"), sem("oT_there")
                y_mm, r_there, x3_there, x3_kept = sem("y_mm"), sem("r_there"), sem("x3_there"), sem("x3_kept")
                ch_v = Chain(sem("ch_v"))
                lags = [0, 1, 2, 3, 4, 5]
                first, last = 3, SEQS // 2
                block = ph.enter_context(nc.Block())
                small = [(w_q, bd_q), (w_k, bd_k), (w_vT, bd_vT), (c_center, center), (w_1, w1), (w_2, w2),
                         (g_w, gn_w), (g_b, gn_b), (t_q, dec_q), (t_k, dec_k), (m_head, head1), (m_blk, blk1),
                         (w_r, router1)]
                n_w = 16 * len(small)

                @block.sync
                def _(sp):
                    for to, src in small:
                        sp.dma_start(to[:], src).then_inc(s_w, 16)
                    for e in range(E):
                        sp.wait_ge(x2_there, e + 2)
                        load_expert(sp, 1, e, s_wx1)
                    tiles.fill(sp)

                @block.gpsimd
                def _(pool):
                    def body(ts):
                        z, y, a, b, c, d = ts
                        if z:
                            comb.gather(pool, z)
                        if c:
                            norm.power(pool, c)
                        if y:
                            comb.norm.power(pool, y)
                        if d:
                            router.scatter(pool, x3[d.odd], d)

                    run_steps(pool, first, last, SEQS, lags, body)
                    for i in range(2):
                        pool.wait_ge(router.sent[i], SCATTERS * SEQS // 2)

                @block.scalar
                def _(act):
                    act.wait_ge(wv_mm, 1)
                    nc.scalar.copy(w_v[:], psum[7][:, 0:P]).then_inc(wv_there, 1)

                    def body(ts):
                        z, y, a, b, c, d = ts
                        if d:
                            act.wait_ge(router.tp, d.n + 1)
                            nc.scalar.copy(router.xT[:], T0[:, :]).then_inc(router.xT_there, 1)
                        if b:
                            act.wait_ge(g_mm, b.n + 1)
                            nc.scalar.activation(sgT[:], T1[:, :], ACT.Silu).then_inc(sg_there, 1)
                        if a:
                            act.wait_ge(xT_mm, a.n + 1)
                            nc.scalar.copy(xT[a.odd][:], T0[:, :]).then_inc(xT_ev, 1)
                        if b:
                            act.wait_ge(sg_there, b.n + 1)
                            wait_count(act, oT_there, b.n - 1)
                            nc.scalar.activation(sgb[b.odd][:], sgT[:], ACT.Identity, bias=g_b[:, 0:1]
                                                 ).then_inc(sgb_there, 1)
                        if a:
                            nc.scalar.copy(xres[:, bass.ds(a.n * CH, CH), :], xb[a.odd][:]).then_inc(x2_kept, 1)
                        if d:
                            act.wait_ge(x3_there, d.n + 1)
                            nc.scalar.copy(xres[:, bass.ds(d.n * CH, CH), :], x3[d.odd][:]).then_inc(x3_kept, 1)
                        if a:
                            act.wait_ge(qr_there, a.n + 1)
                            wait_count(act, sc_mm, 2 * CH * (a.n - 1))
                            for hd in range(H1):
                                li = nc.scalar.activation(qx[a.odd][:, :, hd, :],
                                                          qr[a.odd][:].rearrange("p (c t) -> p c t", c=CH),
                                                          ACT.Copy, scale=m_head[:, hd:hd + 1])
                            li.then_inc(qx_there, 1)
                            act.wait_ge(v_mm, a.n + 1)
                            nc.scalar.copy(v[a.odd][:], A0[:].rearrange("p (c n) -> p c n", c=CH)).then_inc(v_ev, 1)
                            act.wait_ge(kt_mm, a.n + 1)
                            nc.scalar.copy(kt[a.odd][:], A1[:, 0:(CH - 1) * P].rearrange("p (c k) -> p c k", c=CH - 1)
                                           ).then_inc(kt_ev, 1)
                        if c:
                            wait_count(act, router.sent[c.odd], SCATTERS * c.half)
                            wait_count(act, x3_kept, c.n - 1)
                            norm.apply(act, r, x3[c.odd], c, x3_there)
                        if b:
                            act.wait_ge(o_mm, b.n + 1)
                            wait_count(act, on_there, b.n)
                            nc.scalar.activation(osq[:], O[:].rearrange("p (c n) -> p c n", c=CH), ACT.Square
                                                 ).then_inc(sq_there, 1)
                            nc.scalar.copy(oc[:], O[:].rearrange("p (c n) -> p c n", c=CH)).then_inc(oc_there, 1)
                        if y:
                            wait_count(act, xT_mm, y.n - 1)
                            wait_count(act, x2_kept, y.n - 1)
                            comb.norm.apply(act, comb.r, xb[y.odd], y, x2_there)

                    act.wait_ge(s_w, n_w)
                    nc.scalar.preload_act_table_set("silu_and_others")
                    run_steps(act, first, last, SEQS, lags, body)

                @block.vector
                def _(dve):
                    def masked_scores(b, c):
                        for j, bank in enumerate((S0, S1)):
                            dve.wait_ge(sc_mm, 2 * CH * b.n + 2 * c + j + 1)
                            nc.vector.tensor_tensor(sT[c % 2][:, 4 * j:4 * j + 4, :],
                                                    bank[:].rearrange("p (h t) -> p h t", h=4),
                                                    c_causal[:].unsqueeze(1).to_broadcast([P, 4, P]),
                                                    ALU.mult).then_inc(sT_there, 1)

                    def state(b, c):
                        dve.wait_ge(U_mm, (CH - 1) * b.n + c + 1)
                        nc.vector.tensor_tensor(S[c % 2][:], U[:, 0:P], m_blk[:], ALU.mult).then_inc(S_there, 1)

                    def body(ts):
                        z, y, a, b, c, d = ts
                        if isinstance(z and z.n, int) and z.n == 2:
                            dve.wait_ge(s_w, n_w)
                        if z:
                            comb.indices(dve, z)
                        if b:
                            masked_scores(b, 0)
                            state(b, 0)
                            masked_scores(b, 1)
                        if c:
                            dve.wait_ge(sq_there, c.n + 1)
                            ch_v.start(dve, c)
                            ch_v.link(nc.vector.tensor_reduce(ssq[:], osq[:].rearrange("p c (h n) -> p (c h) n", h=H1),
                                                              AX.X, ALU.add))
                            ch_v.link(nc.vector.tensor_scalar(var[:], ssq[:], 1.0 / DH1, LN_EPS, ALU.mult, ALU.add))
                            ch_v.end()
                            root.compute(dve, var, c)
                            dve.wait_ge(oc_there, c.n + 1)
                            nc.vector.tensor_tensor(
                                on[:].rearrange("p c (h n) -> p (c h) n", h=H1),
                                oc[:].rearrange("p c (h n) -> p (c h) n", h=H1),
                                root.y[:].unsqueeze(2).to_broadcast([P, CHT, DH1]), ALU.mult).then_inc(on_there, 1)
                        if b:
                            state(b, 1)
                        if a:
                            dve.wait_ge(qk_mm, a.n + 1)
                            nc.vector.tensor_tensor(kT[a.odd][:], A1[:], t_k[:], ALU.mult).then_inc(kT_there, 1)
                            nc.vector.tensor_tensor(qr[a.odd][:], A0[:], t_q[:], ALU.mult).then_inc(qr_there, 1)
                        if b:
                            masked_scores(b, 2)
                        if c:
                            dve.wait_ge(oT_mm, c.n + 1)
                            dve.wait_ge(sgb_there, c.n + 1)
                            nc.vector.scalar_tensor_tensor(oT[:], T1[:], g_w[:, 0:1], sgb[c.odd][:], ALU.mult, ALU.add
                                                           ).then_inc(oT_there, 1)
                        if b:
                            state(b, 2)
                        if d:
                            router.choose(dve, LG, d)
                        if c:
                            dve.wait_ge(y_mm, c.n + 1)
                            dve.wait_ge(x2_kept, c.n + 1)
                            wait_count(dve, x3_there, c.n)
                            nc.vector.tensor_tensor(r[:], T0[:].rearrange("p (c d) -> p c d", c=CH),
                                                    xres[:, bass.ds(c.n * CH, CH), :], ALU.add).then_inc(r_there, 1)
                            dve.wait_ge(r_there, c.n + 1)
                            norm.statistics(dve, r, c)
                        if b:
                            masked_scores(b, 3)
                        if y:
                            wait_count(dve, x2_there, y.n)
                            comb.add(dve, y)
                        if d:
                            router.rows_of(dve, RK, d)

                    run_steps(dve, first, last, SEQS, lags, body)
                    tiles.table(dve)

                @block.tensor
                def _(pe):
                    pe.wait_ge(s_w, n_w)
                    nc.tensor.matmul(psum[7][:, 0:P], w_vT[:], c_center[:], start=True, stop=True).then_inc(wv_mm, 1)
                    pe.wait_ge(wv_there, 1)

                    def scores(b, c):
                        for j, bank in enumerate((S0, S1)):
                            wait_count(pe, sT_there, 2 * CH * b.n + 2 * c + j - 1)
                            nc.tensor.matmul(bank[:], kT[b.odd][:, c * P:(c + 1) * P],
                                             qx[b.odd][:, c, 4 * j:4 * j + 4, :].rearrange("p h t -> p (h t)"),
                                             start=True, stop=True).then_inc(sc_mm, 1)

                    def state(b, c):
                        wait_count(pe, S_there, (CH - 1) * b.n + c)
                        nc.tensor.matmul(U[:, 0:P], kt[b.odd][:, c, :], v[b.odd][:, c, :],
                                         start=(c == 0), stop=(c == CH - 2), skip_group_check=True).then_inc(U_mm, 1)

                    def outputs(b, c):
                        at = c * D
                        if c == 0:
                            wait_count(pe, oc_there, b.n)
                        else:
                            pe.wait_ge(S_there, (CH - 1) * b.n + c)
                            nc.tensor.matmul(O[:, at:at + D], qr[b.odd][:, c * P:(c + 1) * P], S[(c - 1) % 2][:],
                                             start=False, stop=False, skip_group_check=True)
                        pe.wait_ge(sT_there, 2 * CH * b.n + 2 * c + 2)
                        for hd in range(H1):
                            mm = nc.tensor.matmul(O[:, at + hd * DH1:at + (hd + 1) * DH1], sT[c % 2][:, hd, :],
                                                  v[b.odd][:, c, hd * DH1:(hd + 1) * DH1],
                                                  start=(c == 0 and hd == 0), stop=(hd == H1 - 1), skip_group_check=True)
                        if c == CH - 1:
                            mm.then_inc(o_mm, 1)

                    def body(ts):
                        z, y, a, b, c, d = ts
                        if b:
                            pe.wait_ge(qx_there, b.n + 1)
                            scores(b, 0)
                        if d:
                            pe.wait_ge(x3_there, d.n + 1)
                            router.transposes(pe, T0, x3[d.odd], d)
                        if b:
                            wait_count(pe, oT_there, b.n - 1)
                            wait_count(pe, sg_there, b.n)
                            nc.tensor.matmul(T1[:], w_1[:], xT[b.odd][:], start=True, stop=True).then_inc(g_mm, 1)
                        if a:
                            pe.wait_ge(x2_there, a.n + 1)
                            if d:
                                pe.wait_ge(router.xT_there, d.n + 1)
                            else:
                                wait_count(pe, r_there, a.n - 2)
                                wait_count(pe, xT_ev, a.n)
                            for j in range(CH):
                                mm = nc.tensor.transpose(T0[:, j * P:(j + 1) * P], xb[a.odd][:, j, :], c_ident[:])
                            mm.then_inc(xT_mm, 1)
                        if b:
                            scores(b, 1)
                        if d:
                            router.logits_mm(pe, LG, d)
                        if b:
                            pe.wait_ge(kt_ev, b.n + 1)
                            state(b, 0)
                            outputs(b, 0)
                            state(b, 1)
                        if a:
                            pe.wait_ge(xT_ev, a.n + 1)
                            wait_count(pe, kt_ev, a.n)
                            nc.tensor.matmul(A1[:], w_k[:], xT[a.odd][:], start=True, stop=True)
                            nc.tensor.matmul(A0[:], w_q[:], xT[a.odd][:], start=True, stop=True).then_inc(qk_mm, 1)
                        if b:
                            scores(b, 2)
                            outputs(b, 1)
                        if c:
                            pe.wait_ge(on_there, c.n + 1)
                            if b:
                                pe.wait_ge(sg_there, b.n + 1)
                            else:
                                pe.wait_ge(oT_there, c.n)
                            for i in range(CH):
                                mm = nc.tensor.transpose(T1[:, i * P:(i + 1) * P], on[:, i, :], c_ident[:])
                            mm.then_inc(oT_mm, 1)
                        if b:
                            state(b, 2)
                        if a:
                            pe.wait_ge(qr_there, a.n + 1)
                            for j in range(CH):
                                mm = nc.tensor.matmul(A0[:, j * P:(j + 1) * P], xT[a.odd][:, j * P:(j + 1) * P], w_v[:],
                                                      start=True, stop=True)
                            mm.then_inc(v_mm, 1)
                            for j in range(CH - 1):
                                mm = nc.tensor.transpose(A1[:, j * P:(j + 1) * P], kT[a.odd][:, j * P:(j + 1) * P],
                                                         c_ident[:])
                            mm.then_inc(kt_mm, 1)
                        if c:
                            pe.wait_ge(oT_there, c.n + 1)
                            if a:
                                pe.wait_ge(xT_ev, a.n + 1)
                            else:
                                pe.wait_ge(router.xT_there, d.n + 1)
                            for i in range(CH):
                                mm = nc.tensor.matmul(T0[:, i * D:(i + 1) * D], oT[:, i * P:(i + 1) * P], w_2[:],
                                                      start=True, stop=True)
                            mm.then_inc(y_mm, 1)
                        if b:
                            scores(b, 3)
                            outputs(b, 2)
                        if d:
                            router.ranks_mm_(pe, RK, d)
                        if b:
                            outputs(b, 3)

                    run_steps(pe, first, last, SEQS, lags, body)

        def finish():
            ph = ExitStack()
            with ph:
                def sb(name, shape, dt=F32):
                    return ph.enter_context(nc.sbuf_tensor("f_" + name, shape, dt))

                def sem(name):
                    return new_sem(ph, "f_" + name)

                x4 = [sb(f"x4{i}", [P, CH, D]) for i in range(2)]
                comb = Combine(sb, sem, NormDve)
                x4_there = sem("x4_there")
                stored = [sem(f"stored{i}") for i in range(2)]
                lags = [0, 1]
                first, last = 2, SEQS // 2
                block = ph.enter_context(nc.Block())

                @block.gpsimd
                def _(pool):
                    def body(ts):
                        if ts[0]:
                            comb.gather(pool, ts[0])

                    run_steps(pool, first, last, SEQS, lags, body)

                @block.vector
                def _(dve):
                    def body(ts):
                        z, y = ts
                        if z:
                            comb.indices(dve, z)
                        if y:
                            wait_count(dve, x4_there, y.n)
                            comb.add(dve, y)
                            wait_count(dve, stored[y.odd], 16 * y.half)
                            comb.norm.apply(dve, comb.r, x4[y.odd], y, x4_there)

                    run_steps(dve, first, last, SEQS, lags, body)

                @block.sync
                def _(sp):
                    def body(ts):
                        y = ts[1]
                        if y:
                            sp.wait_ge(x4_there, y.n + 1)
                            sp.dma_start(out_seq[:, bass.ds(y.n, 1)].rearrange("p b c d -> p (b c) d"),
                                         x4[y.odd][:]).then_inc(stored[y.odd], 16)

                    run_steps(sp, first, last, SEQS, lags, body)
                    for i in range(2):
                        sp.wait_ge(stored[i], 16 * SEQS // 2)

        for phase in (retention0, lambda: experts(0), retention1, lambda: experts(1)):
            phase()
            clear_semaphores()
        finish()


def constants():
    import numpy as np

    f = np.float32
    t = np.arange(T, dtype=f)
    inv = (f(1.0) / np.power(f(10000.0), np.arange(0, DK0, 2, dtype=f) / f(DK0))).astype(f)
    ang = (t[:, None] * inv[None, :]).astype(f).astype(np.float64)
    half = DK0 // 2
    log0 = np.log1p(-np.exp2(-5.0 - np.arange(H0)))
    hd = np.arange(P)
    j = hd % DK0
    cos = np.cos(ang).T[j % half]
    sin = np.sin(ang).T[j % half] * np.where(j < half, -1.0, 1.0)[:, None]
    fall = np.exp(log0[hd // DK0][:, None] * t[None, :].astype(np.float64))
    rope_q = np.stack([cos, sin], 1) * (fall * DK0 ** -0.5)[:, None, :]
    rope_k = np.stack([cos, sin], 1) / fall[:, None, :]
    lin = np.linspace(np.log(1.0 / 512.0), np.log(1.0 / 32.0), H1)
    gam = (1.0 - np.exp(lin)).astype(f).astype(np.float64)[hd // DH1]
    dec_q = gam[:, None] ** t[None, :].astype(np.float64)
    dec_k = 1.0 / dec_q
    ins = {
        "rope_q": rope_q, "rope_k": rope_k, "dec_q": dec_q, "dec_k": dec_k,
        "center": np.eye(P) - ((hd // DH1)[:, None] == (hd // DH1)[None, :]) / DH1,
        "ident": np.eye(P), "causal": hd[None, :] >= hd[:, None],
        "head0": (hd // DK0)[:, None] == np.arange(H0)[None, :],
        "head1": (hd // DH1)[:, None] == np.arange(H1)[None, :],
        "blk0": (hd // DK0)[:, None] == (np.arange(H0 * DV0) // DV0)[None, :],
        "blk1": (hd // DH1)[:, None] == (hd // DH1)[None, :],
        "iota_e": np.tile(np.arange(E), (P, 1)), "region0": np.tile(np.arange(E) * REGION, (P, 1)),
        "iota_s": np.arange(STEPS)[None, :], "tri": hd[:, None] < hd[None, :],
    }
    out = {k: np.ascontiguousarray(a, dtype=f) for k, a in ins.items()}
    return out


def block_diagonal(w):
    import numpy as np

    n, a, b = w.shape
    full = np.zeros((n * a, n * b), w.dtype)
    for i in range(n):
        full[i * a:(i + 1) * a, i * b:(i + 1) * b] = w[i]
    return full


def kernel(**inputs):
    import numpy as np
    import concourse.bacc as bacc
    from concourse.bass_utils import run_bass_kernel_spmd

    g = {k: np.asarray(v) for k, v in inputs.items()}
    swap = (np.arange(P) // DK0) * DK0 + (np.arange(P) + DK0 // 2) % DK0
    wq, wk = g["L0_attn_Wq"], g["L0_attn_Wk"]
    arrays = {
        "x": g["L0_attn_x"], "wq": wq.T, "wqp": wq[swap].T, "wk": wk.T, "wkp": wk[swap].T,
        "wvg": np.concatenate([g["L0_attn_Wv"].T, g["L0_attn_Wg"].T], 1),
        "wo": g["L0_attn_Wo"].T.reshape(2, P, D).transpose(1, 0, 2),
        "gnorm": np.tile(g["L0_attn_g_norm_w"], 2)[:, None],
        "router0": g["L0_ffn_router_kernel_DE"], "gate0": g["L0_ffn_kernel_gating_EDF"],
        "up0": g["L0_ffn_kernel_up_EDF"], "down0": g["L0_ffn_kernel_down_EFD"],
        "bd_q": block_diagonal(g["L1_attn_Wq"]), "bd_k": block_diagonal(g["L1_attn_Wk"]),
        "bd_vT": block_diagonal(g["L1_attn_Wv"]).T,
        "w1": g["L1_attn_W1"], "w2": g["L1_attn_W2"],
        "gn_w": g["L1_attn_gn_w"][:, None], "gn_b": g["L1_attn_gn_b"][:, None],
        "router1": g["L1_ffn_Wg"], "gate1": g["L1_ffn_W1"], "up1": g["L1_ffn_W3"], "down1": g["L1_ffn_W2"],
        **constants(),
    }
    order = ["x", "wq", "wqp", "wk", "wkp", "wvg", "wo", "gnorm", "rope_q", "rope_k", "router0", "gate0", "up0",
             "down0", "bd_q", "bd_k", "bd_vT", "center", "w1", "w2", "gn_w", "gn_b", "dec_q", "dec_k", "router1",
             "gate1", "up1", "down1", "ident", "causal", "tri", "head0", "head1", "blk0", "blk1", "iota_e",
             "region0", "iota_s"]
    nc = bacc.Bacc("TRN2", target_bir_lowering=False, num_devices=1)
    given, args = {}, []
    for name in order:
        a = np.ascontiguousarray(arrays[name])
        given[f"in_{name}"] = a
        args.append(nc.dram_tensor(f"in_{name}", a.shape, mybir.dt.from_np(a.dtype), kind="ExternalInput").ap())
    args.append(nc.dram_tensor("out_0", (SEQS, T, D), F32, kind="ExternalOutput").ap())
    build(nc, *args)
    r = run_bass_kernel_spmd(nc, [given], core_ids=[0])
    return r.results[0]["out_0"]
```

```python
import concourse.bass as bass
from concourse import mybir
from contextlib import ExitStack

P = 128
SEQS, T, D = 16, 512, 128
CH = T // P
TILES = SEQS * CH
TOKENS = SEQS * T
E, TOPK = 8, 2
ROWS = 256
STEPS = TOKENS * TOPK // ROWS + E
REGION = TOKENS + ROWS
WIDE = D + 1
RESULTS = TOPK * TOKENS
SPARE = 2 * E
LN_EPS = 1e-5
H0, DK0, DV0 = 4, 32, 64
H1, DH1 = 8, 16
F0, F1 = 256, 512

F32 = mybir.dt.float32
F32R = mybir.dt.float32r
BF16 = mybir.dt.bfloat16
I32 = mybir.dt.int32
U32 = mybir.dt.uint32
ALU = mybir.AluOpType
ACT = mybir.ActivationFunctionType
AX = mybir.AxisListType

class Turn:

    def __init__(self, n, half, odd, quarter=None, slot=None):
        self.n, self.half, self.odd, self.quarter, self.slot = n, half, odd, quarter, slot

def turn(i, sub, lag, count, unroll):
    k = sub - lag
    if isinstance(i, int):
        n = unroll * i + k
        return Turn(n, n // 2, n % 2, n // 4, n % 4) if 0 <= n < count else None
    if unroll == 4:
        return Turn(i * 4 + k, i * 2 + k // 2, k % 2, i + k // 4, k % 4)
    return Turn(i * 2 + k, i + k // 2, k % 2)

def wait_count(eng, sem, n):
    if isinstance(n, int) and n <= 0:
        return
    eng.wait_ge(sem, n)

class Chain:

    def __init__(self, sem):
        self.sem, self.per, self.k = sem, 0, 0

    def start(self, eng, t):
        self.eng, self.t, self.k = eng, t, 0

    def link(self, ins):
        self.k += 1
        ins.then_inc(self.sem, 1)
        self.eng.wait_ge(self.sem, self.t.n * self.per + self.k)

    def end(self):
        assert self.per in (0, self.k)
        self.per = self.k

def run_steps(eng, first, last, count, lags, body, between=(), unroll=2):
    total = count + max(lags)
    for s in range(unroll * first):
        body([turn(s // unroll, s % unroll, lag, count, unroll) for lag in lags])
        if s < len(between):
            between[s]()
    with eng.Fori(first, last) as i:
        for sub in range(unroll):
            body([turn(i, sub, lag, count, unroll) for lag in lags])
    for s in range(unroll * last, total):
        body([turn(s // unroll, s % unroll, lag, count, unroll) for lag in lags])

def build(nc, x, w_proj, wo, gnorm, rope, router0, gate0, up0, down0,
          bd_q, bd_k, bd_vT, center, w1, w2, gn_w, gn_b, dec_q, dec_k, router1, gate1, up1, down1,
          ident, causal, tri, head0, head1, blk0, blk1, iota_e, region0, iota_s, spare, place, out):
    scattered = nc.dram_tensor("scattered", (E * REGION + (SPARE - E) * ROWS, WIDE), F32, kind="Internal").ap()
    expert_out = nc.dram_tensor("expert_out", (RESULTS + SPARE * ROWS, D), F32, kind="Internal").ap()
    results = expert_out[0:RESULTS].rearrange("(k b c p) d -> p (k b) c d", k=TOPK, b=SEQS, p=P)
    x_seq = x.rearrange("b (c p) d -> p b c d", p=P)
    out_seq = out.rearrange("b (c p) d -> p b c d", p=P)

    whole = ExitStack()
    with whole:
        def keep(name, shape, dt=F32):
            return whole.enter_context(nc.sbuf_tensor(name, shape, dt))

        c_ident = keep("c_ident", [P, P])
        c_causal = keep("c_causal", [P, P])
        c_tri = keep("c_tri", [P, P], BF16)
        c_ones = keep("c_ones", [P, P], BF16)
        c_iota = keep("c_iota", [P, E])
        c_zero = keep("c_zero", [P, ROWS // P], U32)
        c_region = keep("c_region", [P, E])
        c_half = keep("c_half", [P, 2 * T // 16])
        xres = keep("xres", [P, TILES, D])
        top_l = keep("top_l", [P, SEQS, TOPK * CH])
        logits = keep("logits", [P, TILES, E])
        w_top = keep("w_top", [P, SEQS, TOPK * CH])
        base = keep("base", [P, E])
        c_steps = keep("c_steps", [1, STEPS])
        c_place = keep("c_place", [P, TOPK, TILES])
        t_ex = keep("t_ex", [1, STEPS], I32)
        t_row = keep("t_row", [1, STEPS], I32)
        psum = [whole.enter_context(nc.psum_tensor(f"bank{i}", [P, 512], F32)) for i in range(8)]
        s_const = whole.enter_context(nc.semaphore("s_const"))
        s_cset = whole.enter_context(nc.semaphore("s_cset"))
        w_gu = keep("w_gu", [P, E, 2, F1])
        w_dn = keep("w_dn", [P, E, F1 // P, D])
        s_wx0 = whole.enter_context(nc.semaphore("s_wx0"))
        s_wx1 = whole.enter_context(nc.semaphore("s_wx1"))

        def load_expert(sp, layer, e, sem):
            g, u, dn, f = ((gate0, up0, down0, F0), (gate1, up1, down1, F1))[layer]
            sp.dma_start(w_gu[:, e, 0, 0:f], g[e]).then_inc(sem, 16)
            sp.dma_start(w_gu[:, e, 1, 0:f], u[e]).then_inc(sem, 16)
            sp.dma_start(w_dn[:, e, 0:f // P, :], dn[e].rearrange("(j p) d -> p j d", p=P)).then_inc(sem, 16)

        used = []

        def new_sem(phase, name):
            used.append(phase.enter_context(nc.semaphore(name)))
            return used[-1]

        def clear_semaphores():
            with nc.Block() as between:
                @between.gpsimd
                def _(pool):
                    numbers = sorted(s.num for s in used)
                    at = 0
                    while at < len(numbers):
                        to = at
                        while to + 1 < len(numbers) and numbers[to + 1] == numbers[to] + 1:
                            to += 1
                        pool.sem_clear(range(numbers[at], numbers[to] + 1))
                        at = to + 1
            used.clear()

        mark = keep("mark", [1, 5])

        def wait_apart(eng, at=4):
            if eng is nc.gpsimd:
                return nc.gpsimd.tensor_tensor(mark[:, at:at + 1], c_half[0:1, 0:1], c_half[0:1, 0:1], ALU.add)
            return nc.vector.memset(mark[:, at:at + 1], 0.0)

        class InverseRoot:

            def __init__(self, name, sb, sem, n):
                self.half = sb(name + "_half", [P, n])
                self.bits = sb(name + "_bits", [P, n], I32)
                self.sq = sb(name + "_sq", [P, n])
                self.y = sb(name + "_y", [P, n])
                self.chain = Chain(sem(name + "_chain"))

            def compute(self, dve, v, t):
                L = self.chain.link
                self.chain.start(dve, t)
                nc.vector.tensor_scalar(self.half[:], v[:], -0.5, None, ALU.mult)
                L(nc.vector.tensor_scalar(self.bits[:], v[:].bitcast(I32), 1, None, ALU.arith_shift_right))
                L(nc.vector.tensor_scalar(self.y[:].bitcast(I32), self.bits[:], -1.0, float(0x5F3759DF),
                                          ALU.mult, ALU.add))
                for _ in range(3):
                    L(nc.vector.tensor_tensor(self.sq[:], self.y[:], self.y[:], ALU.mult))
                    L(nc.vector.tensor_tensor(self.sq[:], self.sq[:], self.half[:], ALU.mult))
                    L(nc.vector.scalar_tensor_tensor(self.y[:], self.sq[:], 1.5, self.y[:], ALU.add, ALU.mult))
                self.chain.end()

        class Norm:

            def __init__(self, name, sb, sem):
                self.neg = [sb(f"{name}_neg{i}", [P, CH]) for i in range(2)]
                self.bias = [sb(f"{name}_bias{i}", [P, CH]) for i in range(2)]
                self.powed = Chain(sem(name + "_powed"))
                self.stats = sb(name + "_stats", [P, CH, 6])
                self.mv = [sb(f"{name}_mv{i}", [P, CH, 2]) for i in range(2)]
                self.ve = [sb(f"{name}_ve{i}", [P, CH]) for i in range(2)]
                self.rstd = [sb(f"{name}_rstd{i}", [P, CH]) for i in range(2)]
                self.chain = Chain(sem(name + "_chain"))
                self.var = sem(name + "_var")
                self.inv = sem(name + "_inv")

            def statistics(self, dve, r, t):
                for c in range(CH):
                    last = nc.vector.bn_stats(self.stats[:, c, :], r[:, c, :])
                self.chain.start(dve, t)
                self.chain.link(last)
                wait_apart(dve)
                for c in range(CH):
                    last = nc.vector.bn_aggr(self.mv[t.odd][:, c, :], self.stats[:, c, :])
                self.chain.link(last)
                self.chain.end()
                nc.vector.tensor_scalar(self.neg[t.odd][:], self.mv[t.odd][:, :, 0], -1.0, None, ALU.mult)
                nc.vector.tensor_scalar(self.ve[t.odd][:], self.mv[t.odd][:, :, 1], LN_EPS, None, ALU.add).then_inc(self.var, 1)

            def power(self, pool, t):
                pool.wait_ge(self.var, t.n + 1)
                self.powed.start(pool, t)
                self.powed.link(nc.gpsimd.tensor_tensor(self.rstd[t.odd][:], self.ve[t.odd][:], c_half[:, 0:CH], ALU.pow))
                self.powed.end()
                nc.gpsimd.tensor_tensor(self.bias[t.odd][:], self.neg[t.odd][:], self.rstd[t.odd][:], ALU.mult).then_inc(self.inv, 1)

            def apply(self, act, r, to, t, done):
                act.wait_ge(self.inv, t.n + 1)
                for c in range(CH):
                    last = nc.scalar.activation(to[:, c, :], r[:, c, :], ACT.Identity, bias=self.bias[t.odd][:, c:c + 1],
                                                scale=self.rstd[t.odd][:, c:c + 1])
                last.then_inc(done, 1)

        class Router:

            def __init__(self, name, sb, sem, w_router):
                self.w = w_router
                self.xT = sb(name + "_xT", [P, T])
                self.lg = sb(name + "_lg", [P, CH, E])
                self.mx = sb(name + "_mx", [P, CH, 8])
                self.mi = sb(name + "_mi", [P, CH, 8], U32)
                self.ix = sb(name + "_ix", [P, TOPK, CH])
                self.pick = sb(name + "_pick", [P, TOPK * CH, E])
                self.picked = sb(name + "_picked", [P, CH, E], BF16)
                self.rows = sb(name + "_rows", [P, CH, E])
                self.rowk = sb(name + "_rowk", [P, TOPK * CH, E])
                self.dst = sb(name + "_dst", [P, TOPK * CH])
                self.idx = [sb(f"{name}_idx{i}", [P, TOPK * CH], U32) for i in range(2)]
                self.chain = Chain(sem(name + "_chain"))
                self.chain2 = Chain(sem(name + "_chain2"))
                self.tp = sem(name + "_tp")
                self.xT_there = sem(name + "_xT_there")
                self.lg_mm = sem(name + "_lg_mm")
                self.picks = sem(name + "_picks")
                self.ranks_mm = sem(name + "_ranks_mm")
                self.idx_there = sem(name + "_idx_there")
                self.x = [[sb(f"{name}_x{k}{i}", [P, CH, WIDE]) for i in range(2)] for k in range(TOPK)]
                self.places = sem(name + "_places")
                self.copied = sem(name + "_copied")
                self.sent = [sem(f"{name}_sent{i}") for i in range(2)]

            def transposes(self, pe, bank, xb, t):
                for c in range(CH):
                    last = nc.tensor.transpose(bank[:, c * P:(c + 1) * P], xb[:, c, :], c_ident[:])
                last.then_inc(self.tp, 1)

            def logits_mm(self, pe, bank, t):
                pe.wait_ge(self.xT_there, t.n + 1)
                wait_count(pe, self.idx_there, t.n)
                for c in range(CH):
                    last = nc.tensor.matmul(bank[:, c * E:(c + 1) * E], self.xT[:, c * P:(c + 1) * P],
                                            self.w[:], start=True, stop=True)
                last.then_inc(self.lg_mm, 1)

            def choose(self, dve, bank, t):
                ch = self.chain
                dve.wait_ge(self.lg_mm, t.n + 1)
                ch.start(dve, t)
                lg = bank[:, 0:CH * E].rearrange("p (c e) -> p c e", c=CH)
                nc.vector.tensor_copy(logits[:, bass.ds(t.n * CH, CH), :], lg)
                ch.link(nc.vector.tensor_copy(self.lg[:], lg))
                wait_apart(dve)
                for c in range(CH):
                    last = nc.vector.max(self.mx[:, c, :], self.lg[:, c, :])
                ch.link(last)
                wait_apart(dve)
                for c in range(CH):
                    last = nc.vector.max_index(self.mi[:, c, :], self.mx[:, c, :], self.lg[:, c, :])
                ch.link(last)
                nc.vector.tensor_copy(top_l[:, bass.ds(t.n, 1), :].rearrange("p o (k c) -> p (o k) c", k=TOPK),
                                      self.mx[:, :, 0:TOPK].rearrange("p c k -> p k c"))
                ch.link(nc.vector.tensor_copy(self.ix[:], self.mi[:, :, 0:TOPK].rearrange("p c k -> p k c")))
                ch.link(nc.vector.tensor_tensor(
                    self.pick[:], c_iota[:].unsqueeze(1).to_broadcast([P, TOPK * CH, E]),
                    self.ix[:].rearrange("p k c -> p (k c)").unsqueeze(2).to_broadcast([P, TOPK * CH, E]),
                    ALU.is_equal))
                ch.end()
                nc.vector.tensor_tensor(self.picked[:], self.pick[:, 0:CH, :], self.pick[:, CH:, :],
                                        ALU.add).then_inc(self.picks, 1)

            def ranks_mm_(self, pe, bank, t):
                pe.wait_ge(self.picks, t.n + 1)
                m = self.picked
                nc.tensor.matmul(bank[:, 0:CH * E], c_tri[:], m[:].rearrange("p c e -> p (c e)"),
                                 start=True, stop=False, skip_group_check=True)
                for c in range(CH - 1):
                    later = CH - 1 - c
                    nc.tensor.matmul(bank[:, (c + 1) * E:CH * E].rearrange("p (c e) -> p c e", e=E), c_ones[:],
                                     m[:, c:c + 1, :].to_broadcast([P, later, E]),
                                     start=False, stop=False, skip_group_check=True)
                for c in range(CH):
                    last = nc.tensor.matmul(bank[:, CH * E:CH * E + E], c_ones[:], m[:, c, :],
                                            start=False, stop=(c == CH - 1), skip_group_check=True)
                last.then_inc(self.ranks_mm, 1)

            def rows_of(self, dve, bank, t):
                ch = self.chain2
                dve.wait_ge(self.ranks_mm, t.n + 1)
                ch.start(dve, t)
                ch.link(nc.vector.tensor_tensor(
                    self.rows[:], bank[:, 0:CH * E].rearrange("p (c e) -> p c e", c=CH),
                    base[:].unsqueeze(1).to_broadcast([P, CH, E]), ALU.add))
                nc.vector.tensor_tensor(base[:], bank[:, CH * E:CH * E + E], base[:], ALU.add)
                for k in range(TOPK):
                    last = nc.vector.tensor_tensor(self.rowk[:, k * CH:(k + 1) * CH, :],
                                                   self.pick[:, k * CH:(k + 1) * CH, :], self.rows[:], ALU.mult)
                ch.link(last)
                ch.link(nc.vector.tensor_reduce(self.dst[:], self.rowk[:], AX.X, ALU.add))
                ch.end()
                nc.vector.tensor_copy(self.idx[t.odd][:], self.dst[:]).then_inc(self.idx_there, 1)

            def put_places(self, pool, t):
                wait_count(pool, self.sent[t.odd], SCATTERS * t.half)
                for k in range(TOPK):
                    nc.gpsimd.tensor_copy(self.x[k][t.odd][:, :, D:WIDE].rearrange("p c o -> p (c o)"),
                                          c_place[:, k:k + 1, bass.ds(t.n * CH, CH)].rearrange("p o c -> p (o c)")
                                          ).then_inc(self.places, 1)

            def copy_rows(self, act, t, there):
                act.wait_ge(there, t.n + 1)
                nc.scalar.copy(self.x[1][t.odd][:, :, 0:D], self.x[0][t.odd][:, :, 0:D]).then_inc(self.copied, 1)

            def scatter(self, pool, t):
                pool.wait_ge(self.idx_there, t.n + 1)
                pool.wait_ge(self.copied, t.n + 1)
                pool.wait_ge(self.places, TOPK * t.n + TOPK)
                wait_apart(pool, t.odd)
                for k in range(TOPK):
                    for c in range(CH):
                        j = k * CH + c
                        nc.gpsimd.indirect_dma_start(
                            out=scattered[0:E * REGION, :],
                            out_offset=bass.IndirectOffsetOnAxis(ap=self.idx[t.odd][:, j:j + 1], axis=0),
                            in_=self.x[k][t.odd][:, c, :], in_offset=None).then_inc(self.sent[t.odd], 16)

        class Tiles:

            def __init__(self, sb, sem):
                self.cnt, self.til, self.one, self.cum = (sb("t_" + n, [P, E]) for n in ("cnt", "til", "one", "cum"))
                self.cnt_i, self.til_i = sb("t_cnt_i", [P, E], I32), sb("t_til_i", [P, E], I32)
                self.free_i = sb("t_free_i", [1, E], I32)
                self.past, self.past_n = sb("t_past", [1, STEPS, E]), sb("t_past_n", [1, STEPS, E])
                self.ex, self.exc, self.before, self.rowf = (
                    sb("t_" + n, [1, STEPS]) for n in ("ex", "exc", "before", "rowf"))
                self.free, self.filled = sem("t_free"), sem("t_filled")
                self.chain = Chain(sem("t_chain"))

            def fill(self, sp):
                sp.dma_start(scattered[E * REGION:, :], spare[E * ROWS:, :]).then_inc(self.filled, 16)
                sp.wait_ge(self.free, 1)
                for e in range(E):
                    row = sp.value_load(self.free_i[0:1, e:e + 1], min_val=0, max_val=E * REGION - ROWS)
                    sp.dma_start(scattered[bass.ds(row, ROWS), :], spare[e * ROWS:(e + 1) * ROWS, :]
                                 ).then_inc(self.filled, 16)
                sp.wait_ge(self.filled, 16 * (E + 1))

            def table(self, dve):
                L = self.chain.link
                self.chain.start(dve, Turn(0, 0, 0))
                cnt, til, cum, ex, exc, rowf = self.cnt, self.til, self.cum, self.ex, self.exc, self.rowf
                L(nc.vector.memset(self.one[:], 1.0))
                nc.vector.tensor_copy(self.free_i[:], base[0:1, :]).then_inc(self.free, 1)
                L(nc.vector.tensor_tensor(cnt[:], base[:], c_region[:], ALU.subtract))
                L(nc.vector.tensor_scalar(self.cnt_i[:], cnt[:], float(ROWS - 1), None, ALU.add))
                L(nc.vector.tensor_scalar(self.til_i[:], self.cnt_i[:], ROWS.bit_length() - 1, None,
                                          ALU.arith_shift_right))
                L(nc.vector.tensor_copy(til[:], self.til_i[:]))
                L(nc.vector.tensor_tensor_scan(cum[:], self.one[:], til[:], 0.0, ALU.mult, ALU.add))
                L(nc.vector.tensor_tensor(self.past[:], c_steps[:].unsqueeze(2).to_broadcast([1, STEPS, E]),
                                          cum[0:1, :].unsqueeze(1).to_broadcast([1, STEPS, E]), ALU.is_ge))
                nc.vector.tensor_reduce(ex[:], self.past[:], AX.X, ALU.add)
                L(nc.vector.tensor_tensor(self.past_n[:], self.past[:],
                                          til[0:1, :].unsqueeze(1).to_broadcast([1, STEPS, E]), ALU.mult))
                nc.vector.tensor_scalar(exc[:], ex[:], float(E - 1), None, ALU.min)
                L(nc.vector.tensor_reduce(self.before[:], self.past_n[:], AX.X, ALU.add))
                L(nc.vector.tensor_tensor(rowf[:], c_steps[:], self.before[:], ALU.subtract))
                L(nc.vector.tensor_scalar(rowf[:], rowf[:], float(ROWS), None, ALU.mult))
                nc.vector.tensor_copy(t_ex[:], exc[:])
                nc.vector.scalar_tensor_tensor(t_row[:], ex[:], float(REGION), rowf[:], ALU.mult, ALU.add)

        SCATTERS = 16 * TOPK * CH

        def retention0():
            ph = ExitStack()
            with ph:
                def sb(name, shape, dt=F32):
                    return ph.enter_context(nc.sbuf_tensor("a_" + name, shape, dt))

                def sem(name):
                    return new_sem(ph, "a_" + name)

                w_raw = sb("w_raw", [P, 4 * P + 2 * H0 * DV0])
                w_hi = sb("w_hi", [P, 4 * P + 2 * H0 * DV0], F32R)
                w_lo = sb("w_lo", [P, 4 * P + 2 * H0 * DV0], F32R)
                w_o = sb("wo", [P, 2, D])
                w_on = sb("won", [P, 2, D])
                tri_f = sb("tri_f", [P, P])
                t_qk = sb("rope", [P, 4, T])
                g_n = sb("gn", [P, 1])
                t_q, t_k = t_qk[:, 0:2, :], t_qk[:, 2:4, :]
                m_head = sb("m_head", [P, H0])
                m_blk = sb("m_blk", [P, H0 * DV0])
                w_r = sb("wr", [P, E])
                xb = [sb(f"xb{i}", [P, CH, D]) for i in range(2)]
                x_hi = [sb(f"x_hi{i}", [P, T], F32R) for i in range(2)]
                x_lo = [sb(f"x_lo{i}", [P, T], F32R) for i in range(2)]
                qm = sb("qm", [P, 2, T])
                km = sb("km", [P, 2, T])
                qr = [sb(f"qr{i}", [P, T]) for i in range(2)]
                kT = [sb(f"kT{i}", [P, T]) for i in range(2)]
                qx = [sb(f"qx{i}", [P, CH, H0, P]) for i in range(2)]
                v = [sb(f"v{i}", [P, CH, H0 * DV0]) for i in range(2)]
                kt = sb("kt", [P, CH - 1, P])
                sg = sb("sg", [P, CH, H0 * DV0])
                sT = [sb(f"sT{i}", [P, H0, P]) for i in range(2)]
                S = [sb(f"S{i}", [P, H0 * DV0]) for i in range(2)]
                osq = sb("osq", [P, CH, H0 * DV0])
                og = sb("og", [P, CH, H0 * DV0])
                ssq = sb("ssq", [P, CH * H0])
                mse = sb("mse", [P, CH * H0])
                root = InverseRoot("rms", sb, sem, CH * H0)
                ogT = sb("ogT", [P, 2, T])
                r = sb("r", [P, CH, D])
                norm = Norm("n", sb, sem)
                router = Router("r", sb, sem, w_r)
                x1 = router.x[0]
                tiles = Tiles(sb, sem)
                T0, T1, S0, S1, U, O, A0, A1 = psum
                LG, RK = U[:, 256:256 + CH * E], U[:, 384:384 + CH * E + E]

                s_x = [sem(f"x{i}") for i in range(2)]
                s_xr = sem("xr")
                s_w = sem("w")
                s_wo = sem("wo_scaled")
                s_id, s_wp, w_hi_there, w_split = sem("ident"), sem("wp"), sem("w_hi_there"), sem("w_split")
                xT_mm, x_hi_there, xT_ev = sem("xT_mm"), sem("x_hi_there"), sem("xT_ev")
                q_mm, k_mm, v_mm, g_mm = sem("q_mm"), sem("k_mm"), sem("v_mm"), sem("g_mm")
                q_ev, k_ev, v_ev, g_ev = sem("q_ev"), sem("k_ev"), sem("v_ev"), sem("g_ev")
                qr_there, qx_there, kT_there = sem("qr_there"), sem("qx_there"), sem("kT_there")
                kt_mm, kt_ev = sem("kt_mm"), sem("kt_ev")
                sc_mm, sT_there = sem("sc_mm"), sem("sT_there")
                U_mm, S_there = sem("U_mm"), sem("S_there")
                o_mm, sq_there, og_there = sem("o_mm"), sem("sq_there"), sem("og_there")
                ogn_there = sem("ogn_there")
                ogT_mm, ogT_ev = sem("ogT_mm"), sem("ogT_ev")
                y_mm, r_there, x1_there, x1_kept = sem("y_mm"), sem("r_there"), sem("x1_there"), sem("x1_kept")
                ch_ss = Chain(sem("ch_ss"))
                lags = [0, 1, 2, 3]
                first, last = 3, SEQS // 2
                n_w, n_const = 16 * 6, 16 * 6
                block = ph.enter_context(nc.Block())
                small = [(t_qk, rope), (m_head, head0), (m_blk, blk0), (w_o, wo), (g_n, gnorm), (w_r, router0)]
                consts = [(c_causal, causal), (c_iota, iota_e), (c_region, region0), (c_steps, iota_s), (c_place, place)]

                @block.sync
                def _(sp):
                    sp.dma_start(c_ident[:], ident).then_inc(s_id, 16)

                    def load(t):
                        wait_count(sp, xT_mm, t.n - 1)
                        sp.dma_start(xb[t.odd][:], x_seq[:, bass.ds(t.n, 1)].rearrange("p b c d -> p (b c) d")
                                     ).then_inc(s_x[t.odd], 16)

                    def body(ts):
                        if ts[0] is None:
                            return
                        load(ts[0])
                        if isinstance(ts[0].n, int) and ts[0].n == 0:
                            sp.dma_start(w_raw[:], w_proj).then_inc(s_wp, 16)
                            for to, src in small:
                                sp.dma_start(to[:], src).then_inc(s_w, 16)
                            for to, src in consts:
                                sp.dma_start(to[:], src).then_inc(s_const, 16)
                            sp.dma_start(tri_f[:], tri).then_inc(s_const, 16)
                        if isinstance(ts[0].n, int) and ts[0].n == 1:
                            for q in range(4):
                                sp.dma_start(xres[:, q * 16:(q + 1) * 16, :],
                                             x_seq[:, q * 4:(q + 1) * 4].rearrange("p b c d -> p (b c) d")
                                             ).then_inc(s_xr, 16)
                        if isinstance(ts[0].n, int) and 2 <= ts[0].n < 2 + E:
                            load_expert(sp, 0, ts[0].n - 2, s_wx0)

                    run_steps(sp, (2 + E) // 2, last, SEQS, [0], body)
                    tiles.fill(sp)

                @block.gpsimd
                def _(pool):
                    nc.gpsimd.memset(c_half[:], -0.5).then_inc(s_cset, 1)
                    nc.gpsimd.memset(c_ones[:], 1.0).then_inc(s_cset, 1)
                    nc.gpsimd.memset(c_zero[:], 0).then_inc(s_cset, 1)
                    pool.wait_ge(s_cset, 3)
                    pool.wait_ge(s_const, n_const)

                    def body(ts):
                        _, b, c, d = ts
                        if c:
                            norm.power(pool, c)
                        if d:
                            router.put_places(pool, d)
                            router.scatter(pool, d)

                    run_steps(pool, first, last, SEQS, lags, body)
                    for i in range(2):
                        pool.wait_ge(router.sent[i], SCATTERS * SEQS // 2)

                @block.scalar
                def _(act):
                    def body(ts):
                        a, b, c, d = ts
                        if a:
                            act.wait_ge(xT_mm, a.n + 1)
                            nc.scalar.copy(x_hi[a.odd][:], T0[:, :]).then_inc(x_hi_there, 1)
                        if d:
                            wait_count(act, router.sent[d.odd], SCATTERS * d.half)
                            wait_count(act, x1_kept, d.n - 1)
                            norm.apply(act, r, x1[d.odd][:, :, 0:D], d, x1_there)
                        if b:
                            act.wait_ge(kt_mm, b.n + 1)
                            nc.scalar.copy(kt[:], T1[:, 0:(CH - 1) * P].rearrange("p (c k) -> p c k", c=CH - 1)
                                           ).then_inc(kt_ev, 1)
                        if d:
                            act.wait_ge(router.tp, d.n + 1)
                            nc.scalar.copy(router.xT[:], T0[:, :]).then_inc(router.xT_there, 1)
                        if b:
                            wait_count(act, og_there, 2 * b.n)
                            act.wait_ge(g_mm, b.n + 1)
                            for j, bank in enumerate((A0, A1)):
                                nc.scalar.activation(sg[:, 2 * j:2 * j + 2, :],
                                                     bank[:].rearrange("p (c n) -> p c n", c=2),
                                                     ACT.Silu).then_inc(g_ev, 1)
                        if d:
                            act.wait_ge(x1_there, d.n + 1)
                            nc.scalar.copy(xres[:, bass.ds(d.n * CH, CH), :], x1[d.odd][:, :, 0:D]).then_inc(x1_kept, 1)
                            router.copy_rows(act, d, x1_there)
                        if b:
                            wait_count(act, ch_ss.sem, 2 * b.n - 1)
                            act.wait_ge(o_mm, 2 * b.n + 1)
                            nc.scalar.activation(osq[:, 0:2, :], O[:].rearrange("p (c n) -> p c n", c=2),
                                                 ACT.Square).then_inc(sq_there, 1)
                        if c:
                            act.wait_ge(ogT_mm, c.n + 1)
                            for j, bank in enumerate((T0, T1)):
                                nc.scalar.copy(ogT[:, j, :], bank[:, :]).then_inc(ogT_ev, 1)
                        if a:
                            if isinstance(a.n, int) and a.n == 0:
                                act.wait_ge(s_w, n_w)
                            act.wait_ge(qr_there, a.n + 1)
                            wait_count(act, sc_mm, CH * (a.n - 1))
                            for h in range(H0):
                                last_i = nc.scalar.activation(
                                    qx[a.odd][:, :, h, :], qr[a.odd][:].rearrange("p (c t) -> p c t", c=CH),
                                    ACT.Copy, scale=m_head[:, h:h + 1])
                            last_i.then_inc(qx_there, 1)
                        if a:
                            act.wait_ge(v_mm, a.n + 1)
                            for j, bank in enumerate((A0, A1)):
                                nc.scalar.copy(v[a.odd][:, 2 * j:2 * j + 2, :],
                                               bank[:].rearrange("p (c n) -> p c n", c=2)).then_inc(v_ev, 1)
                        if b:
                            act.wait_ge(o_mm, 2 * b.n + 2)
                            nc.scalar.activation(osq[:, 2:4, :], O[:].rearrange("p (c n) -> p c n", c=2),
                                                 ACT.Square).then_inc(sq_there, 1)

                    nc.scalar.preload_act_table_set("silu_and_others")
                    act.wait_ge(s_wp, 16)
                    nc.scalar.copy(w_hi[:], w_raw[:]).then_inc(w_hi_there, 1)
                    run_steps(act, first, last, SEQS, lags, body)

                @block.vector
                def _(dve):
                    dve.wait_ge(w_hi_there, 1)
                    nc.vector.tensor_tensor(w_lo[:], w_raw[:], w_hi[:].bitcast(F32), ALU.subtract).then_inc(w_split, 1)

                    def set_up():
                        dve.wait_ge(s_w, n_w)
                        dve.wait_ge(s_const, n_const)
                        nc.vector.tensor_copy(base[:], c_region[:])
                        nc.vector.tensor_copy(c_tri[:], tri_f[:])
                        nc.vector.tensor_scalar(w_on[:], w_o[:], g_n[:, 0:1], None, ALU.mult).then_inc(s_wo, 1)
                        dve.wait_ge(s_wo, 1)
                        dve.wait_ge(s_xr, 64)

                    def masked_scores(b, c):
                        dve.wait_ge(sc_mm, CH * b.n + c + 1)
                        nc.vector.tensor_tensor(sT[c % 2][:], (S0, S1)[c % 2][:].rearrange("p (h t) -> p h t", h=H0),
                                                c_causal[:].unsqueeze(1).to_broadcast([P, H0, P]),
                                                ALU.mult).then_inc(sT_there, 1)

                    def state(b, c):
                        dve.wait_ge(U_mm, (CH - 1) * b.n + c + 1)
                        nc.vector.tensor_tensor(S[c % 2][:], U[:, 0:H0 * DV0], m_blk[:], ALU.mult).then_inc(S_there, 1)

                    def gated(b, j):
                        dve.wait_ge(sq_there, 2 * b.n + j + 1)
                        dve.wait_ge(g_ev, 2 * b.n + 2)
                        nc.vector.tensor_tensor(og[:, 2 * j:2 * j + 2, :], O[:].rearrange("p (c n) -> p c n", c=2),
                                                sg[:, 2 * j:2 * j + 2, :], ALU.mult).then_inc(og_there, 1)

                    def body(ts):
                        a, b, c, d = ts
                        if a:
                            dve.wait_ge(x_hi_there, a.n + 1)
                            nc.vector.tensor_tensor(x_lo[a.odd][:], T0[:], x_hi[a.odd][:].bitcast(F32), ALU.subtract
                                                    ).then_inc(xT_ev, 1)
                            if isinstance(a.n, int) and a.n == 0:
                                set_up()
                        if b:
                            masked_scores(b, 0)
                        if c:
                            ch_ss.start(dve, c)
                            ch_ss.link(nc.vector.tensor_reduce(ssq[:], osq[:].rearrange("p c (h n) -> p (c h) n", h=H0),
                                                               AX.X, ALU.add))
                            ch_ss.link(nc.vector.tensor_scalar(mse[:], ssq[:], 1.0 / DV0, LN_EPS, ALU.mult, ALU.add))
                            ch_ss.end()
                        if b:
                            masked_scores(b, 1)
                            state(b, 0)
                        if c:
                            root.compute(dve, mse, c)
                            nc.vector.tensor_tensor(
                                og[:].rearrange("p c (h n) -> p (c h) n", h=H0),
                                og[:].rearrange("p c (h n) -> p (c h) n", h=H0),
                                root.y[:].unsqueeze(2).to_broadcast([P, CH * H0, DV0]), ALU.mult).then_inc(ogn_there, 1)
                        if b:
                            state(b, 1)
                        if a:
                            dve.wait_ge(q_mm, a.n + 1)
                            for j, bank in enumerate((A0, A1)):
                                last_i = nc.vector.tensor_tensor(qm[:, j, :], bank[:], t_q[:, j, :], ALU.mult)
                            last_i.then_inc(q_ev, 1)
                        if b:
                            masked_scores(b, 2)
                        if a:
                            dve.wait_ge(q_ev, a.n + 1)
                            nc.vector.tensor_tensor(qr[a.odd][:], qm[:, 0, :], qm[:, 1, :], ALU.add).then_inc(qr_there, 1)
                        if b:
                            if c:
                                dve.wait_ge(ogT_mm, c.n + 1)
                            gated(b, 0)
                            state(b, 2)
                        if d:
                            router.choose(dve, LG, d)
                        if a:
                            dve.wait_ge(k_mm, a.n + 1)
                            for j, bank in enumerate((A0, A1)):
                                last_i = nc.vector.tensor_tensor(km[:, j, :], bank[:], t_k[:, j, :], ALU.mult)
                            last_i.then_inc(k_ev, 1)
                        if b:
                            masked_scores(b, 3)
                        if c:
                            dve.wait_ge(y_mm, c.n + 1)
                            wait_count(dve, x1_there, c.n)
                            nc.vector.tensor_tensor(r[:], T0[:].rearrange("p (c d) -> p c d", c=CH),
                                                    xres[:, bass.ds(c.n * CH, CH), :], ALU.add).then_inc(r_there, 1)
                            dve.wait_ge(r_there, c.n + 1)
                            norm.statistics(dve, r, c)
                        if a:
                            dve.wait_ge(k_ev, a.n + 1)
                            nc.vector.tensor_tensor(kT[a.odd][:], km[:, 0, :], km[:, 1, :], ALU.add).then_inc(kT_there, 1)
                        if d:
                            router.rows_of(dve, RK, d)
                        if b:
                            gated(b, 1)

                    run_steps(dve, first, last, SEQS, lags, body)
                    tiles.table(dve)

                @block.tensor
                def _(pe):
                    pe.wait_ge(s_id, 16)

                    def thirds(hi, lo, w_at):
                        return ((hi, w_hi[:, w_at]), (lo, w_hi[:, w_at]), (hi, w_lo[:, w_at]))

                    def project_all(bank, t, i):
                        for k, (x_, w_) in enumerate(thirds(x_hi[t.odd], x_lo[t.odd], slice(i * P, (i + 1) * P))):
                            mm = nc.tensor.matmul(bank[:], w_, x_[:], start=(k == 0), stop=(k == 2))
                        return mm

                    def project_tokens(t, i):
                        n = H0 * DV0
                        for j in range(CH):
                            for k, (x_, w_) in enumerate(thirds(x_hi[t.odd], x_lo[t.odd],
                                                                slice(4 * P + i * n, 4 * P + i * n + n))):
                                mm = nc.tensor.matmul((A0, A1)[j // 2][:, (j % 2) * n:(j % 2) * n + n],
                                                      x_[:, j * P:(j + 1) * P], w_, start=(k == 0), stop=(k == 2))
                        return mm

                    def scores(b, c):
                        wait_count(pe, sT_there, CH * b.n + c - 1)
                        nc.tensor.matmul((S0, S1)[c % 2][:], kT[b.odd][:, c * P:(c + 1) * P],
                                         qx[b.odd][:, c].rearrange("p h t -> p (h t)"),
                                         start=True, stop=True).then_inc(sc_mm, 1)

                    def state(b, c):
                        wait_count(pe, S_there, (CH - 1) * b.n + c)
                        nc.tensor.matmul(U[:, 0:H0 * DV0], kt[:, c, :], v[b.odd][:, c, :],
                                         start=(c == 0), stop=(c == CH - 2), skip_group_check=True).then_inc(U_mm, 1)

                    def outputs(b, c):
                        at = (c % 2) * H0 * DV0
                        if c % 2 == 0:
                            wait_count(pe, og_there, 2 * b.n + c // 2)
                        if c:
                            pe.wait_ge(S_there, (CH - 1) * b.n + c)
                            nc.tensor.matmul(O[:, at:at + H0 * DV0], qr[b.odd][:, c * P:(c + 1) * P], S[(c - 1) % 2][:],
                                             start=(c % 2 == 0), stop=False, skip_group_check=True)
                        pe.wait_ge(sT_there, CH * b.n + c + 1)
                        for h in range(H0):
                            mm = nc.tensor.matmul(O[:, at + h * DV0:at + (h + 1) * DV0], sT[c % 2][:, h, :],
                                                  v[b.odd][:, c, h * DV0:(h + 1) * DV0],
                                                  start=(c == 0 and h == 0), stop=(h == H0 - 1), skip_group_check=True)
                        if c % 2:
                            mm.then_inc(o_mm, 1)

                    def body(ts):
                        a, b, c, d = ts
                        if a:
                            pe.wait_ge(s_x[a.odd], a.half * 16 + 16)
                            wait_count(pe, r_there, a.n - 2)
                            wait_count(pe, xT_ev, a.n)
                            for j in range(CH):
                                mm = nc.tensor.transpose(T0[:, j * P:(j + 1) * P], xb[a.odd][:, j, :], c_ident[:])
                            mm.then_inc(xT_mm, 1)
                        if b:
                            if isinstance(b.n, int) and b.n == 0:
                                pe.wait_ge(s_w, n_w)
                                pe.wait_ge(s_const, n_const)
                                pe.wait_ge(s_wo, 1)
                            pe.wait_ge(v_ev, 2 * b.n + 2)
                            project_tokens(b, 1).then_inc(g_mm, 1)
                            pe.wait_ge(qx_there, b.n + 1)
                            pe.wait_ge(kT_there, b.n + 1)
                            scores(b, 0)
                            wait_count(pe, ogT_ev, 2 * (b.n - 1))
                            wait_count(pe, kt_ev, b.n)
                            for j in range(CH - 1):
                                mm = nc.tensor.transpose(T1[:, j * P:(j + 1) * P], kT[b.odd][:, j * P:(j + 1) * P],
                                                         c_ident[:])
                            mm.then_inc(kt_mm, 1)
                            scores(b, 1)
                        if d:
                            pe.wait_ge(x1_there, d.n + 1)
                            if a:
                                pe.wait_ge(xT_ev, a.n + 1)
                            router.transposes(pe, T0, x1[d.odd][:, :, 0:D], d)
                        if b:
                            outputs(b, 0)
                        if d:
                            router.logits_mm(pe, LG, d)
                        if b:
                            pe.wait_ge(kt_ev, b.n + 1)
                            state(b, 0)
                        if a:
                            pe.wait_ge(xT_ev, a.n + 1)
                            if b:
                                pe.wait_ge(g_ev, 2 * b.n + 2)
                            if isinstance(a.n, int) and a.n == 0:
                                pe.wait_ge(w_split, 1)
                            project_all(A0, a, 0)
                            project_all(A1, a, 1).then_inc(q_mm, 1)
                        if b:
                            state(b, 1)
                            scores(b, 2)
                            outputs(b, 1)
                            scores(b, 3)
                        if c:
                            pe.wait_ge(ogn_there, c.n + 1)
                            if d:
                                pe.wait_ge(router.xT_there, d.n + 1)
                            else:
                                pe.wait_ge(xT_ev, a.n + 1)
                            if b:
                                pe.wait_ge(kt_ev, b.n + 1)
                            for j in range(2):
                                for i in range(CH):
                                    mm = nc.tensor.transpose((T0, T1)[j][:, i * P:(i + 1) * P],
                                                             og[:, i, j * P:(j + 1) * P], c_ident[:])
                            mm.then_inc(ogT_mm, 1)
                        if b:
                            state(b, 2)
                        if a:
                            pe.wait_ge(q_ev, a.n + 1)
                            project_all(A0, a, 2)
                            project_all(A1, a, 3).then_inc(k_mm, 1)
                        if c:
                            pe.wait_ge(ogT_ev, 2 * c.n + 2)
                            for i in range(CH):
                                for j in range(2):
                                    mm = nc.tensor.matmul(T0[:, i * D:(i + 1) * D], ogT[:, j, i * P:(i + 1) * P],
                                                          w_on[:, j, :], start=(j == 0), stop=(j == 1))
                            mm.then_inc(y_mm, 1)
                        if b:
                            outputs(b, 2)
                        if d:
                            router.ranks_mm_(pe, RK, d)
                        if a:
                            pe.wait_ge(k_ev, a.n + 1)
                            project_tokens(a, 0).then_inc(v_mm, 1)
                        if b:
                            outputs(b, 3)

                    run_steps(pe, first, last, SEQS, lags, body)

        def experts(layer):
            F = (F0, F1)[layer]
            FC = F // P
            PAIRS = FC // 2
            ph = ExitStack()
            with ph:
                def sb(name, shape, dt=F32):
                    return ph.enter_context(nc.sbuf_tensor(f"e{layer}_" + name, shape, dt))

                def sem(name):
                    return new_sem(ph, f"e{layer}_" + name)

                at = [sb(f"at{i}", [P, ROWS // P], U32) for i in range(4)]
                idx = [sb(f"idx{i}", [P, ROWS // P], U32) for i in range(4)]
                ex_l = sb("ex_l", [P, TILES, E])
                zsum = sb("zsum", [P, TILES])
                p2 = sb("p2", [P, SEQS, CH])
                dif = sb("dif", [P, SEQS, CH])
                thn = sb("thn", [P, SEQS, CH])

                xg = [sb(f"xg{i}", [P, ROWS // P, WIDE]) for i in range(4)]
                x_hi = [sb(f"x_hi{i}", [P, ROWS], F32R) for i in range(4)]
                x_lo = [sb(f"x_lo{i}", [P, ROWS], F32R) for i in range(4)]
                w_hi = [sb(f"w_hi{i}", [P, 2, F], F32R) for i in range(4)]
                w_lo = [sb(f"w_lo{i}", [P, 2, F], F32R) for i in range(4)]
                sgl = [sb(f"sgl{j}", [P, 2, ROWS]) for j in range(2)]
                h = [sb(f"h{i}", [P, FC, ROWS]) for i in range(2)]
                ysb = [sb(f"ysb{i}", [P, ROWS // P, D]) for i in range(4)]
                TP, GB, UB, YB = psum[0:2], psum[2:4], psum[4:6], psum[6:8]

                ch_r = Chain(sem("ch_r"))
                marked = sem("marked")
                SENT = 16 * (ROWS // P)
                ld = [sem(f"ld{i}") for i in range(4)]
                st = [sem(f"st{i}") for i in range(4)]
                x_mm, x_hi_there, x_ev = sem("x_mm"), sem("x_hi_there"), sem("x_ev")
                w_hi_there, w_there = sem("w_hi_there"), sem("w_there")
                g_mm, u_mm, sg_there, h_there = sem("g_mm"), sem("u_mm"), sem("sg_there"), sem("h_there")
                y_mm, y_there = sem("y_mm"), sem("y_there")
                at_there, idx_there = sem("at_there"), sem("idx_there")
                s_lx, s_ex, s_dif, s_th = sem("lx"), sem("ex_there"), sem("dif"), sem("th")
                lags = [0, 2, 4, 5]
                first, last = 3, STEPS // 4
                block = ph.enter_context(nc.Block())

                def bank_of(j, t):
                    return j if PAIRS == 2 else t.odd

                def banks_before(t, j):
                    return t.n * PAIRS + j - 1 if PAIRS == 2 else t.n - 1

                @block.sync
                def _(sp):
                    def body(ts):
                        a = ts[0]
                        if a:
                            wait_count(sp, x_ev, a.n - 3)
                            row = sp.value_load(t_row[0:1, bass.ds(a.n, 1)], min_val=0, max_val=E * REGION + (SPARE - E - 1) * ROWS)
                            sp.dma_start(xg[a.slot][:], scattered[bass.ds(row, ROWS), :].rearrange("(r p) d -> p r d", p=P)
                                         ).then_inc(ld[a.slot], 16)

                    run_steps(sp, first, last, STEPS, [0], body, unroll=4)

                @block.gpsimd
                def _(pool):
                    def body(ts):
                        e, d = ts
                        if e:
                            pool.wait_ge(at_there, e.n + 1)
                            wait_count(pool, st[e.slot], SENT * e.quarter)
                            nc.gpsimd.tensor_tensor(idx[e.slot][:], at[e.slot][:], c_zero[:], ALU.add
                                                    ).then_inc(idx_there, 1)
                        if d:
                            pool.wait_ge(idx_there, d.n + 1)
                            pool.wait_ge(y_there, d.n + 1)
                            wait_count(pool, marked, d.n)
                            wait_apart(pool, 2 + d.odd).then_inc(marked, 1)
                            for i in range(ROWS // P):
                                nc.gpsimd.indirect_dma_start(
                                    out=expert_out, out_offset=bass.IndirectOffsetOnAxis(
                                        ap=idx[d.slot][:, i:i + 1], axis=0),
                                    in_=ysb[d.slot][:, i, :], in_offset=None).then_inc(st[d.slot], 16)

                    run_steps(pool, first, last, STEPS, [lags[-1], lags[-1] + 1], body, unroll=4)
                    for i in range(4):
                        pool.wait_ge(st[i], SENT * STEPS // 4)

                @block.scalar
                def _(act):
                    def body(ts):
                        _, b, c = ts[:3]
                        if b:
                            wait_count(act, u_mm, PAIRS * (b.n - 3))
                            e = act.value_load(t_ex[0:1, bass.ds(b.n, 1)], min_val=0, max_val=E - 1)
                            nc.scalar.copy(w_hi[b.slot][:], w_gu[:, bass.ds(e, 1), :, 0:F].rearrange(
                                "p o g f -> p (o g) f")).then_inc(w_hi_there, 1)
                            act.wait_ge(x_mm, b.n + 1)
                            nc.scalar.copy(x_hi[b.slot][:], TP[b.odd][:, 0:ROWS]).then_inc(x_hi_there, 1)
                        if c:
                            for j in range(PAIRS):
                                act.wait_ge(g_mm, PAIRS * c.n + j + 1)
                                wait_count(act, h_there, banks_before(c, j))
                                nc.scalar.activation(sgl[bank_of(j, c)][:],
                                                     GB[bank_of(j, c)][:].rearrange("p (k n) -> p k n", k=2),
                                                     ACT.Silu).then_inc(sg_there, 1)
                        d = ts[4]
                        if d:
                            act.wait_ge(y_mm, d.n + 1)
                            wait_count(act, st[d.slot], SENT * d.quarter)
                            nc.scalar.copy(ysb[d.slot][:], YB[d.odd][:, 0:ROWS].rearrange("p (r d) -> p r d", d=D)
                                           ).then_inc(y_there, 1)

                    def exp_piece():
                        if layer == 0:
                            act.wait_ge(s_lx, 1)
                            nc.scalar.activation(ex_l[:], ex_l[:], ACT.Exp)
                            nc.scalar.activation(p2[:], p2[:], ACT.Exp).then_inc(s_ex, 1)
                            nc.scalar.preload_act_table_set("silu_and_others")

                    def tanh_piece():
                        act.wait_ge(s_dif, 1)
                        nc.scalar.activation(thn[:], dif[:], ACT.Tanh, scale=0.5).then_inc(s_th, 1)

                    def nothing():
                        pass

                    act.wait_ge((s_wx0, s_wx1)[layer], 16 * 3 * E)
                    nc.scalar.preload_act_table_set("silu_and_others")
                    run_steps(act, first, last, STEPS, lags + [lags[-1] + 1], body,
                              [nothing, nothing, nothing, nothing, nothing, exp_piece, tanh_piece], unroll=4)

                @block.vector
                def _(dve):
                    l1, l2 = top_l[:, :, 0:CH], top_l[:, :, CH:]

                    def difference_piece():
                        if layer:
                            nc.vector.tensor_tensor(dif[:], l1, l2, ALU.subtract).then_inc(s_dif, 1)
                            return
                        nc.vector.tensor_tensor(p2[:], l2, l1, ALU.subtract)

                        def by_seq(a):
                            return a[:].rearrange("p (b c) e -> p b c e", b=SEQS)

                        nc.vector.tensor_tensor(by_seq(ex_l), by_seq(logits), l1.unsqueeze(3).to_broadcast(
                            [P, SEQS, CH, E]), ALU.subtract).then_inc(s_lx, 1)

                    def probabilities_piece():
                        if layer:
                            return
                        L = ch_r.link
                        ch_r.start(dve, Turn(0, 0, 0))
                        dve.wait_ge(s_ex, 1)
                        nc.vector.tensor_scalar(dif[:], p2[:], -1.0, 1.0, ALU.mult, ALU.add)
                        L(nc.vector.tensor_reduce(zsum[:], ex_l[:], AX.X, ALU.add))
                        L(nc.vector.reciprocal(zsum[:], zsum[:]))
                        nc.vector.tensor_tensor(dif[:], dif[:], zsum[:].rearrange("p (b c) -> p b c", b=SEQS),
                                                ALU.mult).then_inc(s_dif, 1)

                    def weights_piece():
                        dve.wait_ge(s_th, 1)
                        nc.vector.tensor_scalar(w_top[:, :, 0:CH], thn[:], 0.5, 0.5, ALU.mult, ALU.add)
                        nc.vector.tensor_scalar(w_top[:, :, CH:], thn[:], -0.5, 0.5, ALU.mult, ALU.add)
                        nc.vector.tensor_copy(base[:], c_region[:])

                    def nothing():
                        pass

                    between = [nothing, nothing, nothing, nothing, nothing, difference_piece, probabilities_piece, weights_piece]

                    def body(ts):
                        _, b, c, _ = ts
                        if b:
                            e = dve.value_load(t_ex[0:1, bass.ds(b.n, 1)], min_val=0, max_val=E - 1)
                            dve.wait_ge(ld[b.slot], b.quarter * 16 + 16)
                            wait_count(dve, idx_there, b.n - 3)
                            nc.vector.tensor_copy(at[b.slot][:], xg[b.slot][:, :, D:WIDE].rearrange("p r o -> p (r o)")
                                                  ).then_inc(at_there, 1)
                            dve.wait_ge(w_hi_there, b.n + 1)
                            nc.vector.tensor_tensor(
                                w_lo[b.slot][:], w_gu[:, bass.ds(e, 1), :, 0:F].rearrange("p o g f -> p (o g) f"),
                                w_hi[b.slot][:].bitcast(F32), ALU.subtract).then_inc(w_there, 1)
                            dve.wait_ge(x_hi_there, b.n + 1)
                            nc.vector.tensor_tensor(x_lo[b.slot][:], TP[b.odd][:, 0:ROWS], x_hi[b.slot][:].bitcast(F32),
                                                    ALU.subtract).then_inc(x_ev, 1)
                        if c:
                            for j in range(PAIRS):
                                dve.wait_ge(u_mm, PAIRS * c.n + j + 1)
                                dve.wait_ge(sg_there, PAIRS * c.n + j + 1)
                                nc.vector.tensor_tensor(h[c.odd][:, 2 * j:2 * j + 2, :],
                                                        UB[bank_of(j, c)][:].rearrange("p (k n) -> p k n", k=2),
                                                        sgl[bank_of(j, c)][:], ALU.mult).then_inc(h_there, 1)

                    run_steps(dve, first, last, STEPS, lags, body, between, unroll=4)

                @block.tensor
                def _(pe):
                    pe.wait_ge((s_wx0, s_wx1)[layer], 16 * 3 * E)

                    def body(ts):
                        _, b, c, d = ts
                        if b:
                            pe.wait_ge(ld[b.slot], b.quarter * 16 + 16)
                            wait_count(pe, x_ev, b.n - 1)
                            for i in range(ROWS // P):
                                mm = nc.tensor.transpose(TP[b.odd][:, i * P:(i + 1) * P], xg[b.slot][:, i, 0:D], c_ident[:])
                            mm.then_inc(x_mm, 1)
                        if c:
                            pe.wait_ge(w_there, c.n + 1)
                            pe.wait_ge(x_ev, c.n + 1)
                            for j in range(PAIRS):
                                wait_count(pe, h_there, banks_before(c, j))
                                for g, banks, done in ((0, GB, g_mm), (1, UB, u_mm)):
                                    for i in range(2):
                                        f = (2 * j + i) * P
                                        for k, (w_, x_) in enumerate(((w_hi, x_hi), (w_hi, x_lo), (w_lo, x_hi))):
                                            mm = nc.tensor.matmul(banks[bank_of(j, c)][:, i * ROWS:(i + 1) * ROWS],
                                                                  w_[c.slot][:, g, f:f + P], x_[c.slot][:],
                                                                  start=(k == 0), stop=(k == 2))
                                    mm.then_inc(done, 1)
                        if d:
                            pe.wait_ge(h_there, PAIRS * d.n + PAIRS)
                            wait_count(pe, y_there, d.n - 1)
                            e = pe.value_load(t_ex[0:1, bass.ds(d.n, 1)], min_val=0, max_val=E - 1)
                            for i in range(ROWS // P):
                                for f in range(FC):
                                    mm = nc.tensor.matmul(YB[d.odd][:, i * D:(i + 1) * D],
                                                          h[d.odd][:, f, i * P:(i + 1) * P],
                                                          w_dn[:, bass.ds(e, 1), f, :].rearrange("p o d -> p (o d)"),
                                                          start=(f == 0), stop=(f == FC - 1))
                            mm.then_inc(y_mm, 1)

                    run_steps(pe, first, last, STEPS, lags, body, unroll=4)

        class Combine:

            def __init__(self, sb, sem, slots):
                self.slots = slots
                self.wt = [sb(f"cw{i}", [P, TOPK * CH]) for i in range(slots)]
                self.y = [sb(f"cy{i}", [P, TOPK * CH, D]) for i in range(slots)]
                self.r = [sb(f"cr{i}", [P, CH, D]) for i in range(slots)]
                self.norm = Norm("cn", sb, sem)
                self.chain = Chain(sem("cchain"))
                self.wt_there = sem("cwt")
                self.got = [sem(f"cgot{i}") for i in range(slots)]
                self.used = sem("cused")

            def slot(self, t):
                return t.slot if self.slots == 4 else t.odd

            def round(self, t):
                return t.quarter if self.slots == 4 else t.half

            def weights(self, dve, t):
                wait_count(dve, self.used, t.n + 1 - self.slots)
                nc.vector.tensor_copy(self.wt[self.slot(t)][:],
                                      w_top[:, bass.ds(t.n, 1), :].rearrange("p o n -> p (o n)")
                                      ).then_inc(self.wt_there, 1)

            def load(self, sp, t):
                wait_count(sp, self.used, t.n + 1 - self.slots)
                for k in range(TOPK):
                    sp.dma_start(self.y[self.slot(t)][:, k * CH:(k + 1) * CH, :],
                                 results[:, bass.ds(t.n + k * SEQS, 1)].rearrange("p o c d -> p (o c) d")
                                 ).then_inc(self.got[self.slot(t)], 16)

            def wait_loaded(self, eng, t):
                eng.wait_ge(self.got[self.slot(t)], 16 * TOPK * self.round(t) + 16 * TOPK)
                eng.wait_ge(self.wt_there, t.n + 1)

            def add(self, dve, t):
                self.wait_loaded(dve, t)
                y, w, r = self.y[self.slot(t)], self.wt[self.slot(t)], self.r[self.slot(t)]
                self.chain.start(dve, t)
                for c in range(CH):
                    last = nc.vector.scalar_tensor_tensor(
                        r[:, c, :], y[:, c, :], w[:, c:c + 1],
                        xres[:, bass.ds(t.n * CH + c, 1), :].rearrange("p o d -> p (o d)"), ALU.mult, ALU.add)
                self.chain.link(last)
                self.chain.end()
                self.add_second(dve, t)

            def scale_first(self, act, t, done):
                self.wait_loaded(act, t)
                y, w = self.y[self.slot(t)], self.wt[self.slot(t)]
                for c in range(CH):
                    last = nc.scalar.activation(y[:, c, :], y[:, c, :], ACT.Copy, scale=w[:, c:c + 1])
                last.then_inc(done, 1)

            def add_first(self, pool, t, scaled, done):
                pool.wait_ge(scaled, t.n + 1)
                nc.gpsimd.tensor_tensor(self.r[self.slot(t)][:], self.y[self.slot(t)][:, 0:CH, :],
                                        xres[:, bass.ds(t.n * CH, CH), :], ALU.add).then_inc(done, 1)

            def add_second(self, dve, t):
                y, w, r = self.y[self.slot(t)], self.wt[self.slot(t)], self.r[self.slot(t)]
                for c in range(CH):
                    last = nc.vector.scalar_tensor_tensor(r[:, c, :], y[:, CH + c, :], w[:, CH + c:CH + c + 1],
                                                          r[:, c, :], ALU.mult, ALU.add)
                last.then_inc(self.used, 1)
                dve.wait_ge(self.used, t.n + 1)
                self.norm.statistics(dve, r, t)

        def retention1():
            ph = ExitStack()
            with ph:
                def sb(name, shape, dt=F32):
                    return ph.enter_context(nc.sbuf_tensor("b_" + name, shape, dt))

                def sem(name):
                    return new_sem(ph, "b_" + name)

                w_q, w_k = sb("wq", [P, P]), sb("wk", [P, P])
                w_vT, c_center = sb("wvT", [P, P]), sb("center", [P, P])
                w_v = sb("wv", [P, P])
                w_1, w_2 = sb("w1", [P, P]), sb("w2", [P, P])
                g_w, g_b = sb("gw", [P, 1]), sb("gb", [P, 1])
                t_q, t_k = sb("tq", [P, T]), sb("tk", [P, T])
                m_head = sb("m_head", [P, H1])
                m_blk = sb("m_blk", [P, P])
                w_r = sb("wr", [P, E])
                xb = [sb(f"xb{i}", [P, CH, D]) for i in range(2)]
                xT = [sb(f"xT{i}", [P, T]) for i in range(2)]
                qr = [sb(f"qr{i}", [P, T]) for i in range(2)]
                kT = [sb(f"kT{i}", [P, T]) for i in range(2)]
                qx = [sb(f"qx{i}", [P, CH, H1, P]) for i in range(2)]
                kt = [sb(f"kt{i}", [P, CH - 1, P]) for i in range(2)]
                v = [sb(f"v{i}", [P, CH, P]) for i in range(2)]
                sT = [sb(f"sT{i}", [P, H1, P]) for i in range(2)]
                S = [sb(f"S{i}", [P, P]) for i in range(2)]
                oc = sb("oc", [P, CH, D])
                on = sb("on", [P, CH, D])
                osq = sb("osq", [P, CH, D])
                ssq = sb("ssq", [P, CH * H1])
                var = sb("var", [P, CH * H1])
                root = InverseRoot("gn", sb, sem, CH * H1)
                sgT = sb("sgT", [P, T])
                sgb = [sb(f"sgb{i}", [P, T]) for i in range(2)]
                oT = sb("oT", [P, T])
                r = sb("r", [P, CH, D])
                comb = Combine(sb, sem, 2)
                norm = Norm("n", sb, sem)
                router = Router("r", sb, sem, w_r)
                x3 = router.x[0]
                tiles = Tiles(sb, sem)
                T0, T1, S0, S1, U, O, A0, A1 = psum
                LG, RK = U[:, 256:256 + CH * E], U[:, 384:384 + CH * E + E]
                CHT = CH * H1

                s_w = sem("w")
                wv_mm, wv_there = sem("wv_mm"), sem("wv_there")
                x2_there, x2_kept = sem("x2_there"), sem("x2_kept")
                xT_mm, xT_ev = sem("xT_mm"), sem("xT_ev")
                qk_mm, qr_there, kT_there = sem("qk_mm"), sem("qr_there"), sem("kT_there")
                v_mm, v_ev, kt_mm, kt_ev = sem("v_mm"), sem("v_ev"), sem("kt_mm"), sem("kt_ev")
                qx_there = sem("qx_there")
                sc_mm, sT_there = sem("sc_mm"), sem("sT_there")
                U_mm, S_there = sem("U_mm"), sem("S_there")
                g_mm, sg_there, sgb_there = sem("g_mm"), sem("sg_there"), sem("sgb_there")
                o_mm, sq_there, oc_there, on_there = sem("o_mm"), sem("sq_there"), sem("oc_there"), sem("on_there")
                oT_mm, oT_there = sem("oT_mm"), sem("oT_there")
                y_mm, r_there, x3_there, x3_kept = sem("y_mm"), sem("r_there"), sem("x3_there"), sem("x3_kept")
                ch_v = Chain(sem("ch_v"))
                lags = [0, 1, 2, 3, 4, 5]
                first, last = 4, SEQS // 2
                block = ph.enter_context(nc.Block())
                small = [(w_q, bd_q), (w_k, bd_k), (w_vT, bd_vT), (c_center, center), (w_1, w1), (w_2, w2),
                         (g_w, gn_w), (g_b, gn_b), (t_q, dec_q), (t_k, dec_k), (m_head, head1), (m_blk, blk1),
                         (w_r, router1)]
                n_w = 16 * len(small)

                @block.sync
                def _(sp):
                    def body(ts):
                        z = ts[0]
                        if z:
                            comb.load(sp, z)
                            if isinstance(z.n, int) and 2 <= z.n < 2 + E:
                                load_expert(sp, 1, z.n - 2, s_wx1)

                    run_steps(sp, (2 + E) // 2, last, SEQS, [0], body)
                    tiles.fill(sp)

                @block.gpsimd
                def _(pool):
                    def body(ts):
                        z, y, a, b, c, d = ts
                        if c:
                            norm.power(pool, c)
                        if y:
                            comb.norm.power(pool, y)
                        if d:
                            router.put_places(pool, d)
                            router.scatter(pool, d)

                    run_steps(pool, first, last, SEQS, lags, body)
                    for i in range(2):
                        pool.wait_ge(router.sent[i], SCATTERS * SEQS // 2)

                @block.scalar
                def _(act):
                    for to, src in small:
                        act.dma_start(to[:], src).then_inc(s_w, 16)
                    act.wait_ge(wv_mm, 1)
                    nc.scalar.copy(w_v[:], psum[7][:, 0:P]).then_inc(wv_there, 1)

                    def body(ts):
                        z, y, a, b, c, d = ts
                        if d:
                            act.wait_ge(router.tp, d.n + 1)
                            nc.scalar.copy(router.xT[:], T0[:, :]).then_inc(router.xT_there, 1)
                        if b:
                            act.wait_ge(g_mm, b.n + 1)
                            nc.scalar.activation(sgT[:], T1[:, :], ACT.Silu).then_inc(sg_there, 1)
                        if a:
                            act.wait_ge(xT_mm, a.n + 1)
                            nc.scalar.copy(xT[a.odd][:], T0[:, :]).then_inc(xT_ev, 1)
                        if b:
                            act.wait_ge(sg_there, b.n + 1)
                            wait_count(act, oT_there, b.n - 1)
                            nc.scalar.activation(sgb[b.odd][:], sgT[:], ACT.Identity, bias=g_b[:, 0:1]
                                                 ).then_inc(sgb_there, 1)
                        if a:
                            nc.scalar.copy(xres[:, bass.ds(a.n * CH, CH), :], xb[a.odd][:]).then_inc(x2_kept, 1)
                        if d:
                            act.wait_ge(x3_there, d.n + 1)
                            nc.scalar.copy(xres[:, bass.ds(d.n * CH, CH), :], x3[d.odd][:, :, 0:D]).then_inc(x3_kept, 1)
                            router.copy_rows(act, d, x3_there)
                        if a:
                            act.wait_ge(qr_there, a.n + 1)
                            wait_count(act, sc_mm, 2 * CH * (a.n - 1))
                            for hd in range(H1):
                                li = nc.scalar.activation(qx[a.odd][:, :, hd, :],
                                                          qr[a.odd][:].rearrange("p (c t) -> p c t", c=CH),
                                                          ACT.Copy, scale=m_head[:, hd:hd + 1])
                            li.then_inc(qx_there, 1)
                            act.wait_ge(v_mm, a.n + 1)
                            nc.scalar.copy(v[a.odd][:], A0[:].rearrange("p (c n) -> p c n", c=CH)).then_inc(v_ev, 1)
                            act.wait_ge(kt_mm, a.n + 1)
                            nc.scalar.copy(kt[a.odd][:], A1[:, 0:(CH - 1) * P].rearrange("p (c k) -> p c k", c=CH - 1)
                                           ).then_inc(kt_ev, 1)
                        if b:
                            act.wait_ge(o_mm, b.n + 1)
                            wait_count(act, on_there, b.n)
                            nc.scalar.activation(osq[:], O[:].rearrange("p (c n) -> p c n", c=CH), ACT.Square
                                                 ).then_inc(sq_there, 1)
                            nc.scalar.copy(oc[:], O[:].rearrange("p (c n) -> p c n", c=CH)).then_inc(oc_there, 1)
                        if c:
                            wait_count(act, router.sent[c.odd], SCATTERS * c.half)
                            wait_count(act, x3_kept, c.n - 1)
                            norm.apply(act, r, x3[c.odd][:, :, 0:D], c, x3_there)
                        if y:
                            wait_count(act, xT_mm, y.n - 1)
                            wait_count(act, x2_kept, y.n - 1)
                            comb.norm.apply(act, comb.r[y.odd], xb[y.odd], y, x2_there)

                    act.wait_ge(s_w, n_w)
                    nc.scalar.preload_act_table_set("silu_and_others")
                    run_steps(act, first, last, SEQS, lags, body)

                @block.vector
                def _(dve):
                    def masked_scores(b, c):
                        for j, bank in enumerate((S0, S1)):
                            dve.wait_ge(sc_mm, 2 * CH * b.n + 2 * c + j + 1)
                            nc.vector.tensor_tensor(sT[c % 2][:, 4 * j:4 * j + 4, :],
                                                    bank[:].rearrange("p (h t) -> p h t", h=4),
                                                    c_causal[:].unsqueeze(1).to_broadcast([P, 4, P]),
                                                    ALU.mult).then_inc(sT_there, 1)

                    def state(b, c):
                        dve.wait_ge(U_mm, (CH - 1) * b.n + c + 1)
                        nc.vector.tensor_tensor(S[c % 2][:], U[:, 0:P], m_blk[:], ALU.mult).then_inc(S_there, 1)

                    def body(ts):
                        z, y, a, b, c, d = ts
                        if a and isinstance(a.n, int) and a.n == 0:
                            dve.wait_ge(s_w, n_w)
                        if b:
                            masked_scores(b, 0)
                        if c:
                            dve.wait_ge(sq_there, c.n + 1)
                            ch_v.start(dve, c)
                            ch_v.link(nc.vector.tensor_reduce(ssq[:], osq[:].rearrange("p c (h n) -> p (c h) n", h=H1),
                                                              AX.X, ALU.add))
                            ch_v.link(nc.vector.tensor_scalar(var[:], ssq[:], 1.0 / DH1, LN_EPS, ALU.mult, ALU.add))
                            ch_v.end()
                        if b:
                            masked_scores(b, 1)
                        if z:
                            comb.weights(dve, z)
                        if b:
                            state(b, 0)
                        if c:
                            root.compute(dve, var, c)
                            dve.wait_ge(oc_there, c.n + 1)
                            nc.vector.tensor_tensor(
                                on[:].rearrange("p c (h n) -> p (c h) n", h=H1),
                                oc[:].rearrange("p c (h n) -> p (c h) n", h=H1),
                                root.y[:].unsqueeze(2).to_broadcast([P, CHT, DH1]), ALU.mult).then_inc(on_there, 1)
                        if b:
                            state(b, 1)
                        if a:
                            dve.wait_ge(qk_mm, a.n + 1)
                            nc.vector.tensor_tensor(kT[a.odd][:], A1[:], t_k[:], ALU.mult).then_inc(kT_there, 1)
                            nc.vector.tensor_tensor(qr[a.odd][:], A0[:], t_q[:], ALU.mult).then_inc(qr_there, 1)
                        if b:
                            masked_scores(b, 2)
                        if c:
                            dve.wait_ge(oT_mm, c.n + 1)
                            dve.wait_ge(sgb_there, c.n + 1)
                            nc.vector.scalar_tensor_tensor(oT[:], T1[:], g_w[:, 0:1], sgb[c.odd][:], ALU.mult, ALU.add
                                                           ).then_inc(oT_there, 1)
                        if b:
                            state(b, 2)
                        if d:
                            router.choose(dve, LG, d)
                        if b:
                            masked_scores(b, 3)
                        if c:
                            dve.wait_ge(y_mm, c.n + 1)
                            dve.wait_ge(x2_kept, c.n + 1)
                            wait_count(dve, x3_there, c.n)
                            nc.vector.tensor_tensor(r[:], T0[:].rearrange("p (c d) -> p c d", c=CH),
                                                    xres[:, bass.ds(c.n * CH, CH), :], ALU.add).then_inc(r_there, 1)
                            dve.wait_ge(r_there, c.n + 1)
                            norm.statistics(dve, r, c)
                        if y:
                            wait_count(dve, x2_there, y.n - 1)
                            comb.add(dve, y)
                        if d:
                            router.rows_of(dve, RK, d)

                    run_steps(dve, first, last, SEQS, lags, body)
                    tiles.table(dve)

                @block.tensor
                def _(pe):
                    pe.wait_ge(s_w, n_w)
                    nc.tensor.matmul(psum[7][:, 0:P], w_vT[:], c_center[:], start=True, stop=True).then_inc(wv_mm, 1)
                    pe.wait_ge(wv_there, 1)

                    def scores(b, c):
                        for j, bank in enumerate((S0, S1)):
                            wait_count(pe, sT_there, 2 * CH * b.n + 2 * c + j - 1)
                            nc.tensor.matmul(bank[:], kT[b.odd][:, c * P:(c + 1) * P],
                                             qx[b.odd][:, c, 4 * j:4 * j + 4, :].rearrange("p h t -> p (h t)"),
                                             start=True, stop=True).then_inc(sc_mm, 1)

                    def state(b, c):
                        wait_count(pe, S_there, (CH - 1) * b.n + c)
                        nc.tensor.matmul(U[:, 0:P], kt[b.odd][:, c, :], v[b.odd][:, c, :],
                                         start=(c == 0), stop=(c == CH - 2), skip_group_check=True).then_inc(U_mm, 1)

                    def outputs(b, c):
                        at = c * D
                        if c == 0:
                            wait_count(pe, oc_there, b.n)
                        else:
                            pe.wait_ge(S_there, (CH - 1) * b.n + c)
                            nc.tensor.matmul(O[:, at:at + D], qr[b.odd][:, c * P:(c + 1) * P], S[(c - 1) % 2][:],
                                             start=False, stop=False, skip_group_check=True)
                        pe.wait_ge(sT_there, 2 * CH * b.n + 2 * c + 2)
                        for hd in range(H1):
                            mm = nc.tensor.matmul(O[:, at + hd * DH1:at + (hd + 1) * DH1], sT[c % 2][:, hd, :],
                                                  v[b.odd][:, c, hd * DH1:(hd + 1) * DH1],
                                                  start=(c == 0 and hd == 0), stop=(hd == H1 - 1), skip_group_check=True)
                        if c == CH - 1:
                            mm.then_inc(o_mm, 1)

                    def body(ts):
                        z, y, a, b, c, d = ts
                        if b:
                            pe.wait_ge(qx_there, b.n + 1)
                            scores(b, 0)
                        if d:
                            pe.wait_ge(x3_there, d.n + 1)
                            router.transposes(pe, T0, x3[d.odd][:, :, 0:D], d)
                        if b:
                            wait_count(pe, oT_there, b.n - 1)
                            wait_count(pe, sg_there, b.n)
                            nc.tensor.matmul(T1[:], w_1[:], xT[b.odd][:], start=True, stop=True).then_inc(g_mm, 1)
                            scores(b, 1)
                        if d:
                            router.logits_mm(pe, LG, d)
                        if a:
                            pe.wait_ge(x2_there, a.n + 1)
                            if d:
                                pe.wait_ge(router.xT_there, d.n + 1)
                            else:
                                wait_count(pe, r_there, a.n - 2)
                                wait_count(pe, xT_ev, a.n)
                            for j in range(CH):
                                mm = nc.tensor.transpose(T0[:, j * P:(j + 1) * P], xb[a.odd][:, j, :], c_ident[:])
                            mm.then_inc(xT_mm, 1)
                        if b:
                            pe.wait_ge(kt_ev, b.n + 1)
                            state(b, 0)
                            outputs(b, 0)
                        if a:
                            pe.wait_ge(xT_ev, a.n + 1)
                            wait_count(pe, kt_ev, a.n)
                            nc.tensor.matmul(A1[:], w_k[:], xT[a.odd][:], start=True, stop=True)
                            nc.tensor.matmul(A0[:], w_q[:], xT[a.odd][:], start=True, stop=True).then_inc(qk_mm, 1)
                        if b:
                            state(b, 1)
                            scores(b, 2)
                            outputs(b, 1)
                        if c:
                            pe.wait_ge(on_there, c.n + 1)
                            if b:
                                pe.wait_ge(sg_there, b.n + 1)
                            else:
                                pe.wait_ge(oT_there, c.n)
                            for i in range(CH):
                                mm = nc.tensor.transpose(T1[:, i * P:(i + 1) * P], on[:, i, :], c_ident[:])
                            mm.then_inc(oT_mm, 1)
                        if b:
                            state(b, 2)
                            scores(b, 3)
                        if c:
                            pe.wait_ge(oT_there, c.n + 1)
                            if a:
                                pe.wait_ge(xT_ev, a.n + 1)
                            else:
                                pe.wait_ge(router.xT_there, d.n + 1)
                            for i in range(CH):
                                mm = nc.tensor.matmul(T0[:, i * D:(i + 1) * D], oT[:, i * P:(i + 1) * P], w_2[:],
                                                      start=True, stop=True)
                            mm.then_inc(y_mm, 1)
                        if b:
                            outputs(b, 2)
                        if a:
                            pe.wait_ge(qr_there, a.n + 1)
                            for j in range(CH):
                                mm = nc.tensor.matmul(A0[:, j * P:(j + 1) * P], xT[a.odd][:, j * P:(j + 1) * P], w_v[:],
                                                      start=True, stop=True)
                            mm.then_inc(v_mm, 1)
                            for j in range(CH - 1):
                                mm = nc.tensor.transpose(A1[:, j * P:(j + 1) * P], kT[a.odd][:, j * P:(j + 1) * P],
                                                         c_ident[:])
                            mm.then_inc(kt_mm, 1)
                        if d:
                            router.ranks_mm_(pe, RK, d)
                        if b:
                            outputs(b, 3)

                    run_steps(pe, first, last, SEQS, lags, body)

        def finish():
            ph = ExitStack()
            with ph:
                def sb(name, shape, dt=F32):
                    return ph.enter_context(nc.sbuf_tensor("f_" + name, shape, dt))

                def sem(name):
                    return new_sem(ph, "f_" + name)

                x4 = [sb(f"x4{i}", [P, CH, D]) for i in range(4)]
                comb = Combine(sb, sem, 4)
                x4_there, scaled, summed = sem("x4_there"), sem("scaled"), sem("summed")
                stored = [sem(f"stored{i}") for i in range(4)]
                lags = [0, 1, 2, 3]
                first, last = 2, SEQS // 4
                block = ph.enter_context(nc.Block())

                @block.gpsimd
                def _(pool):
                    def body(ts):
                        _, y, w, _ = ts
                        if y:
                            wait_count(pool, x4_there, y.n - 3)
                            comb.add_first(pool, y, scaled, summed)
                        if w:
                            comb.norm.power(pool, w)

                    run_steps(pool, first, last, SEQS, lags, body, unroll=4)

                @block.vector
                def _(dve):
                    def body(ts):
                        z, _, w, _ = ts
                        if z:
                            comb.weights(dve, z)
                        if w:
                            dve.wait_ge(summed, w.n + 1)
                            wait_count(dve, x4_there, w.n - 1)
                            comb.add_second(dve, w)

                    run_steps(dve, first, last, SEQS, lags, body, unroll=4)

                @block.scalar
                def _(act):
                    def body(ts):
                        _, w, _, y = ts
                        if w:
                            comb.scale_first(act, w, scaled)
                        if y:
                            wait_count(act, stored[y.slot], 16 * y.quarter)
                            comb.norm.apply(act, comb.r[y.slot], x4[y.slot], y, x4_there)
                            act.wait_ge(x4_there, y.n + 1)
                            act.dma_start(out_seq[:, bass.ds(y.n, 1)].rearrange("p b c d -> p (b c) d"),
                                          x4[y.slot][:]).then_inc(stored[y.slot], 16)

                    run_steps(act, first, last, SEQS, lags, body, unroll=4)
                    for i in range(4):
                        act.wait_ge(stored[i], 16 * SEQS // 4)

                @block.sync
                def _(sp):
                    def body(ts):
                        if ts[0]:
                            comb.load(sp, ts[0])

                    run_steps(sp, first, last, SEQS, lags, body, unroll=4)

        for phase in (retention0, lambda: experts(0), retention1, lambda: experts(1)):
            phase()
            clear_semaphores()
        finish()

def constants():
    import numpy as np

    f = np.float32
    t = np.arange(T, dtype=f)
    inv = (f(1.0) / np.power(f(10000.0), np.arange(0, DK0, 2, dtype=f) / f(DK0))).astype(f)
    ang = (t[:, None] * inv[None, :]).astype(f).astype(np.float64)
    half = DK0 // 2
    log0 = np.log1p(-np.exp2(-5.0 - np.arange(H0)))
    hd = np.arange(P)
    j = hd % DK0
    cos = np.cos(ang).T[j % half]
    sin = np.sin(ang).T[j % half] * np.where(j < half, -1.0, 1.0)[:, None]
    fall = np.exp(log0[hd // DK0][:, None] * t[None, :].astype(np.float64))
    rope_q = np.stack([cos, sin], 1) * (fall * DK0 ** -0.5)[:, None, :]
    rope_k = np.stack([cos, sin], 1) / fall[:, None, :]
    lin = np.linspace(np.log(1.0 / 512.0), np.log(1.0 / 32.0), H1)
    gam = (1.0 - np.exp(lin)).astype(f).astype(np.float64)[hd // DH1]
    dec_q = gam[:, None] ** t[None, :].astype(np.float64)
    dec_k = 1.0 / dec_q
    ins = {
        "rope": np.concatenate([rope_q, rope_k], 1), "dec_q": dec_q, "dec_k": dec_k,
        "center": np.eye(P) - ((hd // DH1)[:, None] == (hd // DH1)[None, :]) / DH1,
        "ident": np.eye(P), "causal": hd[None, :] >= hd[:, None],
        "head0": (hd // DK0)[:, None] == np.arange(H0)[None, :],
        "head1": (hd // DH1)[:, None] == np.arange(H1)[None, :],
        "blk0": (hd // DK0)[:, None] == (np.arange(H0 * DV0) // DV0)[None, :],
        "blk1": (hd // DH1)[:, None] == (hd // DH1)[None, :],
        "iota_e": np.tile(np.arange(E), (P, 1)), "region0": np.tile(np.arange(E) * REGION, (P, 1)),
        "iota_s": np.arange(STEPS)[None, :], "tri": hd[:, None] < hd[None, :],
    }
    place = np.arange(TOPK)[None, :, None] * TOKENS + np.arange(TILES)[None, None, :] * P + hd[:, None, None]
    spare = np.zeros((SPARE * ROWS, WIDE))
    spare[:, D] = RESULTS + np.arange(SPARE * ROWS)
    ins |= {"place": place, "spare": spare}
    out = {k: np.ascontiguousarray(a, dtype=f) for k, a in ins.items()}
    return out

def block_diagonal(w):
    import numpy as np

    n, a, b = w.shape
    full = np.zeros((n * a, n * b), w.dtype)
    for i in range(n):
        full[i * a:(i + 1) * a, i * b:(i + 1) * b] = w[i]
    return full

def kernel(**inputs):
    import numpy as np
    import concourse.bacc as bacc
    from concourse.bass_utils import run_bass_kernel_spmd

    g = {k: np.asarray(v) for k, v in inputs.items()}
    swap = (np.arange(P) // DK0) * DK0 + (np.arange(P) + DK0 // 2) % DK0
    wq, wk = g["L0_attn_Wq"], g["L0_attn_Wk"]
    arrays = {
        "x": g["L0_attn_x"],
        "w_proj": np.concatenate([wq.T, wq[swap].T, wk.T, wk[swap].T, g["L0_attn_Wv"].T, g["L0_attn_Wg"].T], 1),
        "wo": g["L0_attn_Wo"].T.reshape(2, P, D).transpose(1, 0, 2),
        "gnorm": np.tile(g["L0_attn_g_norm_w"], 2)[:, None],
        "router0": g["L0_ffn_router_kernel_DE"], "gate0": g["L0_ffn_kernel_gating_EDF"],
        "up0": g["L0_ffn_kernel_up_EDF"], "down0": g["L0_ffn_kernel_down_EFD"],
        "bd_q": block_diagonal(g["L1_attn_Wq"]), "bd_k": block_diagonal(g["L1_attn_Wk"]),
        "bd_vT": block_diagonal(g["L1_attn_Wv"]).T,
        "w1": g["L1_attn_W1"], "w2": g["L1_attn_W2"],
        "gn_w": g["L1_attn_gn_w"][:, None], "gn_b": g["L1_attn_gn_b"][:, None],
        "router1": g["L1_ffn_Wg"], "gate1": g["L1_ffn_W1"], "up1": g["L1_ffn_W3"], "down1": g["L1_ffn_W2"],
        **constants(),
    }
    order = ["x", "w_proj", "wo", "gnorm", "rope", "router0", "gate0", "up0",
             "down0", "bd_q", "bd_k", "bd_vT", "center", "w1", "w2", "gn_w", "gn_b", "dec_q", "dec_k", "router1",
             "gate1", "up1", "down1", "ident", "causal", "tri", "head0", "head1", "blk0", "blk1", "iota_e",
             "region0", "iota_s", "spare", "place"]
    nc = bacc.Bacc("TRN2", target_bir_lowering=False, num_devices=1)
    given, args = {}, []
    for name in order:
        a = np.ascontiguousarray(arrays[name])
        given[f"in_{name}"] = a
        args.append(nc.dram_tensor(f"in_{name}", a.shape, mybir.dt.from_np(a.dtype), kind="ExternalInput").ap())
    args.append(nc.dram_tensor("out_0", (SEQS, T, D), F32, kind="ExternalOutput").ap())
    build(nc, *args)
    r = run_bass_kernel_spmd(nc, [given], core_ids=[0])
    return r.results[0]["out_0"]
```
